# Optimizing a Trainium2 kernel written in Bass

```python
import numpy as np
import jax
import jax.numpy as jnp

def _softmax(x, axis=-1):
    return jax.nn.softmax(x, axis=axis)

def _gelu(x):
    return jax.nn.gelu(x, approximate=True)

def _silu(x):
    return jax.nn.silu(x)

def _sigmoid(x):
    return jax.nn.sigmoid(x)

def _layernorm(x, axis=-1, eps=1e-05):
    m = jnp.mean(x, axis=axis, keepdims=True)
    v = jnp.var(x, axis=axis, keepdims=True)
    return (x - m) / jnp.sqrt(v + eps)

def _scatter_add(tgt, idx, src, axis=0):
    return tgt.at[idx].add(src)

def _segment_sum(src, seg, n):
    return jax.ops.segment_sum(src, seg, n)
kernel_name = 'mk_gnn_preln_d2_gnn_r8_9fa53c'

def setup_inputs(seed: int=0):
    np.random.seed(seed)
    _w = jnp.asarray

    def _rec_inputs():
        import jax
        import jax.numpy as jnp
        _gk = jax.random.key(seed)
        x = -0.0004942 + 1 * jax.random.normal(jax.random.fold_in(_gk, 1), (6250, 128), jnp.float32)
        _s = jax.random.randint(jax.random.fold_in(_gk, 2), (100000,), 0, 6250, jnp.int32)
        _d = jax.random.randint(jax.random.fold_in(_gk, 3), (100000,), 0, 6250, jnp.int32)
        _loop = jnp.arange(6250, dtype=jnp.int32)
        src = jnp.concatenate([_s, _d, _loop])
        dst = jnp.concatenate([_d, _s, _loop])
        _o = jnp.argsort(dst, stable=True)
        src = src[_o]
        dst = dst[_o]
        edge_attr_128 = -8.16379e-05 + 0.999858 * jax.random.normal(jax.random.fold_in(_gk, 12), (206250, 128), jnp.float32)
        edge_attr_4 = 0.00132558 + 1.00026 * jax.random.normal(jax.random.fold_in(_gk, 13), (206250, 4), jnp.float32)
        return (x, src, dst, edge_attr_128, edge_attr_4)
    x, src, dst, edge_attr_128, edge_attr_4 = _rec_inputs()

    def _L0_gnn_setup():
        import jax, jax.numpy as jnp
        import numpy as np
        N, E, D, H, HD, TD, ED, G = (3750, 60000, 128, 8, 16, 512, 4, 8)

        def group_norm(x, gamma, beta, num_groups=G, eps=1e-05):
            n, c = x.shape
            xr = x.reshape(n, num_groups, c // num_groups)
            mu = xr.mean(-1, keepdims=True)
            var = ((xr - mu) ** 2).mean(-1, keepdims=True)
            xn = (xr - mu) * jax.lax.rsqrt(var + eps)
            return xn.reshape(n, c) * gamma + beta

        def mesh_conv(x, src, dst, ea, w1, b1, g, bt, w2, b2):
            m = jnp.concatenate([x[dst], x[src], ea], axis=-1) @ w1 + b1
            m = jax.nn.silu(group_norm(m, g, bt))
            m = m @ w2 + b2
            n = x.shape[0]
            out = jax.ops.segment_sum(m, dst, num_segments=n)
            cnt = jax.ops.segment_sum(jnp.ones((dst.shape[0],), m.dtype), dst, num_segments=n)
            return out / jnp.clip(cnt, 1.0)[:, None]
        key = jax.random.key(seed)
        ks = jax.random.split(key, 32)
        inp = {}
        inp['x'] = jax.random.normal(ks[0], (N, D), jnp.float32)
        inp['edge_src'] = jax.random.randint(ks[1], (E,), 0, N, jnp.int32)
        inp['edge_dst'] = jax.random.randint(ks[2], (E,), 0, N, jnp.int32)
        inp['edge_attr'] = jax.random.normal(ks[3], (E, ED), jnp.float32)
        inp['t_emb'] = jax.random.normal(ks[4], (TD,), jnp.float32)
        s = 0.02
        inp['c1_w1'] = jax.random.normal(ks[5], (2 * D + ED, D)) * s
        inp['c1_b1'] = jnp.zeros((D,))
        inp['c1_g'] = jnp.ones((D,))
        inp['c1_bt'] = jnp.zeros((D,))
        inp['c1_w2'] = jax.random.normal(ks[6], (D, D)) * s
        inp['c1_b2'] = jnp.zeros((D,))
        inp['c2_w1'] = jax.random.normal(ks[7], (2 * D + ED, D)) * s
        inp['c2_b1'] = jnp.zeros((D,))
        inp['c2_g'] = jnp.ones((D,))
        inp['c2_bt'] = jnp.zeros((D,))
        inp['c2_w2'] = jax.random.normal(ks[8], (D, D)) * s
        inp['c2_b2'] = jnp.zeros((D,))
        inp['tm_w'] = jax.random.normal(ks[9], (TD, D)) * s
        inp['tm_b'] = jnp.zeros((D,))
        inp['n1_g'] = jnp.ones((D,))
        inp['n1_b'] = jnp.zeros((D,))
        inp['n2_g'] = jnp.ones((D,))
        inp['n2_b'] = jnp.zeros((D,))
        inp['qw'] = jax.random.normal(ks[10], (D, D)) * s
        inp['qb'] = jnp.zeros((D,))
        inp['kw'] = jax.random.normal(ks[11], (D, D)) * s
        inp['kb'] = jnp.zeros((D,))
        inp['vw'] = jax.random.normal(ks[12], (D, D)) * s
        inp['vb'] = jnp.zeros((D,))
        inp['ew'] = jax.random.normal(ks[13], (ED, H)) * s
        inp['eb'] = jnp.zeros((H,))
        inp['ow'] = jax.random.normal(ks[14], (D, D)) * s
        inp['ob'] = jnp.zeros((D,))
        inp['an_g'] = jnp.ones((D,))
        inp['an_b'] = jnp.zeros((D,))
        return inp
    _L0_gnn_all = _L0_gnn_setup()
    _L0_gnn_in = {k: v for k, v in _L0_gnn_all.items() if k in ('t_emb', 'c1_w1', 'c1_b1', 'c1_g', 'c1_bt', 'c1_w2', 'c1_b2', 'c2_w1', 'c2_b1', 'c2_g', 'c2_bt', 'c2_w2', 'c2_b2', 'tm_w', 'tm_b', 'n1_g', 'n1_b', 'n2_g', 'n2_b', 'qw', 'qb', 'kw', 'kb', 'vw', 'vb', 'ew', 'eb', 'ow', 'ob', 'an_g', 'an_b')}
    del _L0_gnn_all

    def _L1_gnn_setup():
        import jax, jax.numpy as jnp
        import numpy as np
        N_NODES = 6250
        N_EDGES = 100000
        D_IN = 128
        OUT = 128
        H = 4
        D = OUT // H
        NEG_SLOPE = 0.2

        def _leaky_relu(x):
            return jnp.where(x >= 0, x, NEG_SLOPE * x)

        def _edge_softmax(e, dst, n_nodes):
            m = jax.ops.segment_max(e, dst, num_segments=n_nodes)
            m = jnp.where(jnp.isfinite(m), m, 0.0)
            ex = jnp.exp(e - m[dst])
            s = jax.ops.segment_sum(ex, dst, num_segments=n_nodes)
            return ex / s[dst]
        key = jax.random.key(seed)
        ks = jax.random.split(key, 10)
        return {'X': jax.random.normal(ks[0], (N_NODES, D_IN), dtype=jnp.float32), 'X_edge': jax.random.normal(ks[1], (N_EDGES, D_IN), dtype=jnp.float32), 'W_src': jax.random.normal(ks[2], (OUT, D_IN), dtype=jnp.float32) * 0.05, 'W_dst': jax.random.normal(ks[3], (OUT, D_IN), dtype=jnp.float32) * 0.05, 'W_edge': jax.random.normal(ks[4], (OUT, D_IN), dtype=jnp.float32) * 0.05, 'attn_src': jax.random.normal(ks[5], (H, D), dtype=jnp.float32), 'attn_dst': jax.random.normal(ks[6], (H, D), dtype=jnp.float32), 'attn_edge': jax.random.normal(ks[7], (H, D), dtype=jnp.float32), 'src': jax.random.randint(ks[8], (N_EDGES,), 0, N_NODES, dtype=jnp.int32), 'dst': jax.random.randint(ks[9], (N_EDGES,), 0, N_NODES, dtype=jnp.int32)}
    _L1_gnn_all = _L1_gnn_setup()
    _L1_gnn_in = {k: v for k, v in _L1_gnn_all.items() if k in ('W_src', 'W_dst', 'W_edge', 'attn_src', 'attn_dst', 'attn_edge')}
    del _L1_gnn_all
    return {'x': x, 'src': src, 'dst': dst, 'edge_attr_128': edge_attr_128, 'edge_attr_4': edge_attr_4, 'L0_gnn_t_emb': _L0_gnn_in['t_emb'], 'L0_gnn_c1_w1': _L0_gnn_in['c1_w1'], 'L0_gnn_c1_b1': _L0_gnn_in['c1_b1'], 'L0_gnn_c1_g': _L0_gnn_in['c1_g'], 'L0_gnn_c1_bt': _L0_gnn_in['c1_bt'], 'L0_gnn_c1_w2': _L0_gnn_in['c1_w2'], 'L0_gnn_c1_b2': _L0_gnn_in['c1_b2'], 'L0_gnn_c2_w1': _L0_gnn_in['c2_w1'], 'L0_gnn_c2_b1': _L0_gnn_in['c2_b1'], 'L0_gnn_c2_g': _L0_gnn_in['c2_g'], 'L0_gnn_c2_bt': _L0_gnn_in['c2_bt'], 'L0_gnn_c2_w2': _L0_gnn_in['c2_w2'], 'L0_gnn_c2_b2': _L0_gnn_in['c2_b2'], 'L0_gnn_tm_w': _L0_gnn_in['tm_w'], 'L0_gnn_tm_b': _L0_gnn_in['tm_b'], 'L0_gnn_n1_g': _L0_gnn_in['n1_g'], 'L0_gnn_n1_b': _L0_gnn_in['n1_b'], 'L0_gnn_n2_g': _L0_gnn_in['n2_g'], 'L0_gnn_n2_b': _L0_gnn_in['n2_b'], 'L0_gnn_qw': _L0_gnn_in['qw'], 'L0_gnn_qb': _L0_gnn_in['qb'], 'L0_gnn_kw': _L0_gnn_in['kw'], 'L0_gnn_kb': _L0_gnn_in['kb'], 'L0_gnn_vw': _L0_gnn_in['vw'], 'L0_gnn_vb': _L0_gnn_in['vb'], 'L0_gnn_ew': _L0_gnn_in['ew'], 'L0_gnn_eb': _L0_gnn_in['eb'], 'L0_gnn_ow': _L0_gnn_in['ow'], 'L0_gnn_ob': _L0_gnn_in['ob'], 'L0_gnn_an_g': _L0_gnn_in['an_g'], 'L0_gnn_an_b': _L0_gnn_in['an_b'], 'L1_gnn_W_src': _L1_gnn_in['W_src'], 'L1_gnn_W_dst': _L1_gnn_in['W_dst'], 'L1_gnn_W_edge': _L1_gnn_in['W_edge'], 'L1_gnn_attn_src': _L1_gnn_in['attn_src'], 'L1_gnn_attn_dst': _L1_gnn_in['attn_dst'], 'L1_gnn_attn_edge': _L1_gnn_in['attn_edge']}

def reference(x, src, dst, edge_attr_128, edge_attr_4, L0_gnn_t_emb, L0_gnn_c1_w1, L0_gnn_c1_b1, L0_gnn_c1_g, L0_gnn_c1_bt, L0_gnn_c1_w2, L0_gnn_c1_b2, L0_gnn_c2_w1, L0_gnn_c2_b1, L0_gnn_c2_g, L0_gnn_c2_bt, L0_gnn_c2_w2, L0_gnn_c2_b2, L0_gnn_tm_w, L0_gnn_tm_b, L0_gnn_n1_g, L0_gnn_n1_b, L0_gnn_n2_g, L0_gnn_n2_b, L0_gnn_qw, L0_gnn_qb, L0_gnn_kw, L0_gnn_kb, L0_gnn_vw, L0_gnn_vb, L0_gnn_ew, L0_gnn_eb, L0_gnn_ow, L0_gnn_ob, L0_gnn_an_g, L0_gnn_an_b, L1_gnn_W_src, L1_gnn_W_dst, L1_gnn_W_edge, L1_gnn_attn_src, L1_gnn_attn_dst, L1_gnn_attn_edge):
    import jax
    import jax.numpy as jnp

    def _L0_gnn_ref(x, edge_src, edge_dst, edge_attr, t_emb, c1_w1, c1_b1, c1_g, c1_bt, c1_w2, c1_b2, c2_w1, c2_b1, c2_g, c2_bt, c2_w2, c2_b2, tm_w, tm_b, n1_g, n1_b, n2_g, n2_b, qw, qb, kw, kb, vw, vb, ew, eb, ow, ob, an_g, an_b):
        import jax, jax.numpy as jnp
        import numpy as np
        N, E, D, H, HD, TD, ED, G = (3750, 60000, 128, 8, 16, 512, 4, 8)

        def group_norm(x, gamma, beta, num_groups=G, eps=1e-05):
            n, c = x.shape
            xr = x.reshape(n, num_groups, c // num_groups)
            mu = xr.mean(-1, keepdims=True)
            var = ((xr - mu) ** 2).mean(-1, keepdims=True)
            xn = (xr - mu) * jax.lax.rsqrt(var + eps)
            return xn.reshape(n, c) * gamma + beta

        def mesh_conv(x, src, dst, ea, w1, b1, g, bt, w2, b2):
            m = jnp.concatenate([x[dst], x[src], ea], axis=-1) @ w1 + b1
            m = jax.nn.silu(group_norm(m, g, bt))
            m = m @ w2 + b2
            n = x.shape[0]
            out = jax.ops.segment_sum(m, dst, num_segments=n)
            cnt = jax.ops.segment_sum(jnp.ones((dst.shape[0],), m.dtype), dst, num_segments=n)
            return out / jnp.clip(cnt, 1.0)[:, None]
        src, dst = (edge_src, edge_dst)
        n = x.shape[0]
        h = mesh_conv(x, src, dst, edge_attr, c1_w1, c1_b1, c1_g, c1_bt, c1_w2, c1_b2)
        h = jax.nn.silu(group_norm(h, n1_g, n1_b))
        h = h + (jax.nn.silu(t_emb) @ tm_w + tm_b)
        h = mesh_conv(h, src, dst, edge_attr, c2_w1, c2_b1, c2_g, c2_bt, c2_w2, c2_b2)
        h = jax.nn.silu(group_norm(h, n2_g, n2_b))
        h = h + x
        q = (h @ qw + qb).reshape(n, H, HD)
        k = (h @ kw + kb).reshape(n, H, HD)
        v = (h @ vw + vb).reshape(n, H, HD)
        scale = HD ** (-0.5)
        logits = (q[dst] * k[src]).sum(-1) * scale + (edge_attr @ ew + eb)
        amax = jax.ops.segment_max(logits, dst, num_segments=n)
        pe = jnp.exp(logits - amax[dst])
        ssum = jax.ops.segment_sum(pe, dst, num_segments=n)
        w = pe / jnp.clip(ssum[dst], 1e-06)
        o = jax.ops.segment_sum(w[:, :, None] * v[src], dst, num_segments=n)
        o = o.reshape(n, D) @ ow + ob
        o = group_norm(o, an_g, an_b)
        return h + o

    def _L1_gnn_ref(X, X_edge, W_src, W_dst, W_edge, attn_src, attn_dst, attn_edge, src, dst):
        import jax, jax.numpy as jnp
        import numpy as np
        N_NODES = 6250
        N_EDGES = 100000
        D_IN = 128
        OUT = 128
        H = 4
        D = OUT // H
        NEG_SLOPE = 0.2

        def _leaky_relu(x):
            return jnp.where(x >= 0, x, NEG_SLOPE * x)

        def _edge_softmax(e, dst, n_nodes):
            m = jax.ops.segment_max(e, dst, num_segments=n_nodes)
            m = jnp.where(jnp.isfinite(m), m, 0.0)
            ex = jnp.exp(e - m[dst])
            s = jax.ops.segment_sum(ex, dst, num_segments=n_nodes)
            return ex / s[dst]
        n = X.shape[0]
        h_src = (X @ W_src.T).reshape(n, H, D)
        h_dst = (X @ W_dst.T).reshape(n, H, D)
        e_src = jnp.einsum('nhd,hd->nh', h_src, attn_src)
        e_dst = jnp.einsum('nhd,hd->nh', h_dst, attn_dst)
        e = _leaky_relu(e_src[src] + e_dst[dst])
        a = _edge_softmax(e, dst, n)
        m = a[:, :, None] * h_src[src]
        h_neigh = jax.ops.segment_sum(m, dst, num_segments=n)
        h_edge = (X_edge @ W_edge.T).reshape(-1, H, D)
        e_edge = jnp.einsum('ehd,hd->eh', h_edge, attn_edge)
        e2 = _leaky_relu(e_edge + e_dst[dst])
        a2 = _edge_softmax(e2, dst, n)
        h_edge_agg = jax.ops.segment_sum(a2[:, :, None] * h_edge, dst, num_segments=n)
        h = h_dst + h_neigh + h_edge_agg
        return h.reshape(n, H * D)
    h = jnp.maximum(_layernorm(x, axis=-1), 0.0)
    x = x + _L0_gnn_ref(h, src, dst, edge_attr_4, L0_gnn_t_emb, L0_gnn_c1_w1, L0_gnn_c1_b1, L0_gnn_c1_g, L0_gnn_c1_bt, L0_gnn_c1_w2, L0_gnn_c1_b2, L0_gnn_c2_w1, L0_gnn_c2_b1, L0_gnn_c2_g, L0_gnn_c2_bt, L0_gnn_c2_w2, L0_gnn_c2_b2, L0_gnn_tm_w, L0_gnn_tm_b, L0_gnn_n1_g, L0_gnn_n1_b, L0_gnn_n2_g, L0_gnn_n2_b, L0_gnn_qw, L0_gnn_qb, L0_gnn_kw, L0_gnn_kb, L0_gnn_vw, L0_gnn_vb, L0_gnn_ew, L0_gnn_eb, L0_gnn_ow, L0_gnn_ob, L0_gnn_an_g, L0_gnn_an_b)
    h = jnp.maximum(_layernorm(x, axis=-1), 0.0)
    x = x + _L1_gnn_ref(h, edge_attr_128, L1_gnn_W_src, L1_gnn_W_dst, L1_gnn_W_edge, L1_gnn_attn_src, L1_gnn_attn_dst, L1_gnn_attn_edge, src, dst)
    return x

_drawn_inputs = setup_inputs


def setup_inputs(seed=0):
    import zlib

    import numpy as np

    out = dict(_drawn_inputs(seed))
    spreads = {'L0_gnn_c1_b1': (0.0, 0.1),
     'L0_gnn_c1_g': (1.0, 0.2),
     'L0_gnn_c1_bt': (0.0, 0.484),
     'L0_gnn_c1_b2': (0.0, 0.1),
     'L0_gnn_c2_b1': (0.0, 0.1),
     'L0_gnn_c2_g': (1.0, 0.2),
     'L0_gnn_c2_bt': (0.0, 0.306),
     'L0_gnn_c2_b2': (0.0, 0.1),
     'L0_gnn_tm_b': (0.0, 0.1),
     'L0_gnn_n1_g': (1.0, 0.2),
     'L0_gnn_n1_b': (0.0, 0.349),
     'L0_gnn_n2_g': (1.0, 0.2),
     'L0_gnn_n2_b': (0.0, 0.1),
     'L0_gnn_qb': (0.0, 0.8),
     'L0_gnn_kb': (0.0, 2.0),
     'L0_gnn_vb': (0.0, 0.1),
     'L0_gnn_eb': (0.0, 2.0),
     'L0_gnn_ob': (0.0, 0.1),
     'L0_gnn_an_g': (1.0, 0.2),
     'L0_gnn_an_b': (0.0, 0.1)}
    factors = {'edge_attr_4': 5.259,
     'L0_gnn_qw': 8.0,
     'L0_gnn_kw': 8.0,
     'L0_gnn_ew': 8.0,
     'L1_gnn_attn_dst': 3.134}
    for name, (base, spread) in spreads.items():
        noise = np.random.default_rng([zlib.crc32(name.encode()), seed]).standard_normal(out[name].shape)
        drawn = base * np.exp(spread * noise) if base else spread * noise
        out[name] = jnp.asarray(drawn.astype(out[name].dtype))
    for name, factor in factors.items():
        out[name] = (out[name] * factor).astype(out[name].dtype)
    return out
```

```python
import numpy as np
from contextlib import ExitStack

import concourse.bass as bass
from concourse import mybir

F32, BF16, I32 = mybir.dt.float32, mybir.dt.bfloat16, mybir.dt.int32
ALU, ACT, AX = mybir.AluOpType, mybir.ActivationFunctionType, mybir.AxisListType
ACT_ENGINE, SP_ENGINE = mybir.EngineType.Activation, mybir.EngineType.SP

P = 128
N = 6250
E = 206250
NBLK = -(-N // P)
NP = NBLK * P
NW = NP + P
GB = 7
NGRP = NBLK // GB
GW = GB * P
QT = 4
BT = 16
BQ = BT // QT
QE, BE = QT * P, BT * P
NB = -(-E // BE)
T = NB * BT
EP = T * P
RB = 3
BODY = (NB - 2) // RB
assert NBLK % GB == 0 and BODY * RB + 2 == NB
TC = -(-T // P)
TP = TC * P
ED = 4
H0, D0 = 8, 16
H1, D1 = 4, 32
NS = 8
MR = 32
SMW = MR + NS
EPS = 1e-5
BIG = 1e30
SKIP = 1e6
MAGIC = float(0x5F3759DF)
HEAD = 64


class Batch:

    def __init__(self, q, c):
        self.q, self.c = q, c
        self.i = q * RB + c

    def next(self):
        return Batch(self.q, self.c + 1) if self.c + 1 < RB else Batch(self.q + 1, 0)

    def quad(self, k):
        return self.i * BQ + k


def done(eng, sem, n):
    if not isinstance(n, int) or n > 0:
        eng.wait_ge(sem, n + HEAD)


def settle(eng, passed):
    eng.sem_inc(passed, 1)


def run_batches(eng, step):
    with eng.Fori(0, BODY) as j:
        for c in range(RB):
            b = Batch(j, c)
            step(b, b.next())
    step(Batch(BODY, 0), Batch(BODY, 1))
    step(Batch(BODY, 1), None)


class Chain:

    def __init__(self, eng, sem, base=0):
        self.eng, self.sem, self.base, self.n = eng, sem, base, 0

    def __call__(self, ins):
        self.n += 1
        ins.then_inc(self.sem, 1)
        self.eng.wait_ge(self.sem, self.base + self.n)


def bc(ap, shape):
    return ap.to_broadcast(shape)


def rsqrt(nc, link, x, y, a):
    yi, xi = y.bitcast(I32), x.bitcast(I32)
    link(nc.vector.tensor_scalar(yi, xi, 1, None, ALU.logical_shift_right))
    link(nc.vector.tensor_scalar(yi, yi, -1.0, MAGIC, ALU.mult, ALU.add))
    for _ in range(3):
        link(nc.vector.tensor_tensor(a, y, y, ALU.mult))
        link(nc.vector.scalar_tensor_tensor(a, a, -0.5, x, ALU.mult, ALU.mult))
        link(nc.vector.scalar_tensor_tensor(y, a, 1.5, y, ALU.add, ALU.mult))


def group_norm(nc, link, h, sq, mean, rstd, tmp, gamma, beta, width):
    G = GW // width
    h, sq = h[:, :, :], sq[:, :, :]
    mean, rstd, tmp = mean[:, 0:G], rstd[:, 0:G], tmp[:, 0:G]
    hg, sg = (v.rearrange("p b (g w) -> p (b g) w", w=width) for v in (h, sq))
    wide = [P, G, width]
    link(nc.vector.tensor_reduce(mean, hg, AX.X, ALU.add))
    link(nc.vector.tensor_scalar(mean, mean, 1.0 / width, None, ALU.mult))
    link(nc.vector.tensor_tensor(hg, hg, bc(mean.unsqueeze(2), wide), ALU.subtract))
    link(nc.vector.tensor_tensor(sq, h, h, ALU.mult))
    link(nc.vector.tensor_reduce(mean, sg, AX.X, ALU.add))
    link(nc.vector.tensor_scalar(mean, mean, 1.0 / width, EPS, ALU.mult, ALU.add))
    rsqrt(nc, link, mean, rstd, tmp)
    link(nc.vector.tensor_tensor(hg, hg, bc(rstd.unsqueeze(2), wide), ALU.mult))
    if gamma is not None:
        link(nc.vector.tensor_tensor(h, h, bc(gamma.unsqueeze(1), [P, GB, P]), ALU.mult))
        link(nc.vector.tensor_tensor(h, h, bc(beta.unsqueeze(1), [P, GB, P]), ALU.add))


class Stage:

    def __init__(self, nc, name):
        self.nc, self.name, self.ctx, self.sems = nc, name, ExitStack(), []
        self.passed = self.sem("passed")

    def __enter__(self):
        return self

    def __exit__(self, *exc):
        self.ctx.close()
        if exc[0] is None:
            self.nc.clear_and_free_semaphores(self.sems)
            self.nc.all_engine_barrier()

    def sb(self, name, shape, dt=F32):
        return self.ctx.enter_context(self.nc.sbuf_tensor(f"{self.name}_{name}", shape, dt))

    def ps(self, name, shape):
        return self.ctx.enter_context(self.nc.psum_tensor(f"{self.name}_{name}", shape, F32))

    def sem(self, name):
        s = self.nc.alloc_semaphore(f"{self.name}_{name}")
        self.sems.append(s)
        return s


def prepare(nc, w, C, D):
    with Stage(nc, "prep") as st:
        dst_b = st.sb("dst_b", [NB, P * BT], I32)
        dst_r = st.sb("dst_r", [NB, BE], I32)
        n0_b = st.sb("n0_b", [NB, BT], I32)
        rel_c = st.sb("rel_c", [NB, 2, P * BT])
        rel_f = st.sb("rel_f", [NB, BE])
        rel_h = st.sb("rel_h", [NB, BE], BF16)
        mask = st.sb("mask", [NB, BT, P + 1])
        iota_i = st.sb("iota_i", [P, P], I32)
        iota_pi = st.sb("iota_pi", [P, 1], I32)
        sc_i = st.sb("sc_i", [P, 2, TC], I32)
        sc_f = st.sb("sc_f", [P, 2, TC])
        zero = st.sb("zero", [P, 2 * P + SMW])
        temb = st.sb("temb", [P, 4])
        tmw = st.sb("tmw", [P, 4, P])
        tmb = st.sb("tmb", [1, P])
        te_row = st.sb("te_row", [1, P])
        mean = st.sb("mean", [P, 16])
        wg = st.sb("wg", [P, 3, P])
        attn = st.sb("attn", [P, 3])
        head = st.sb("head", [P, H1])
        abd = st.sb("abd", [P, 3, H1])
        p_te, p_teb = st.ps("p_te", [P, 512]), st.ps("p_teb", [P, 512])
        p_w = st.ps("p_w", [P, 512])
        p_a = st.ps("p_a", [P, 512])
        loaded, cols_stored, stored = st.sem("loaded"), st.sem("cols_stored"), st.sem("stored")
        pool_made, dve_made, chain = st.sem("pool_made"), st.sem("dve_made"), st.sem("chain")
        temb_ready, te_ready, teb_ready = st.sem("temb_ready"), st.sem("te_ready"), st.sem("teb_ready")
        te_copied, wt_ready, heads_ready = st.sem("te_copied"), st.sem("wt_ready"), st.sem("heads_ready")

        loads = [(dst_b[:, :], w["dst_b"]), (dst_r[:, :], w["dst_r"]), (n0_b[:, :], w["n0_b"]),
                 (sc_i[:, 0, :], w["n0_c"]), (sc_i[:, 1, :], w["n0_next"]),
                 (temb[:, :], w["t_emb"].rearrange("(p c) -> p c", p=P)),
                 (tmw[:, :, :], w["tm_w"].rearrange("(p c) f -> p c f", p=P)),
                 (tmb[:, :], w["tm_b"].unsqueeze(0))]
        for l in (1, 2):
            loads += [(C[f"wab{l}"][:, 0, :], w[f"c{l}_w1"][0:P, :]), (C[f"wab{l}"][:, 1, :], w[f"c{l}_w1"][P:2 * P, :]),
                      (C[f"wc{l}"][0:ED, :], w[f"c{l}_w1"][2 * P:2 * P + ED, :]),
                      (C[f"wc{l}"][ED:ED + 1, :], w[f"c{l}_b1"].unsqueeze(0)), (C[f"w2{l}"][:, :], w[f"c{l}_w2"])]
        loads += [(C["wq"][:, :], w["qw"]), (C["wkv"][:, 0, :], w["kw"]), (C["wkv"][:, 1, :], w["vw"]),
                  (C["wo"][:, :], w["ow"]), (C["we"][0:ED, :], w["ew"]), (C["we"][ED:ED + 1, :], w["eb"].unsqueeze(0))]
        for n in ROWS:
            loads.append((C["rows"][:, ROWS.index(n), :], w[n].unsqueeze(0).to_broadcast([P, P])))
        for n, s in enumerate(("src", "dst", "edge")):
            loads += [(wg[:, n, :], w["W_" + s]),
                      (attn[:, n:n + 1], w["attn_" + s].rearrange("h d -> (h d)").unsqueeze(1))]

        block = st.ctx.enter_context(nc.Block())

        @block.sync
        def _(sp):
            for dst, src in loads:
                sp.dma_start(dst, src).then_inc(loaded, 16)
            sp.wait_ge(pool_made, 3)
            for name, width in FOLDED.items():
                sp.dma_start(D[name].rearrange("(b p) c -> p b c", p=P),
                             bc(zero[:, 0:width].unsqueeze(1), [P, NBLK, width])).then_inc(stored, 16)
            for name in ("a1", "a2", "q"):
                sp.dma_start(D[name][NP:NW, :], zero[:, 0:P]).then_inc(stored, 16)
            sp.dma_start(D["ed"][NP:NW, :], zero[:, 0:NS]).then_inc(stored, 16)
            sp.wait_ge(dve_made, 1)
            sp.dma_start(D["cols"].rearrange("b p (a t) -> b a p t", a=2)[:, 0, :, :],
                         rel_c[:, 0, :].rearrange("b (p t) -> b p t", t=BT)).then_inc(stored, 16)
            sp.dma_start(D["cols"].rearrange("b p (a t) -> b a p t", a=2)[:, 1, :, :],
                         rel_c[:, 1, :].rearrange("b (p t) -> b p t", t=BT)).then_inc(stored, 16)
            sp.dma_start(D["places"], rel_h[:, :]).then_inc(stored, 16)
            m = D["mask"].rearrange("(b t h) e -> b t h e", t=BT, h=NS)
            for h in range(NS):
                sp.dma_start(m[:, :, h, :], mask[:, :, :]).then_inc(stored, 16)
            sp.wait_ge(stored, 16 * (len(FOLDED) + 4 + 3 + NS))

        @block.gpsimd
        def _(pool):
            pool.memset(C["ident"][:, :], 0.0).then_inc(pool_made, 1)
            pool.memset(head[:, :], 1.0).then_inc(pool_made, 1)
            pool.memset(zero[:, :], 0.0).then_inc(pool_made, 1)
            pool.memset(C["expand"][:, :, :], 1.0).then_inc(pool_made, 1)
            pool.iota(iota_i[:, :], pattern=[[1, P]], base=0, channel_multiplier=0).then_inc(pool_made, 1)
            pool.iota(iota_pi[:, :], pattern=[[1, 1]], base=0, channel_multiplier=1).then_inc(pool_made, 1)
            pool.wait_ge(pool_made, 6)
            pool.affine_select(out=C["ident"][:, :], in_=C["ident"][:, :], compare_op=ALU.not_equal, fill=1.0,
                               base=0, pattern=[[-1, P]], channel_multiplier=1).then_inc(pool_made, 1)
            pool.affine_select(out=head[:, :], in_=head[:, :], compare_op=ALU.is_ge, fill=0.0,
                               base=0, pattern=[[-D1, H1]], channel_multiplier=1).then_inc(pool_made, 1)
            for n, (first, width) in enumerate(((0, D0), (0, D1), (H1, D1))):
                e = C["expand"][:, n, :]
                pool.affine_select(out=e, in_=e, compare_op=ALU.is_ge, fill=0.0, base=width * (MR + first),
                                   pattern=[[1, P]], channel_multiplier=-width).then_inc(pool_made, 1)
            pool.wait_ge(pool_made, 11)
            pool.affine_select(out=head[:, :], in_=head[:, :], compare_op=ALU.is_ge, fill=0.0,
                               base=D1 - 1, pattern=[[D1, H1]], channel_multiplier=-1).then_inc(pool_made, 1)
            for n, (first, width) in enumerate(((0, D0), (0, D1), (H1, D1))):
                e = C["expand"][:, n, :]
                pool.affine_select(out=e, in_=e, compare_op=ALU.is_ge, fill=0.0, base=width - 1 - width * (MR + first),
                                   pattern=[[-1, P]], channel_multiplier=width).then_inc(pool_made, 1)

        @block.scalar
        def _(act):
            act.wait_ge(loaded, 16 * len(loads))
            act.activation(temb[:, :], temb[:, :], ACT.Silu).then_inc(temb_ready, 1)

        @block.tensor
        def _(pe):
            pe.wait_ge(loaded, 16 * len(loads))
            pe.wait_ge(temb_ready, 1)
            for c in range(4):
                mm = nc.tensor.matmul(p_te[0:1, 0:P], temb[:, c:c + 1], tmw[:, c, :], start=c == 0, stop=c == 3)
            mm.then_inc(te_ready, 1)
            pe.wait_ge(dve_made, 2)
            pe.wait_ge(pool_made, 15)
            nc.tensor.matmul(p_teb[:, 0:P], C["ones"][0:1, :], te_row[:, :], start=True, stop=True).then_inc(teb_ready, 1)
            for n in range(3):
                nc.tensor.transpose(p_w[:, n * P:(n + 1) * P], wg[:, n, :], C["ident"][:, :])
                mm = nc.tensor.matmul(p_a[:, n * H1:(n + 1) * H1], wg[:, n, :], abd[:, n, :], start=True, stop=True)
            mm.then_inc(wt_ready, 1)

        @block.vector
        def _(dve):
            link = Chain(dve, chain)
            dve.wait_ge(pool_made, 6)
            dve.wait_ge(loaded, 16 * len(loads))
            link(nc.vector.tensor_copy(C["iota_row"][:, :], iota_i[:, :]))
            link(nc.vector.tensor_copy(C["iota_col"][:, :], iota_pi[:, :]))
            link(nc.vector.memset(C["ones"][:, :], 1.0))
            n0_e = n0_b[:, :].unsqueeze(1)
            link(nc.vector.tensor_tensor(rel_c[:, 0, :].rearrange("b (p t) -> b p t", t=BT),
                                         dst_b[:, :].rearrange("b (p t) -> b p t", t=BT),
                                         bc(n0_e, [NB, P, BT]), ALU.subtract))
            rel_t = rel_f[:, :].rearrange("b (t e) -> b t e", e=P)
            link(nc.vector.tensor_tensor(rel_t, dst_r[:, :].rearrange("b (t e) -> b t e", e=P),
                                         bc(n0_b[:, :].unsqueeze(2), [NB, BT, P]), ALU.subtract))
            link(nc.vector.tensor_copy(rel_h[:, :], rel_f[:, :]))
            link(nc.vector.memset(rel_c[:, 1, 0:BT], 1.0))
            link(nc.vector.tensor_tensor(rel_c[:, 1, BT:], rel_c[:, 0, BT:], rel_c[:, 0, 0:BE - BT], ALU.not_equal))
            link(nc.vector.memset(mask[:, :, :], -BIG))
            link(nc.vector.tensor_tensor(mask[:, :, 1:P], rel_t[:, :, 1:P], rel_t[:, :, 0:P - 1], ALU.not_equal))
            link(nc.vector.tensor_scalar(mask[:, :, 1:P], mask[:, :, 1:P], -BIG, None, ALU.mult))
            nc.vector.engine_nop().then_inc(dve_made, 1) if False else dve.sem_inc(dve_made, 1)
            link(nc.vector.tensor_copy(sc_f[:, :, :], sc_i[:, :, :]))
            link(nc.vector.tensor_tensor(sc_f[:, 1, :], sc_f[:, 0, :], sc_f[:, 1, :], ALU.is_equal))
            link(nc.vector.scalar_tensor_tensor(C["fold_row"][:, :], sc_f[:, 1, :], SKIP, sc_f[:, 0, :], ALU.mult, ALU.add))
            for l in (1, 2):
                for t, rows, n in ((C[f"wab{l}"], P, 2), (C[f"wc{l}"], ED + 1, 1)):
                    v = t[0:rows].rearrange("p a (g w) -> p (a g) w", w=D0) if n == 2 else \
                        t[0:rows].rearrange("p (g w) -> p g w", w=D0)
                    link(nc.vector.tensor_reduce(mean[0:rows, 0:n * H0], v, AX.X, ALU.add))
                    link(nc.vector.tensor_scalar(mean[0:rows, 0:n * H0], mean[0:rows, 0:n * H0], 1.0 / D0, None, ALU.mult))
                    link(nc.vector.tensor_tensor(v, v, bc(mean[0:rows, 0:n * H0].unsqueeze(2), [rows, n * H0, D0]), ALU.subtract))
            dve.wait_ge(te_ready, 1)
            link(nc.vector.tensor_tensor(te_row[:, :], p_te[0:1, 0:P], tmb[:, :], ALU.add))
            dve.wait_ge(pool_made, 15)
            for n in range(3):
                link(nc.vector.tensor_scalar(abd[:, n, :], head[:, :], attn[:, n:n + 1], None, ALU.mult))
            dve.sem_inc(dve_made, 1)
            dve.wait_ge(teb_ready, 1)
            link(nc.vector.tensor_copy(C["te"][:, :], p_teb[:, 0:P]))
            dve.wait_ge(wt_ready, 1)
            link(nc.vector.tensor_copy(C["wsd"][:, :, :], p_w[:, 0:2 * P].rearrange("p (a f) -> p a f", a=2)))
            link(nc.vector.tensor_copy(C["wet"][:, :], p_w[:, 2 * P:3 * P]))
            link(nc.vector.tensor_copy(C["wsa"][:, 0:2 * H1], p_a[:, 0:2 * H1]))
            link(nc.vector.tensor_copy(C["wsa"][:, 2 * H1:3 * H1], p_a[:, H1:2 * H1]))
            link(nc.vector.tensor_copy(C["wea"][:, :], p_a[:, 2 * H1:3 * H1]))


ROWS = ["c1_g", "c1_bt", "c1_b2", "n1_g", "n1_b", "c2_g", "c2_bt", "c2_b2", "n2_g", "n2_b", "qb", "kb", "vb",
        "ob", "an_g", "an_b"]
FOLDED = {"fold1": P + 1, "fold2": P, "fold3": P + SMW, "fold4": 2 * P + SMW}


def row(C, name):
    return C["rows"][:, ROWS.index(name), :]


def conv_edges(nc, l, w, C, D, acc, first, count, first_count):
    a_table, b_table = D[f"a{l}"], D[f"b{l}"]
    gamma, beta, wc = row(C, f"c{l}_g"), row(C, f"c{l}_bt"), C[f"wc{l}"]
    GQ, WQ, PQ = RB * BQ, 4, 6
    with Stage(nc, f"conv{l}") as st:
        idx = st.sb("idx", [P, RB, BT], I32)
        cols = st.sb("cols", [P, RB, 2 * BT])
        n0 = st.sb("n0", [1, RB, BT], I32)
        gath = st.sb("gath", [P, GQ, QT, P])
        win = st.sb("win", [P, WQ, QT, P])
        ea = st.sb("ea", [ED + 1, WQ, QE])
        places = st.sb("places", [P, PQ, QE], BF16)
        hotT = st.sb("hotT", [P, PQ, QE])
        hot = st.sb("hot", [P, 2, QT, P])
        sq = st.sb("sq", [P, 2, QE])
        var, rstd, tmp = st.sb("var", [P, BT * H0]), st.sb("rstd", [P, BT * H0]), st.sb("tmp", [P, BT * H0])
        u = st.sb("u", [P, 2, QE])
        m = st.sb("m", [P, 2, QE])
        z = [st.ps(f"z{n}", [P, QE]) for n in range(4)]
        sums = [st.ps(f"sums{n}", [P, QE]) for n in range(2)]
        counts = [st.ps(f"counts{n}", [P, QE]) for n in range(2)]

        meta_landed = [st.sem(f"meta_landed{c}") for c in range(RB)]
        gath_landed = [st.sem(f"gath_landed{n}") for n in range(GQ)]
        win_landed = [st.sem(f"win_landed{n}") for n in range(WQ)]
        places_landed = [st.sem(f"places_landed{n}") for n in range(PQ)]
        hotT_ready, hot_ready, var_ready, normed, u_ready = (
            st.sem(n) for n in ("hotT_ready", "hot_ready", "var_ready", "normed", "u_ready"))
        scaled, newton = st.sem("scaled"), st.sem("newton")
        z_ready, sums_ready = st.sem("z_ready"), st.sem("sums_ready")
        sq_ready, m_ready, sums_copied, first_copied = (
            st.sem(n) for n in ("sq_ready", "m_ready", "sums_copied", "first_copied"))
        cleared = st.sem("cleared")
        META = 3 * 16
        NEWTON = 12
        block = st.ctx.enter_context(nc.Block())

        @block.sync
        def _(sp):
            def fetch(b, _):
                done(sp, z_ready, (b.i - RB + 1) * BQ)
                done(sp, hot_ready, (b.i - RB + 1) * BQ)
                done(sp, sums_copied, (b.i - RB) * BT + 1)
                settle(sp, st.passed)
                sp.dma_start(idx[:, b.c, :], w["src_b"][bass.ds(b.i, 1), :, :].rearrange("a p t -> (a p) t"))\
                  .then_inc(meta_landed[b.c], 16)
                sp.dma_start(cols[:, b.c, :], D["cols"][bass.ds(b.i, 1), :, :].rearrange("a p t -> (a p) t"))\
                  .then_inc(meta_landed[b.c], 16)
                sp.dma_start(n0[:, b.c, :], w["n0_b"][bass.ds(b.i, 1), :]).then_inc(meta_landed[b.c], 16)
                sp.wait_ge(meta_landed[b.c], (b.q + 1) * META)
                settle(sp, st.passed)
                _, starts = nc.values_load_multi_w_load_instructions(
                    n0[0:1, b.c, :], engines=(SP_ENGINE,), min_val=0, max_val=N,
                    skip_runtime_bounds_check_because="destinations are node numbers")
                for k in range(BQ):
                    s6, s4 = (b.c * BQ + k) % PQ, k
                    done(sp, hotT_ready, b.quad(k) - PQ + 1)
                    settle(sp, st.passed)
                    sp.dma_start(places[:, s6, :],
                                 D["places"][bass.ds(b.i, 1), k * QE:(k + 1) * QE].to_broadcast([P, QE]))\
                      .then_inc(places_landed[s6], 16)
                    done(sp, z_ready, b.quad(k) - WQ + 1)
                    settle(sp, st.passed)
                    sp.dma_start(ea[:, s4, :], w["ea"][:, bass.ds(b.i * BE + k * QE, QE)]).then_inc(win_landed[s4], 16)
                    for t in range(QT):
                        sp.dma_start(win[:, s4, t, :], a_table[bass.ds(starts[k * QT + t], P), :])\
                          .then_inc(win_landed[s4], 16)
            run_batches(sp, fetch)

        @block.gpsimd
        def _(pool):
            def gather(b, _):
                pool.wait_ge(meta_landed[b.c], (b.q + 1) * META)
                for k in range(BQ):
                    done(pool, z_ready, b.quad(k) - GQ + 1)
                    settle(pool, st.passed)
                    for t in range(QT):
                        pool.indirect_dma_start(
                            gath[:, b.c * BQ + k, t, :], None, b_table,
                            bass.IndirectOffsetOnAxis(ap=idx[:, b.c, k * QT + t:k * QT + t + 1], axis=0))\
                            .then_inc(gath_landed[b.c * BQ + k], 16)
            run_batches(pool, gather)

        @block.tensor
        def _(pe):
            pe.sem_inc(z_ready, HEAD)
            pe.sem_inc(sums_ready, HEAD)

            def pre_activation(b, k):
                s6, s4, s12 = (b.c * BQ + k) % PQ, k, b.c * BQ + k
                pe.wait_ge(gath_landed[s12], (b.q + 1) * QT * 16)
                done(pe, normed, b.quad(k) - 4 + 1)
                nc.tensor.matmul(z[k][:, :], C["ident"][:, :], gath[:, s12, :, :].rearrange("p t f -> p (t f)"),
                                 start=True, stop=False, skip_group_check=True)
                pe.wait_ge(win_landed[s4], (b.i + 1) * (QT + 1) * 16)
                done(pe, hotT_ready, b.quad(k) + 1)
                for t in range(QT):
                    zt = z[k][:, t * P:(t + 1) * P]
                    nc.tensor.matmul(zt, hotT[:, s6, t * P:(t + 1) * P], win[:, s4, t, :], start=False, stop=False,
                                     skip_group_check=True)
                    mm = nc.tensor.matmul(zt, ea[:, s4, t * P:(t + 1) * P], wc[:, :], start=False, stop=t == QT - 1,
                                          skip_group_check=True)
                mm.then_inc(z_ready, 1)

            def sum_up(b, k):
                s2, g = k % 2, b.quad(k)
                done(pe, m_ready, g + 1)
                done(pe, hot_ready, g + 1)
                done(pe, first_copied, g - 2 + 1)
                for t in range(QT):
                    mm = nc.tensor.matmul(sums[s2][:, t * P:(t + 1) * P], m[:, s2, t * P:(t + 1) * P], hot[:, s2, t, :],
                                          start=True, stop=True)
                if l == 1:
                    mm = nc.tensor.matmul(counts[s2][0:1, :], C["ones"][:, 0:1],
                                          hot[:, s2, :, :].rearrange("p t n -> p (t n)"), start=True, stop=True)
                mm.then_inc(sums_ready, 1)

            def step(b, nxt):
                for k in range(BQ):
                    if nxt:
                        pre_activation(nxt, k)
                    sum_up(b, k)
            for k in range(BQ):
                pre_activation(Batch(0, 0), k)
            run_batches(pe, step)

        @block.scalar
        def _(act):
            for s in (sq_ready, m_ready, sums_copied, first_copied):
                act.sem_inc(s, HEAD)

            def square(b, k):
                g, s2 = b.quad(k), k % 2
                done(act, z_ready, g + 1)
                done(act, var_ready, g - 2 + 1)
                act.activation(sq[:, s2, :], z[k][:, :], ACT.Square, scale=D0 ** -0.5).then_inc(sq_ready, 1)

            def copies(b, k, starts):
                g, s2 = b.quad(k), k % 2
                done(act, sums_ready, g + 1)
                for t in range(QT):
                    n = g * QT + t
                    done(act, sums_copied, n)
                    if l == 1:
                        act.copy(count[:, bass.ds(starts[k * QT + t] + 1, P - 1)],
                                 counts[s2][0:1, t * P + 1:(t + 1) * P])
                    act.copy(acc[:, bass.ds(starts[k * QT + t] + 1, P - 1)], sums[s2][:, t * P + 1:(t + 1) * P])\
                       .then_inc(sums_copied, 1)
                if l == 1:
                    act.copy(first_count[:, bass.ds(g * QT, QT)],
                             counts[s2][0:1, :].rearrange("p (t n) -> p t n", n=P)[:, :, 0])
                act.copy(first[:, bass.ds(g * QT, QT)], sums[s2][:, :].rearrange("p (t n) -> p t n", n=P)[:, :, 0])\
                   .then_inc(first_copied, 1)

            def step(b, nxt):
                act.wait_ge(meta_landed[b.c], (b.q + 1) * META)
                settle(act, st.passed)
                _, starts = nc.values_load_multi_w_load_instructions(
                    n0[0:1, b.c, :], engines=(ACT_ENGINE,), min_val=0, max_val=N,
                    skip_runtime_bounds_check_because="destinations are node numbers")
                for k in range(BQ):
                    g, s2 = b.quad(k), k % 2
                    done(act, u_ready, g + 1)
                    done(act, sums_ready, g - 2 + 1)
                    act.activation(m[:, s2, :], u[:, s2, :], ACT.Silu).then_inc(m_ready, 1)
                    if nxt:
                        square(nxt, k)
                    copies(b, k, starts)
            act.wait_ge(cleared, 1)
            for k in range(BQ):
                square(Batch(0, 0), k)
            run_batches(act, step)

        @block.vector
        def _(dve):
            for s in (hotT_ready, hot_ready, var_ready, normed, scaled, u_ready):
                dve.sem_inc(s, HEAD)
            nc.vector.memset(first[:, :], 0.0)
            if l == 1:
                nc.vector.memset(count[:, :], 0.0)
                nc.vector.memset(first_count[:, :], 0.0)
            nc.vector.memset(acc[:, :], 0.0).then_inc(cleared, 1)

            def one_hot_T(b, k):
                s6 = (b.c * BQ + k) % PQ
                dve.wait_ge(places_landed[s6], ((b.i * BQ + k) // PQ + 1) * 16 if isinstance(b.i, int)
                            else (b.q * (GQ // PQ) + (b.c * BQ + k) // PQ + 1) * 16)
                done(dve, z_ready, b.quad(k) - PQ + 1)
                nc.vector.tensor_scalar(hotT[:, s6, :], places[:, s6, :], C["iota_col"][:, 0:1], None, ALU.is_equal)\
                  .then_inc(hotT_ready, 1)

            def step(b, nxt):
                dve.wait_ge(meta_landed[b.c], (b.q + 1) * META)
                for k in range(BQ):
                    done(dve, sq_ready, b.quad(k) + 1)
                    if k == 0:
                        done(dve, normed, b.quad(0))
                    nc.vector.tensor_reduce(var[:, k * QT * H0:(k + 1) * QT * H0],
                                            sq[:, k % 2, :].rearrange("p (g w) -> p g w", w=D0), AX.X, ALU.add)\
                      .then_inc(var_ready, 1)
                done(dve, var_ready, b.quad(BQ))
                link = Chain(dve, newton, b.i * NEWTON)
                link(nc.vector.tensor_scalar(var[:, :], var[:, :], EPS, None, ALU.add))
                rsqrt(nc, link, var[:, :], rstd[:, :], tmp[:, :])
                assert link.n == NEWTON
                for k in range(BQ):
                    g, s2 = b.quad(k), k % 2
                    if nxt:
                        one_hot_T(nxt, k)
                    done(dve, m_ready, g - 2 + 1)
                    ug = u[:, s2, :].rearrange("p (g w) -> p g w", w=D0)
                    ut = u[:, s2, :].rearrange("p (t f) -> p t f", f=P)
                    r = rstd[:, k * QT * H0:(k + 1) * QT * H0].unsqueeze(2)
                    nc.vector.tensor_tensor(ug, z[k][:, :].rearrange("p (g w) -> p g w", w=D0),
                                            bc(r, [P, QT * H0, D0]), ALU.mult).then_inc(normed, 1)
                    done(dve, sums_ready, g - 2 + 1)
                    for t in range(QT):
                        ins = nc.vector.tensor_scalar(hot[:, s2, t, :], C["iota_row"][:, :],
                                                      cols[:, b.c, k * QT + t:k * QT + t + 1], None, ALU.is_equal)
                    ins.then_inc(hot_ready, 1)
                    done(dve, normed, g + 1)
                    nc.vector.tensor_tensor(ut, ut, bc(gamma.unsqueeze(1), [P, QT, P]), ALU.mult).then_inc(scaled, 1)
                    done(dve, scaled, g + 1)
                    nc.vector.tensor_tensor(ut, ut, bc(beta.unsqueeze(1), [P, QT, P]), ALU.add).then_inc(u_ready, 1)
            for k in range(BQ):
                one_hot_T(Batch(0, 0), k)
            run_batches(dve, step)


def attention_edges(nc, gat, w, C, D, acc, first, acc_e, first_e, small, first_small):
    table = D["g"] if gat else D["kv"]
    RW = P + H1 if gat else 2 * P
    win_table, WW = (D["ed"], NS) if gat else (D["q"], P)
    GQ, WQ, PQ, XQ = RB * BQ, 4, 4, 6
    with Stage(nc, "gat" if gat else "attn") as st:
        idx = st.sb("idx", [P, RB, BT], I32)
        cols = st.sb("cols", [P, RB, 2 * BT])
        n0 = st.sb("n0", [1, RB, BT], I32)
        mask = st.sb("mask", [P, RB, P + 1])
        gath = st.sb("gath", [P, GQ, QT, RW])
        win = st.sb("win", [P, WQ, QT, WW])
        places = st.sb("places", [P, PQ, QE], BF16)
        hotT = st.sb("hotT", [P, PQ, QE])
        hot = st.sb("hot", [P, 2, QT, P])
        logit = st.sb("logit", [P, BT, NS])
        logit2 = st.sb("logit2", [P, BT, NS])
        run_max, seg_max = st.sb("run_max", [P, P]), st.sb("seg_max", [P, P])
        below = st.sb("below", [P, P])
        sm = st.sb("sm", [P, RB, BT, SMW])
        val = st.sb("val", [P, 2, QT, P])
        p_logit = st.ps("p_logit", [P, 512])
        p_turn = st.ps("p_turn", [P, 512])
        if gat:
            xe = st.sb("xe", [P, WQ, QT, P])
            xeT = st.sb("xeT", [P, XQ, QE])
            val_e = st.sb("val_e", [P, 2, QT, P])
            p_xeT, p_he = st.ps("p_xeT", [P, QE]), st.ps("p_he", [P, QE])
            sums, sums_e, smalls = ([st.ps("sums", [P, QE])], [st.ps("sums_e", [P, QE])], [st.ps("smalls", [P, QE])])
        else:
            ea = st.sb("ea", [ED + 1, WQ, QE])
            prod = st.sb("prod", [P, 2, QE])
            p_q = [st.ps(f"p_q{n}", [P, QE]) for n in range(2)]
            sums = [st.ps(f"sums{n}", [P, QE]) for n in range(2)]
            smalls = [st.ps(f"smalls{n}", [P, QE]) for n in range(2)]
        NO = len(sums)

        meta_landed = [st.sem(f"meta_landed{c}") for c in range(RB)]
        gath_landed = [st.sem(f"gath_landed{n}") for n in range(GQ)]
        win_landed = [st.sem(f"win_landed{n}") for n in range(WQ)]
        places_landed = [st.sem(f"places_landed{n}") for n in range(PQ)]
        hotT_ready, hot_ready, cleared = st.sem("hotT_ready"), st.sem("hot_ready"), st.sem("cleared")
        scored, sums_ready, first_copied, small_copied = (
            st.sem(n) for n in ("scored", "sums_ready", "first_copied", "small_copied"))
        logit_ready, logitT_ready, below_ready, ex_ready, turned = (
            st.sem(n) for n in ("logit_ready", "logitT_ready", "below_ready", "ex_ready", "turned"))
        sm_ready, val_ready, chain = st.sem("sm_ready"), st.sem("val_ready"), st.sem("chain")
        part_ready, sums_copied, edge_copied = st.sem("part_ready"), st.sem("sums_copied"), st.sem("edge_copied")
        xeT_ready, xeT_copied, he_ready, val_e_ready = (
            st.sem(n) for n in ("xeT_ready", "xeT_copied", "he_ready", "val_e_ready"))
        META = 4 * 16
        WINS = (QT + 1) * 16
        CHAIN = 6 if gat else 4
        block = st.ctx.enter_context(nc.Block())

        @block.sync
        def _(sp):
            def fetch(b, _):
                done(sp, scored, (b.i - RB + 1) * BQ)
                done(sp, hot_ready, (b.i - RB + 1) * BQ)
                done(sp, small_copied, (b.i - RB) * BT + 1)
                settle(sp, st.passed)
                sp.dma_start(idx[:, b.c, :], w["src_b"][bass.ds(b.i, 1), :, :].rearrange("a p t -> (a p) t"))\
                  .then_inc(meta_landed[b.c], 16)
                sp.dma_start(cols[:, b.c, :], D["cols"][bass.ds(b.i, 1), :, :].rearrange("a p t -> (a p) t"))\
                  .then_inc(meta_landed[b.c], 16)
                sp.dma_start(n0[:, b.c, :], w["n0_b"][bass.ds(b.i, 1), :]).then_inc(meta_landed[b.c], 16)
                sp.dma_start(mask[:, b.c, :], D["mask"][bass.ds(b.i * P, P), :]).then_inc(meta_landed[b.c], 16)
                sp.wait_ge(meta_landed[b.c], (b.q + 1) * META)
                settle(sp, st.passed)
                _, starts = nc.values_load_multi_w_load_instructions(
                    n0[0:1, b.c, :], engines=(SP_ENGINE,), min_val=0, max_val=N,
                    skip_runtime_bounds_check_because="destinations are node numbers")
                for k in range(BQ):
                    s6, s4 = (b.c * BQ + k) % PQ, k
                    done(sp, hotT_ready, b.quad(k) - PQ + 1)
                    settle(sp, st.passed)
                    sp.dma_start(places[:, s6, :],
                                 D["places"][bass.ds(b.i, 1), k * QE:(k + 1) * QE].to_broadcast([P, QE]))\
                      .then_inc(places_landed[s6], 16)
                    done(sp, scored, b.quad(k) - WQ + 1)
                    settle(sp, st.passed)
                    if gat:
                        sp.dma_start(xe[:, s4, :, :], w["xe"][bass.ds(b.i * BE + k * QE, QE), :]
                                     .rearrange("(t p) f -> p t f", p=P)).then_inc(win_landed[s4], 16)
                    else:
                        sp.dma_start(ea[:, s4, :], w["ea"][:, bass.ds(b.i * BE + k * QE, QE)])\
                          .then_inc(win_landed[s4], 16)
                    for t in range(QT):
                        sp.dma_start(win[:, s4, t, :], win_table[bass.ds(starts[k * QT + t], P), :])\
                          .then_inc(win_landed[s4], 16)
            run_batches(sp, fetch)

        @block.gpsimd
        def _(pool):
            def gather(b, _):
                pool.wait_ge(meta_landed[b.c], (b.q + 1) * META)
                for k in range(BQ):
                    done(pool, val_ready, b.quad(k) - GQ + 1)
                    settle(pool, st.passed)
                    for t in range(QT):
                        pool.indirect_dma_start(
                            gath[:, b.c * BQ + k, t, :], None, table,
                            bass.IndirectOffsetOnAxis(ap=idx[:, b.c, k * QT + t:k * QT + t + 1], axis=0))\
                            .then_inc(gath_landed[b.c * BQ + k], 16)
            run_batches(pool, gather)

        @block.tensor
        def _(pe):
            for s in (scored, sums_ready, logitT_ready, turned, xeT_ready, he_ready):
                pe.sem_inc(s, HEAD)

            def score(b, k):
                s6, s4, g = (b.c * BQ + k) % PQ, k, b.quad(k)
                pe.wait_ge(win_landed[s4], (b.i + 1) * WINS)
                if gat:
                    done(pe, xeT_copied, g)
                    for t in range(QT):
                        mm = nc.tensor.transpose(p_xeT[:, t * P:(t + 1) * P], xe[:, s4, t, :], C["ident"][:, :])
                    mm.then_inc(xeT_ready, 1)
                done(pe, hotT_ready, g + 1)
                if k == 0:
                    done(pe, logit_ready, b.i)
                if gat:
                    done(pe, xeT_copied, g + 1)
                else:
                    done(pe, part_ready, g - 2 + 1)
                for t in range(QT):
                    e = slice(t * P, (t + 1) * P)
                    lt = p_logit[:, (k * QT + t) * NS:(k * QT + t + 1) * NS]
                    if gat:
                        nc.tensor.matmul(lt, hotT[:, s6, e], win[:, s4, t, :], start=True, stop=False,
                                         skip_group_check=True)
                        mm = nc.tensor.matmul(lt[:, H1:NS], xeT[:, (b.c * BQ + k) % XQ, e], C["wea"][:, :], start=False, stop=True,
                                              skip_group_check=True)
                    else:
                        nc.tensor.matmul(p_q[k % 2][:, e], hotT[:, s6, e], win[:, s4, t, :], start=True, stop=True)
                        mm = nc.tensor.matmul(lt, ea[:, s4, e], C["we"][:, :], start=True, stop=True)
                mm.then_inc(scored, 1)

            def softmax(b):
                done(pe, logit_ready, b.i + 1)
                nc.tensor.transpose(p_turn[:, 0:P], logit2[:, :, :].rearrange("p t s -> p (t s)"), C["ident"][:, :])\
                  .then_inc(logitT_ready, 1)
                done(pe, ex_ready, b.i + 1)
                nc.tensor.transpose(p_turn[:, P:2 * P], below[:, :], C["ident"][:, :])
                nc.tensor.transpose(p_turn[:, 2 * P:3 * P], seg_max[:, :], C["ident"][:, :]).then_inc(turned, 1)

            def sum_up(b, k):
                s2, g, so = k % 2, b.quad(k), k % NO
                if gat:
                    done(pe, val_e_ready, g)
                    for t in range(QT):
                        mm = nc.tensor.matmul(p_he[:, t * P:(t + 1) * P],
                                              xeT[:, (b.c * BQ + k) % XQ, t * P:(t + 1) * P], C["wet"][:, :],
                                              start=True, stop=True)
                    mm.then_inc(he_ready, 1)
                done(pe, hot_ready, g + 1)
                done(pe, val_ready, g + 1)
                done(pe, sm_ready, b.i + 1)
                done(pe, first_copied, g - NO + 1)
                for t in range(QT):
                    nc.tensor.matmul(smalls[so][0:SMW, t * P:(t + 1) * P], sm[:, b.c, k * QT + t, :], hot[:, s2, t, :],
                                     start=True, stop=True)
                for t in range(QT):
                    mm = nc.tensor.matmul(sums[so][:, t * P:(t + 1) * P], val[:, s2, t, :], hot[:, s2, t, :],
                                          start=True, stop=True)
                if gat:
                    done(pe, val_e_ready, g + 1)
                    for t in range(QT):
                        mm = nc.tensor.matmul(sums_e[so][:, t * P:(t + 1) * P], val_e[:, s2, t, :], hot[:, s2, t, :],
                                              start=True, stop=True)
                mm.then_inc(sums_ready, 1)

            def step(b, nxt):
                for k in range(BQ):
                    if nxt:
                        score(nxt, k)
                    sum_up(b, k)
                if nxt:
                    softmax(nxt)
            for k in range(BQ):
                score(Batch(0, 0), k)
            softmax(Batch(0, 0))
            run_batches(pe, step)

        @block.scalar
        def _(act):
            for s in (ex_ready, first_copied, sums_copied, small_copied, xeT_copied, edge_copied):
                act.sem_inc(s, HEAD)

            def keep_edges(b, k):
                g = b.quad(k)
                done(act, xeT_ready, g + 1)
                done(act, he_ready, g - XQ + 1)
                act.copy(xeT[:, (b.c * BQ + k) % XQ, :], p_xeT[:, :]).then_inc(xeT_copied, 1)

            def exponent(b):
                done(act, below_ready, b.i + 1)
                act.activation(below[:, :], below[:, :], ACT.Exp).then_inc(ex_ready, 1)

            def copies(b, k, starts):
                g, so = b.quad(k), k % NO
                done(act, sums_ready, g + 1)
                outs = [(small, smalls[so][0:SMW, :], small_copied), (acc, sums[so][:, :], sums_copied)]
                if gat:
                    outs.append((acc_e, sums_e[so][:, :], edge_copied))
                for t in range(QT):
                    for kept, new, copied in outs:
                        done(act, copied, g * QT + t)
                        act.copy(kept[:, bass.ds(starts[k * QT + t] + 1, P - 1)], new[:, t * P + 1:(t + 1) * P])\
                           .then_inc(copied, 1)
                firsts = [(first_small, smalls[so][0:SMW, :])] + ([(first_e, sums_e[so][:, :])] if gat else []) + \
                         [(first, sums[so][:, :])]
                for kept, new in firsts:
                    ins = act.copy(kept[:, bass.ds(g * QT, QT)], new.rearrange("p (t n) -> p t n", n=P)[:, :, 0])
                ins.then_inc(first_copied, 1)

            def step(b, nxt):
                act.wait_ge(meta_landed[b.c], (b.q + 1) * META)
                settle(act, st.passed)
                _, starts = nc.values_load_multi_w_load_instructions(
                    n0[0:1, b.c, :], engines=(ACT_ENGINE,), min_val=0, max_val=N,
                    skip_runtime_bounds_check_because="destinations are node numbers")
                for k in range(BQ):
                    if nxt and gat:
                        keep_edges(nxt, k)
                    copies(b, k, starts)
                if nxt:
                    exponent(nxt)
            act.wait_ge(cleared, 1)
            if gat:
                for k in range(BQ):
                    keep_edges(Batch(0, 0), k)
            exponent(Batch(0, 0))
            run_batches(act, step)

        @block.vector
        def _(dve):
            for s in (hotT_ready, hot_ready, logit_ready, below_ready, sm_ready, val_ready, part_ready, val_e_ready, chain):
                dve.sem_inc(s, HEAD)
            nc.vector.memset(sm[:, :, :, :], 0.0)
            nc.vector.memset(small[:, :], 0.0)
            nc.vector.memset(first_small[:, :], 0.0)
            nc.vector.memset(first[:, :], 0.0)
            if gat:
                nc.vector.memset(acc_e[:, :], 0.0)
                nc.vector.memset(first_e[:, :], 0.0)
            nc.vector.memset(acc[:, :], 0.0).then_inc(cleared, 1)
            dve.wait_ge(cleared, 1)

            def one_hot_T(b, k):
                s6 = (b.c * BQ + k) % PQ
                dve.wait_ge(places_landed[s6], (b.q * (GQ // PQ) + (b.c * BQ + k) // PQ + 1) * 16)
                done(dve, scored, b.quad(k) - PQ + 1)
                nc.vector.tensor_scalar(hotT[:, s6, :], places[:, s6, :], C["iota_col"][:, 0:1], None, ALU.is_equal)\
                  .then_inc(hotT_ready, 1)

            def score(b, k):
                if gat:
                    return
                g, s12, s2 = b.quad(k), b.c * BQ + k, k % 2
                dve.wait_ge(gath_landed[s12], (b.q + 1) * QT * 16)
                done(dve, scored, g + 1)
                nc.vector.tensor_tensor(prod[:, s2, :].rearrange("p (t f) -> p t f", f=P),
                                        p_q[s2][:, :].rearrange("p (t f) -> p t f", f=P), gath[:, s12, :, 0:P], ALU.mult)\
                  .then_inc(part_ready, 1)

            def part(b, k):
                if gat:
                    return
                done(dve, part_ready, b.quad(k) + 1)
                if k == 0:
                    done(dve, logit_ready, b.i)
                nc.vector.tensor_reduce(logit[:, k * QT:(k + 1) * QT, :].rearrange("p t s -> p (t s)"),
                                        prod[:, k % 2, :].rearrange("p (g w) -> p g w", w=D0), AX.X, ALU.add)\
                  .then_inc(chain, 1)

            def softmax(b):
                dve.wait_ge(meta_landed[b.c], (b.q + 1) * META)
                own = (CHAIN + (0 if gat else BQ)) * b.i + HEAD + (0 if gat else BQ)
                link = Chain(dve, chain, own)
                pl = p_logit[:, 0:P].rearrange("p (t s) -> p t s", s=NS)
                done(dve, scored, b.quad(BQ))
                done(dve, logitT_ready, b.i)
                if gat:
                    for k in range(BQ):
                        dve.wait_ge(gath_landed[b.c * BQ + k], (b.q + 1) * QT * 16)
                    g = gath[:, b.c * BQ:(b.c + 1) * BQ, :, P:RW].rearrange("p q t s -> p (q t) s")
                    link(nc.vector.tensor_tensor(logit[:, :, 0:H1], pl[:, :, 0:H1], g, ALU.add))
                    link(nc.vector.tensor_copy(logit[:, :, H1:NS], pl[:, :, H1:NS]))
                    nc.vector.scalar_tensor_tensor(logit2[:, :, :], logit[:, :, :], 0.2, logit[:, :, :],
                                                   ALU.mult, ALU.max).then_inc(logit_ready, 1)
                else:
                    dve.wait_ge(chain, own)
                    nc.vector.tensor_tensor(logit2[:, :, :], logit[:, :, :], pl, ALU.add).then_inc(logit_ready, 1)
                done(dve, logitT_ready, b.i + 1)
                done(dve, turned, b.i)
                link(nc.vector.tensor_tensor_scan(run_max[:, :], mask[:, b.c, 0:P], p_turn[:, 0:P], -BIG, ALU.add, ALU.max))
                link(nc.vector.tensor_tensor_scan(seg_max[:, ::-1], mask[:, b.c, P:0:-1], run_max[:, ::-1], -BIG,
                                                  ALU.add, ALU.max))
                nc.vector.tensor_tensor(below[:, :], p_turn[:, 0:P], seg_max[:, :], ALU.subtract).then_inc(below_ready, 1)
                done(dve, turned, b.i + 1)
                done(dve, sums_ready, (b.i - RB + 1) * BQ)
                pt = p_turn[:, P:3 * P].rearrange("p (a t s) -> p a t s", a=2, s=NS)
                link(nc.vector.tensor_copy(sm[:, b.c, :, 0:NS], pt[:, 0, :, :]))
                link_last = nc.vector.tensor_tensor(sm[:, b.c, :, MR:SMW], pt[:, 1, :, :],
                                                    bc(cols[:, b.c, BT:2 * BT].unsqueeze(2), [P, BT, NS]), ALU.mult)
                link_last.then_inc(sm_ready, 1)
                dve.wait_ge(chain, own + link.n)
                if link.n < CHAIN:
                    dve.sem_inc(chain, CHAIN - link.n)

            def weigh(b, k):
                g, s2, s12 = b.quad(k), k % 2, b.c * BQ + k
                done(dve, sums_ready, g - 2 + 1)
                done(dve, sm_ready, b.i + 1)
                wts = sm[:, b.c, k * QT:(k + 1) * QT, :]
                if gat:
                    nc.vector.tensor_tensor(val[:, s2, :, :].rearrange("p t (h d) -> p t h d", d=D1),
                                            gath[:, s12, :, 0:P].rearrange("p t (h d) -> p t h d", d=D1),
                                            bc(wts[:, :, 0:H1].unsqueeze(3), [P, QT, H1, D1]), ALU.mult).then_inc(val_ready, 1)
                else:
                    nc.vector.tensor_tensor(val[:, s2, :, :].rearrange("p t (h d) -> p t h d", d=D0),
                                            gath[:, s12, :, P:2 * P].rearrange("p t (h d) -> p t h d", d=D0),
                                            bc(wts[:, :, 0:H0].unsqueeze(3), [P, QT, H0, D0]), ALU.mult).then_inc(val_ready, 1)
                for t in range(QT):
                    ins = nc.vector.tensor_scalar(hot[:, s2, t, :], C["iota_row"][:, :],
                                                  cols[:, b.c, k * QT + t:k * QT + t + 1], None, ALU.is_equal)
                ins.then_inc(hot_ready, 1)
                if gat:
                    done(dve, he_ready, g + 1)
                    nc.vector.tensor_tensor(val_e[:, s2, :, :].rearrange("p t (h d) -> p t h d", d=D1),
                                            p_he[:, :].rearrange("p (t h d) -> p t h d", h=H1, d=D1),
                                            bc(wts[:, :, H1:NS].unsqueeze(3), [P, QT, H1, D1]), ALU.mult)\
                      .then_inc(val_e_ready, 1)

            def step(b, nxt):
                for k in range(BQ):
                    if nxt:
                        one_hot_T(nxt, k)
                        score(nxt, k)
                    weigh(b, k)
                    if nxt:
                        part(nxt, k)
                if nxt:
                    softmax(nxt)
            b0 = Batch(0, 0)
            for k in range(BQ):
                one_hot_T(b0, k)
                score(b0, k)
                part(b0, k)
            softmax(b0)
            run_batches(dve, step)


def fold(nc, name, w, C, table, first, first_e, first_small, soft):
    with Stage(nc, name) as st:
        n0 = st.sb("n0", [P, TP], I32)
        n0f = st.sb("n0f", [P, TP])
        same = st.sb("same", [P, TP])
        part = st.sb("part", [P, TP + 1])
        W = table.shape[1]
        rows = st.sb("rows", [P, 2, W])
        folded = [st.sb(f"folded{n}", [P, TP]) for n in range(2 if first_e is not None else 1)]
        parts = [first] + ([first_e] if first_e is not None else [])
        SW = 0 if first_small is None else SMW if soft else 1
        small = st.sb("small", [max(SW, 1), TP])
        p_f = [st.ps(f"p_f{n}", [P, 512]) for n in range(2)]
        p_s = st.ps("p_s", [P, 512])
        p_t = [st.ps(f"p_t{n}", [P, 512]) for n in range(2)]
        loaded, chain, ex_ready, expanded, scaled = (st.sem(n) for n in ("loaded", "chain", "ex_ready", "expanded", "scaled"))
        below_ready, summed, turned, rows_ready = (st.sem(n) for n in ("below_ready", "summed", "turned", "rows_ready"))
        stored = [st.sem(f"stored{n}") for n in range(2)]
        if soft:
            run_max, below = st.sb("run_max", [SMW, TP]), st.sb("below", [SMW, TP])
        CH = -(-TP // 512)
        block = st.ctx.enter_context(nc.Block())

        @block.sync
        def _(sp):
            sp.dma_start(n0[:, :], w["n0_p"].to_broadcast([P, TP])).then_inc(loaded, 16)

        @block.vector
        def _(dve):
            link = Chain(dve, chain)
            if soft:
                link(nc.vector.memset(small[:, :], 0.0))
            dve.wait_ge(loaded, 16)
            link(nc.vector.tensor_copy(n0f[:, :], n0[:, :]))
            link(nc.vector.memset(same[:, 0:1], 0.0))
            link(nc.vector.tensor_tensor(same[:, 1:TP], n0f[:, 1:TP], n0f[:, 0:TP - 1], ALU.is_equal))
            if soft:
                m = slice(MR, SMW)
                link(nc.vector.tensor_scalar(part[:, 0:TP], same[:, :], -1.0, BIG, ALU.add, ALU.mult))
                link(nc.vector.memset(part[:, TP:TP + 1], -BIG))
                link(nc.vector.tensor_tensor_scan(run_max[m, :], part[m, 0:TP], first_small[m, :], -BIG, ALU.add, ALU.max))
                link(nc.vector.tensor_tensor_scan(small[m, ::-1], part[m, TP:0:-1], run_max[m, ::-1], -BIG, ALU.add, ALU.max))
                nc.vector.tensor_tensor(below[m, :], first_small[m, :], small[m, :], ALU.subtract).then_inc(below_ready, 1)
                for c in range(CH):
                    e = slice(c * 512, min(TP, (c + 1) * 512))
                    n = e.stop - e.start
                    dve.wait_ge(expanded, c + 1)
                    for i, t in enumerate(parts):
                        link(nc.vector.tensor_tensor(t[:, e], t[:, e], p_f[i][:, 0:n], ALU.mult))
                    link(nc.vector.tensor_tensor(first_small[0:NS, e], first_small[0:NS, e], p_s[0:NS, 0:n], ALU.mult))
                    dve.sem_inc(scaled, 1)
            for i, t in enumerate(parts):
                link(nc.vector.tensor_tensor_scan(folded[i][:, :], same[:, :], t[:, :], 0.0, ALU.mult, ALU.add))
            if SW:
                r = NS if soft else 1
                link(nc.vector.tensor_tensor_scan(small[0:r, :], same[0:r, :], first_small[0:r, :], 0.0, ALU.mult, ALU.add))
            dve.sem_inc(summed, 1)
            for c in range(TC):
                dve.wait_ge(turned, c + 1)
                if c >= 2:
                    dve.wait_ge(stored[c % 2], c // 2 * 16)
                nc.vector.tensor_copy(rows[:, c % 2, :], p_t[c % 2][:, 0:W]).then_inc(rows_ready, 1)

        @block.scalar
        def _(act):
            if soft:
                act.wait_ge(below_ready, 1)
                act.activation(below[MR:SMW, :], below[MR:SMW, :], ACT.Exp).then_inc(ex_ready, 1)

        @block.tensor
        def _(pe):
            if soft:
                pe.wait_ge(ex_ready, 1)
                for c in range(CH):
                    e = slice(c * 512, min(TP, (c + 1) * 512))
                    n = e.stop - e.start
                    if c:
                        pe.wait_ge(scaled, c)
                    for i, lay in enumerate(soft):
                        nc.tensor.matmul(p_f[i][:, 0:n], C["expand"][MR:SMW, lay, :], below[MR:SMW, e], start=True, stop=True)
                    nc.tensor.matmul(p_s[0:NS, 0:n], C["ident"][MR:SMW, MR:SMW], below[MR:SMW, e], start=True, stop=True)\
                      .then_inc(expanded, 1)
            pe.wait_ge(summed, 1)
            for c in range(TC):
                e = slice(c * P, (c + 1) * P)
                if c >= 2:
                    pe.wait_ge(rows_ready, c - 1)
                for i in range(len(parts)):
                    mm = nc.tensor.transpose(p_t[c % 2][:, i * P:(i + 1) * P], folded[i][:, e], C["ident"][:, :])
                if SW:
                    mm = nc.tensor.transpose(p_t[c % 2][:, len(parts) * P:W], small[0:SW, e], C["ident"][0:SW, 0:SW])
                mm.then_inc(turned, 1)

        @block.gpsimd
        def _(pool):
            for c in range(TC):
                pool.wait_ge(rows_ready, c + 1)
                pool.indirect_dma_start(table, bass.IndirectOffsetOnAxis(ap=C["fold_row"][:, c:c + 1], axis=0),
                                        rows[:, c % 2, :], None, bounds_check=NP - 1, oob_is_err=False)\
                    .then_inc(stored[c % 2], 16)
            pool.wait_ge(stored[0], (TC + 1) // 2 * 16)
            pool.wait_ge(stored[1], TC // 2 * 16)


def blocks_of(table, g):
    return table[bass.ds(g * GW, GW), :].rearrange("(b p) c -> p b c", p=P)


def node_stage(nc, kind, w, C, D, hres, cnt, acc, acc_e, small, out):
    soft = kind in ("attn", "gat")
    fold_table = {"first": None, "conv1": D["fold1"], "conv2": D["fold2"], "attn": D["fold3"], "gat": D["fold4"]}[kind]
    FW = fold_table.shape[1] if fold_table is not None else 1
    with Stage(nc, "n_" + kind) as st:
        x = st.sb("x", [P, GB, P])
        fr = st.sb("fr", [P, GB, FW])
        h, sq, h2 = (st.sb(n, [P, GB, P]) for n in ("h", "sq", "h2"))
        totT = st.sb("totT", [P, GW])
        totT_e = st.sb("totT_e", [P, GW])
        mean, rstd, tmp = (st.sb(n, [P, GB * H0]) for n in ("mean", "rstd", "tmp"))
        cT = st.sb("cT", [SMW, GW])
        sb_small = st.sb("sb_small", [P, GB, SMW])
        M, fa, fb, S = (st.sb(n, [P, GB, NS]) for n in ("M", "fa", "fb", "S"))
        made = st.sb("made", [P, GB, 2 * P])
        made_s = st.sb("made_s", [P, GB, 3 * H1])
        p1, p2, p_w = st.ps("p1", [P, 1024]), st.ps("p2", [P, 1024]), st.ps("p_w", [P, 2048])
        p1b = p1[:, 0:GW].rearrange("p (b f) -> p b f", f=P)
        p2b = p2[:, 0:GW].rearrange("p (b f) -> p b f", f=P)
        pwb = p_w[:, 0:GB * 2 * P].rearrange("p (b f) -> p b f", f=2 * P)
        p_ws = p2[:, GW:GW + GB * 3 * H1].rearrange("p (b s) -> p b s", s=3 * H1)
        names = ("loaded", "chain", "copied", "turned1", "tot_ready", "mapped", "pre_act", "acted", "h_ready", "turned2",
                 "hT_ready", "tables_ready", "evacuated", "stored", "below_ready", "ex_ready", "o_ready", "o_turned", "oT_ready")
        (loaded, chain, copied, turned1, tot_ready, mapped, pre_act, acted, h_ready, turned2, hT_ready, tables_ready,
         evacuated, stored, below_ready, ex_ready, o_ready, o_turned, oT_ready) = (st.sem(n) for n in names)
        hT = totT_e if not kind == "gat" else totT
        LOADS = 16 * ((kind in ("first", "attn", "gat")) + (fold_table is not None))
        STORES = 16 * {"first": 2, "conv1": 2, "conv2": 2, "attn": 3, "gat": 1}[kind]
        wide = [P, GB, P]
        lens = {}

        block = st.ctx.enter_context(nc.Block())

        @block.sync
        def _(sp):
            with sp.Fori(0, NGRP) as g:
                sp.wait_ge(evacuated, g + 1)
                settle(sp, st.passed)
                if kind in ("first", "attn", "gat"):
                    sp.dma_start(x[:, :, :], blocks_of(D["base"] if kind == "gat" else w["x"], g)).then_inc(loaded, 16)
                if fold_table is not None:
                    sp.dma_start(fr[:, :, :], blocks_of(fold_table, g)).then_inc(loaded, 16)
                sp.wait_ge(evacuated, g + 2)
                settle(sp, st.passed)
                if kind in ("first", "conv1"):
                    l = 1 if kind == "first" else 2
                    sp.dma_start(blocks_of(D[f"a{l}"], g), made[:, :, 0:P]).then_inc(stored, 16)
                    sp.dma_start(blocks_of(D[f"b{l}"], g), made[:, :, P:2 * P]).then_inc(stored, 16)
                elif kind == "conv2":
                    sp.dma_start(blocks_of(D["q"], g), h[:, :, :]).then_inc(stored, 16)
                    sp.dma_start(blocks_of(D["kv"], g), made[:, :, :]).then_inc(stored, 16)
                elif kind == "attn":
                    sp.dma_start(blocks_of(D["g"], g), made[:, :, 0:P + H1]).then_inc(stored, 16)
                    sp.dma_start(blocks_of(D["base"], g), x[:, :, :]).then_inc(stored, 16)
                    sp.dma_start(blocks_of(D["ed"], g), made_s[:, :, H1:3 * H1]).then_inc(stored, 16)
                else:
                    sp.dma_start(blocks_of(out, g), h[:, :, :]).then_inc(stored, 16)
                sp.wait_ge(stored, (g + 1) * STORES)
                settle(sp, st.passed)

        @block.tensor
        def _(pe):
            ident = C["ident"][:, :]
            with pe.Fori(0, NGRP) as g:
                if kind in ("conv1", "conv2"):
                    pe.wait_ge(loaded, (g + 1) * LOADS)
                    pe.wait_ge(evacuated, g + 1)
                    for b in range(GB):
                        mm = nc.tensor.transpose(p1b[:, b, :], fr[:, b, 0:P], ident)
                    if kind == "conv1":
                        pe.wait_ge(copied, g + 1)
                        settle(pe, st.passed)
                        for b in range(GB):
                            mm = nc.tensor.transpose(p2[:, b:b + 1], cT[0:1, b * P:(b + 1) * P], ident[0:1, 0:1])
                    mm.then_inc(turned1, 1)
                    pe.wait_ge(tot_ready, g + 1)
                    w2 = C["w21" if kind == "conv1" else "w22"]
                    for b in range(GB):
                        mm = nc.tensor.matmul(p1b[:, b, :], totT[:, b * P:(b + 1) * P], w2[:, :], start=True, stop=True)
                    mm.then_inc(mapped, 1)
                if soft:
                    pe.wait_ge(copied, g + 1)
                    pe.wait_ge(evacuated, g + 1)
                    for b in range(GB):
                        e = slice(b * P, (b + 1) * P)
                        nc.tensor.transpose(p1b[:, b, :], totT[:, e], ident)
                        if kind == "gat":
                            nc.tensor.transpose(p2b[:, b, :], totT_e[:, e], ident)
                        mm = nc.tensor.transpose(p_w[:, b * SMW:(b + 1) * SMW], cT[:, e], ident[0:SMW, 0:SMW])
                    mm.then_inc(turned1, 1)
                if kind == "attn":
                    pe.wait_ge(o_ready, g + 1)
                    for b in range(GB):
                        mm = nc.tensor.transpose(p2b[:, b, :], h[:, b, :], ident)
                    mm.then_inc(o_turned, 1)
                    pe.wait_ge(oT_ready, g + 1)
                    for b in range(GB):
                        mm = nc.tensor.matmul(p1b[:, b, :], totT[:, b * P:(b + 1) * P], C["wo"][:, :], start=True, stop=True)
                    mm.then_inc(mapped, 1)
                if kind != "gat":
                    pe.wait_ge(h_ready, g + 1)
                    for b in range(GB):
                        mm = nc.tensor.transpose(p2b[:, b, :], h2[:, b, :], ident)
                    mm.then_inc(turned2, 1)
                    pe.wait_ge(hT_ready, g + 1)
                    rhs = {"first": "wab1", "conv1": "wab2", "conv2": "wkv", "attn": "wsd"}[kind]
                    for b in range(GB):
                        hb = hT[:, b * P:(b + 1) * P]
                        mm = nc.tensor.matmul(pwb[:, b, :], hb, C[rhs][:, :, :].rearrange("p a f -> p (a f)"), start=True, stop=True)
                        if kind == "conv2":
                            mm = nc.tensor.matmul(p1b[:, b, :], hb, C["wq"][:, :], start=True, stop=True)
                        if kind == "attn":
                            mm = nc.tensor.matmul(p_ws[:, b, :], hb, C["wsa"][:, :], start=True, stop=True)
                    mm.then_inc(tables_ready, 1)

        @block.scalar
        def _(act):
            with act.Fori(0, NGRP) as g:
                nodes = bass.ds(g * GW, GW)
                if kind == "conv1":
                    act.wait_ge(evacuated, g + 1)
                    act.copy(cT[0:1, :], small[:, nodes]).then_inc(copied, 1)
                if soft:
                    act.wait_ge(evacuated, g + 1)
                    act.copy(totT[:, :], acc[:, nodes])
                    if kind == "gat":
                        act.copy(totT_e[:, :], acc_e[:, nodes])
                    act.copy(cT[:, :], small[:, nodes]).then_inc(copied, 1)
                    act.wait_ge(below_ready, g + 1)
                    act.activation(fa[:, :, :], fa[:, :, :], ACT.Exp)
                    act.activation(fb[:, :, :], fb[:, :, :], ACT.Exp).then_inc(ex_ready, 1)
                if kind in ("conv1", "conv2"):
                    act.wait_ge(pre_act, g + 1)
                    act.activation(h[:, :, :], h[:, :, :], ACT.Silu).then_inc(acted, 1)
                if kind == "conv2":
                    act.wait_ge(acted, g + 1)

        def vector_pass(dve, g, link):
            nodes, blks = bass.ds(g * GW, GW), bass.ds(g * GB, GB)
            hb = hres[:, blks, :]
            if LOADS:
                dve.wait_ge(loaded, (g + 1) * LOADS)
            if kind == "first":
                link(nc.vector.tensor_copy(h[:, :, :], x[:, :, :]))
                group_norm(nc, link, h, sq, mean, rstd, tmp, None, None, P)
                link(nc.vector.tensor_scalar(h2[:, :, :], h[:, :, :], 0.0, None, ALU.max))
                settle(dve, st.passed)
                link(nc.vector.tensor_copy(hb, h2[:, :, :]))
            if kind in ("conv1", "conv2"):
                l = 1 if kind == "conv1" else 2
                dve.wait_ge(turned1, g + 1)
                cg = cnt[:, :, blks]
                if kind == "conv1":
                    link(nc.vector.tensor_tensor(tmp[:, 0:GB], p2[:, 0:GB], fr[:, :, P:P + 1].rearrange("p b o -> p (b o)"), ALU.add))
                    link(nc.vector.tensor_scalar(mean[:, 0:GB], tmp[:, 0:GB], 1.0, None, ALU.max))
                    link(nc.vector.reciprocal(rstd[:, 0:GB], mean[:, 0:GB]))
                    settle(dve, st.passed)
                    link(nc.vector.tensor_copy(cg[:, 0, :], rstd[:, 0:GB]))
                    link(nc.vector.tensor_scalar(cg[:, 1, :], tmp[:, 0:GB], 1.0, None, ALU.min))
                link(nc.vector.tensor_tensor(totT[:, :], acc[:, nodes], p1[:, 0:GW], ALU.add))
                dve.sem_inc(tot_ready, 1)
                dve.wait_ge(mapped, g + 1)
                link(nc.vector.tensor_tensor(h[:, :, :], p1b, bc(cg[:, 0, :].unsqueeze(2), wide), ALU.mult))
                link(nc.vector.tensor_tensor(sq[:, :, :], bc(row(C, f"c{l}_b2").unsqueeze(1), wide),
                                             bc(cg[:, 1, :].unsqueeze(2), wide), ALU.mult))
                link(nc.vector.tensor_tensor(h[:, :, :], h[:, :, :], sq[:, :, :], ALU.add))
                group_norm(nc, link, h, sq, mean, rstd, tmp, row(C, f"n{l}_g"), row(C, f"n{l}_b"), D0)
                dve.sem_inc(pre_act, 1)
                dve.wait_ge(acted, g + 1)
                if kind == "conv1":
                    link(nc.vector.tensor_tensor(h2[:, :, :], h[:, :, :], bc(C["te"][:, :].unsqueeze(1), wide), ALU.add))
                else:
                    link(nc.vector.tensor_tensor(h2[:, :, :], h[:, :, :], hb, ALU.add))
                    settle(dve, st.passed)
                    link(nc.vector.tensor_copy(hb, h2[:, :, :]))
            if soft:
                dve.wait_ge(turned1, g + 1)
                link(nc.vector.tensor_copy(sb_small[:, :, :], p_w[:, 0:GB * SMW].rearrange("p (b s) -> p b s", s=SMW)))
                F = FW - SMW
                sa, ma = sb_small[:, :, 0:NS], sb_small[:, :, MR:SMW]
                sf, mf = fr[:, :, F:F + NS], fr[:, :, F + MR:FW]
                for s_, m_, f_ in ((sa, ma, fa), (sf, mf, fb)):
                    link(nc.vector.tensor_scalar(f_[:, :, :], s_, 0.0, -BIG, ALU.is_le, ALU.mult))
                    link(nc.vector.tensor_tensor(f_[:, :, :], f_[:, :, :], m_, ALU.add))
                link(nc.vector.tensor_tensor(M[:, :, :], fa[:, :, :], fb[:, :, :], ALU.max))
                link(nc.vector.tensor_tensor(fa[:, :, :], fa[:, :, :], M[:, :, :], ALU.subtract))
                link(nc.vector.tensor_tensor(fb[:, :, :], fb[:, :, :], M[:, :, :], ALU.subtract))
                dve.sem_inc(below_ready, 1)
                dve.wait_ge(ex_ready, g + 1)
                link(nc.vector.tensor_tensor(S[:, :, :], sa, fa[:, :, :], ALU.mult))
                link(nc.vector.tensor_tensor(M[:, :, :], sf, fb[:, :, :], ALU.mult))
                link(nc.vector.tensor_tensor(S[:, :, :], S[:, :, :], M[:, :, :], ALU.add))
                link(nc.vector.tensor_scalar(S[:, :, :], S[:, :, :], 1e-6, None, ALU.max))
                link(nc.vector.reciprocal(M[:, :, :], S[:, :, :]))
                link(nc.vector.tensor_tensor(fa[:, :, :], fa[:, :, :], M[:, :, :], ALU.mult))
                link(nc.vector.tensor_tensor(fb[:, :, :], fb[:, :, :], M[:, :, :], ALU.mult))

                def weighed(dst, psum, rows_, s0, heads, width):
                    hw = [P, GB, heads, width]
                    for d, v, f_ in ((dst, psum, fa), (sq, rows_, fb)):
                        link(nc.vector.tensor_tensor(d[:, :, :].rearrange("p b (h d) -> p b h d", d=width),
                                                     v.rearrange("p b (h d) -> p b h d", d=width),
                                                     bc(f_[:, :, s0:s0 + heads].unsqueeze(3), hw), ALU.mult))
                    link(nc.vector.tensor_tensor(dst[:, :, :], dst[:, :, :], sq[:, :, :], ALU.add))
            if kind == "attn":
                weighed(h, p1b, fr[:, :, 0:P], 0, H0, D0)
                dve.sem_inc(o_ready, 1)
                dve.wait_ge(o_turned, g + 1)
                link(nc.vector.tensor_copy(totT[:, :], p2[:, 0:GW]))
                dve.sem_inc(oT_ready, 1)
                dve.wait_ge(mapped, g + 1)
                link(nc.vector.tensor_tensor(h[:, :, :], p1b, bc(row(C, "ob").unsqueeze(1), wide), ALU.add))
                group_norm(nc, link, h, sq, mean, rstd, tmp, row(C, "an_g"), row(C, "an_b"), D0)
                link(nc.vector.tensor_tensor(h[:, :, :], h[:, :, :], hb, ALU.add))
                link(nc.vector.tensor_tensor(x[:, :, :], x[:, :, :], h[:, :, :], ALU.add))
                link(nc.vector.tensor_copy(h[:, :, :], x[:, :, :]))
                group_norm(nc, link, h, sq, mean, rstd, tmp, None, None, P)
                link(nc.vector.tensor_scalar(h2[:, :, :], h[:, :, :], 0.0, None, ALU.max))
            if kind == "gat":
                weighed(h, p1b, fr[:, :, 0:P], 0, H1, D1)
                link(nc.vector.tensor_tensor(h[:, :, :], h[:, :, :], x[:, :, :], ALU.add))
                weighed(h2, p2b, fr[:, :, P:2 * P], H1, H1, D1)
                link(nc.vector.tensor_tensor(h[:, :, :], h[:, :, :], h2[:, :, :], ALU.add))
            else:
                dve.sem_inc(h_ready, 1)
                dve.wait_ge(turned2, g + 1)
                link(nc.vector.tensor_copy(hT[:, :], p2[:, 0:GW]))
                dve.sem_inc(hT_ready, 1)
                dve.wait_ge(tables_ready, g + 1)
                if kind in ("first", "conv1"):
                    link(nc.vector.tensor_copy(made[:, :, :], pwb))
                if kind == "conv2":
                    link(nc.vector.tensor_tensor(h[:, :, :], p1b, bc(row(C, "qb").unsqueeze(1), wide), ALU.add))
                    link(nc.vector.tensor_scalar(h[:, :, :], h[:, :, :], D0 ** -0.5, None, ALU.mult))
                    link(nc.vector.tensor_tensor(made[:, :, 0:P], pwb[:, :, 0:P], bc(row(C, "kb").unsqueeze(1), wide), ALU.add))
                    link(nc.vector.tensor_tensor(made[:, :, P:2 * P], pwb[:, :, P:2 * P], bc(row(C, "vb").unsqueeze(1), wide), ALU.add))
                if kind == "attn":
                    link(nc.vector.tensor_copy(made_s[:, :, :], p_ws))
                    link(nc.vector.tensor_copy(made[:, :, 0:P], pwb[:, :, 0:P]))
                    link(nc.vector.tensor_copy(made[:, :, P:P + H1], made_s[:, :, 0:H1]))
                    link(nc.vector.tensor_tensor(x[:, :, :], x[:, :, :], pwb[:, :, P:2 * P], ALU.add))
            dve.sem_inc(evacuated, 1)
            if STORES:
                dve.wait_ge(stored, (g + 1) * STORES)

        @block.vector
        def _(dve):
            dve.sem_inc(evacuated, 1)
            LINKS = {"first": 23, "conv1": 32, "conv2": 31, "attn": 67, "gat": 23}[kind]
            with dve.Fori(0, NGRP) as g:
                link = Chain(dve, chain, g * LINKS)
                vector_pass(dve, g, link)
                assert link.n == LINKS, (kind, link.n)


def build(nc, w, out):
    with ExitStack() as ctx:
        def sb(name, shape, dt=F32):
            return ctx.enter_context(nc.sbuf_tensor(name, shape, dt))

        def dram(name, shape, dt=F32):
            return nc.dram_tensor(name, shape, dt, kind="Internal").ap()

        D = {"cols": dram("cols", (NB, P, 2 * BT)), "places": dram("places", (NB, BE), BF16),
             "mask": dram("mask", (T * NS, P + 1)),
             "a1": dram("a1", (NW, P)), "b1": dram("b1", (NP, P)), "a2": dram("a2", (NW, P)), "b2": dram("b2", (NP, P)),
             "base": dram("base", (NP, P)), "q": dram("q", (NW, P)), "kv": dram("kv", (NP, 2 * P)), "g": dram("g", (NP, P + H1)), "ed": dram("ed", (NW, NS))}
        for name, width in FOLDED.items():
            D[name] = dram(name, (NP, width))
        C = {"ident": sb("ident", [P, P]), "ones": sb("ones", [P, P]), "iota_row": sb("iota_row", [P, P], BF16),
             "iota_col": sb("iota_col", [P, 1]), "fold_row": sb("fold_row", [P, TC], I32),
             "expand": sb("expand", [P, 3, P]), "te": sb("te", [P, P]), "rows": sb("rows", [P, len(ROWS), P]),
             "wq": sb("wq", [P, P]), "wkv": sb("wkv", [P, 2, P]), "wo": sb("wo", [P, P]), "we": sb("we", [ED + 1, H0]),
             "wsd": sb("wsd", [P, 2, P]), "wet": sb("wet", [P, P]), "wsa": sb("wsa", [P, 3 * H1]), "wea": sb("wea", [P, H1])}
        for l in (1, 2):
            C[f"wab{l}"], C[f"wc{l}"], C[f"w2{l}"] = sb(f"wab{l}", [P, 2, P]), sb(f"wc{l}", [ED + 1, P]), sb(f"w2{l}", [P, P])
        res = sb("res", [P, NW])
        hres = res[:, 0:NP].rearrange("p (b f) -> p b f", f=P)
        cnt = sb("cnt", [P, 2, NBLK])

        prepare(nc, w, C, D)
        node_stage(nc, "first", w, C, D, hres, cnt, None, None, None, out)
        with nc.sbuf_tensor("acc1", [P, NW], F32) as acc, nc.sbuf_tensor("first1", [P, TP], F32) as first:
            with nc.sbuf_tensor("count", [1, NW], F32) as count, nc.sbuf_tensor("first_count", [1, TP], F32) as first_count:
                conv_edges(nc, 1, w, C, D, acc, first, count, first_count)
                fold(nc, "fold1", w, C, D["fold1"], first, None, first_count, None)
                node_stage(nc, "conv1", w, C, D, hres, cnt, acc, None, count, out)
            conv_edges(nc, 2, w, C, D, acc, first, None, None)
            fold(nc, "fold2", w, C, D["fold2"], first, None, None, None)
            node_stage(nc, "conv2", w, C, D, hres, cnt, acc, None, None, out)
        with nc.sbuf_tensor("acc2", [P, NW], F32) as acc, nc.sbuf_tensor("first2", [P, TP], F32) as first, \
                nc.sbuf_tensor("small", [SMW, NW], F32) as small, nc.sbuf_tensor("first_small", [SMW, TP], F32) as first_small:
            attention_edges(nc, False, w, C, D, acc, first, None, None, small, first_small)
            fold(nc, "fold3", w, C, D["fold3"], first, None, first_small, [0])
            node_stage(nc, "attn", w, C, D, hres, cnt, acc, None, small, out)
            acc_e = res
            with nc.sbuf_tensor("first_e", [P, TP], F32) as first_e:
                attention_edges(nc, True, w, C, D, acc, first, acc_e, first_e, small, first_small)
                fold(nc, "fold4", w, C, D["fold4"], first, first_e, first_small, [1, 2])
                node_stage(nc, "gat", w, C, D, hres, cnt, acc, acc_e, small, out)


def kernel(**inputs):
    import concourse.bacc as bacc
    from concourse.bass_utils import run_bass_kernel_spmd

    src, dst = np.asarray(inputs["src"]), np.asarray(inputs["dst"])
    pad = EP - E
    src = np.concatenate([src, np.zeros(pad, np.int32)])
    dst = np.concatenate([dst, np.full(pad, N, np.int32)])
    n0 = np.concatenate([dst[::P], np.full(TP - T + 1, N, np.int32)])
    arrays = {
        "x": np.concatenate([np.asarray(inputs["x"]), np.zeros((NP - N, P), np.float32)]),
        "src_b": src.reshape(NB, BT, P).transpose(0, 2, 1),
        "dst_b": dst.reshape(NB, BT, P).transpose(0, 2, 1).reshape(NB, BE),
        "dst_r": dst.reshape(NB, BE),
        "n0_b": n0[:T].reshape(NB, BT),
        "n0_p": n0[:TP].reshape(1, TP),
        "n0_c": n0[:TP].reshape(TC, P).T,
        "n0_next": n0[1:].reshape(TC, P).T,
        "ea": np.concatenate([np.concatenate([np.asarray(inputs["edge_attr_4"]), np.zeros((pad, ED), np.float32)]).T,
                              np.ones((1, EP), np.float32)]),
        "xe": np.concatenate([np.asarray(inputs["edge_attr_128"]), np.zeros((pad, P), np.float32)]),
    }
    for name, a in inputs.items():
        if name.startswith(("L0_gnn_", "L1_gnn_")):
            arrays[name[7:]] = np.asarray(a)
    nc = bacc.Bacc("TRN2", target_bir_lowering=False, num_devices=1)
    feeds, w = {}, {}
    for name, a in arrays.items():
        a = np.ascontiguousarray(a)
        feeds["in_" + name] = a
        w[name] = nc.dram_tensor("in_" + name, a.shape, mybir.dt.from_np(a.dtype), kind="ExternalInput").ap()
    out = nc.dram_tensor("out", (NP, P), F32, kind="ExternalOutput").ap()
    build(nc, w, out)
    result = run_bass_kernel_spmd(nc, [feeds], core_ids=[0])
    return result.results[0]["out"][:N]
```

```python
import numpy as np
from contextlib import ExitStack

import concourse.bass as bass
from concourse import mybir

F32, BF16, I32 = mybir.dt.float32, mybir.dt.bfloat16, mybir.dt.int32
ALU, ACT, AX = mybir.AluOpType, mybir.ActivationFunctionType, mybir.AxisListType
ACT_ENGINE, SP_ENGINE = mybir.EngineType.Activation, mybir.EngineType.SP

P = 128
N = 6250
E = 206250
NBLK = -(-N // P)
NP = NBLK * P
NW = NP + P
GB = 7
NGRP = NBLK // GB
GW = GB * P
QT = 4
BT = 16
BQ = BT // QT
QE, BE = QT * P, BT * P
NB = -(-E // BE)
T = NB * BT
EP = T * P
RB = 3
BODY = (NB - 2) // RB
assert NBLK % GB == 0 and BODY * RB + 2 == NB
TC = -(-T // P)
TP = TC * P
ED = 4
H0, D0 = 8, 16
H1, D1 = 4, 32
NS = 8
MR = 32
SMW = MR + NS
EPS = 1e-5
BIG = 1e30
SKIP = 1e6
MAGIC = float(0x5F3759DF)
HEAD = 64


class Batch:

    def __init__(self, q, c):
        self.q, self.c = q, c
        self.i = q * RB + c

    def next(self):
        return Batch(self.q, self.c + 1) if self.c + 1 < RB else Batch(self.q + 1, 0)

    def quad(self, k):
        return self.i * BQ + k


def done(eng, sem, n):
    if not isinstance(n, int) or n > 0:
        eng.wait_ge(sem, n + HEAD)


def settle(eng, passed):
    eng.sem_inc(passed, 1)


def run_batches(eng, step):
    with eng.Fori(0, BODY) as j:
        for c in range(RB):
            b = Batch(j, c)
            step(b, b.next(), b.next().next())
    step(Batch(BODY, 0), Batch(BODY, 1), None)
    step(Batch(BODY, 1), None, None)


class Chain:

    def __init__(self, eng, sem, base=0):
        self.eng, self.sem, self.base, self.n = eng, sem, base, 0

    def __call__(self, ins):
        self.n += 1
        ins.then_inc(self.sem, 1)
        self.eng.wait_ge(self.sem, self.base + self.n)


def bc(ap, shape):
    return ap.to_broadcast(shape)


def rsqrt(nc, link, x, y, a):
    yi, xi = y.bitcast(I32), x.bitcast(I32)
    link(nc.vector.tensor_scalar(yi, xi, 1, None, ALU.logical_shift_right))
    link(nc.vector.tensor_scalar(yi, yi, -1.0, MAGIC, ALU.mult, ALU.add))
    for _ in range(3):
        link(nc.vector.tensor_tensor(a, y, y, ALU.mult))
        link(nc.vector.scalar_tensor_tensor(a, a, -0.5, x, ALU.mult, ALU.mult))
        link(nc.vector.scalar_tensor_tensor(y, a, 1.5, y, ALU.add, ALU.mult))


def group_norm(nc, link, h, sq, mean, rstd, tmp, gamma, beta, width):
    G = GW // width
    h, sq = h[:, :, :], sq[:, :, :]
    mean, rstd, tmp = mean[:, 0:G], rstd[:, 0:G], tmp[:, 0:G]
    hg, sg = (v.rearrange("p b (g w) -> p (b g) w", w=width) for v in (h, sq))
    wide = [P, G, width]
    link(nc.vector.tensor_reduce(mean, hg, AX.X, ALU.add))
    link(nc.vector.tensor_scalar(mean, mean, 1.0 / width, None, ALU.mult))
    link(nc.vector.tensor_tensor(hg, hg, bc(mean.unsqueeze(2), wide), ALU.subtract))
    link(nc.vector.tensor_tensor(sq, h, h, ALU.mult))
    link(nc.vector.tensor_reduce(mean, sg, AX.X, ALU.add))
    link(nc.vector.tensor_scalar(mean, mean, 1.0 / width, EPS, ALU.mult, ALU.add))
    rsqrt(nc, link, mean, rstd, tmp)
    link(nc.vector.tensor_tensor(hg, hg, bc(rstd.unsqueeze(2), wide), ALU.mult))
    if gamma is not None:
        link(nc.vector.tensor_tensor(h, h, bc(gamma.unsqueeze(1), [P, GB, P]), ALU.mult))
        link(nc.vector.tensor_tensor(h, h, bc(beta.unsqueeze(1), [P, GB, P]), ALU.add))


class Stage:

    def __init__(self, nc, name):
        self.nc, self.name, self.ctx, self.sems = nc, name, ExitStack(), []
        self.passed = self.sem("passed")

    def __enter__(self):
        return self

    def __exit__(self, *exc):
        self.ctx.close()
        if exc[0] is None:
            self.nc.clear_and_free_semaphores(self.sems)
            self.nc.all_engine_barrier()

    def sb(self, name, shape, dt=F32):
        return self.ctx.enter_context(self.nc.sbuf_tensor(f"{self.name}_{name}", shape, dt))

    def ps(self, name, shape):
        return self.ctx.enter_context(self.nc.psum_tensor(f"{self.name}_{name}", shape, F32))

    def sem(self, name):
        s = self.nc.alloc_semaphore(f"{self.name}_{name}")
        self.sems.append(s)
        return s


def prepare(nc, w, C, D):
    with Stage(nc, "prep") as st:
        dst_b = st.sb("dst_b", [NB, P * BT], I32)
        dst_r = st.sb("dst_r", [NB, BE], I32)
        n0_b = st.sb("n0_b", [NB, BT], I32)
        rel_c = st.sb("rel_c", [NB, 2, P * BT])
        rel_f = st.sb("rel_f", [NB, BE])
        rel_h = st.sb("rel_h", [NB, BE], BF16)
        mask = st.sb("mask", [NB, BT, P + 1])
        iota_i = st.sb("iota_i", [P, P], I32)
        iota_pi = st.sb("iota_pi", [P, 1], I32)
        sc_i = st.sb("sc_i", [P, 2, TC], I32)
        sc_f = st.sb("sc_f", [P, 2, TC])
        zero = st.sb("zero", [P, 2 * P + SMW])
        temb = st.sb("temb", [P, 4])
        tmw = st.sb("tmw", [P, 4, P])
        tmb = st.sb("tmb", [1, P])
        te_row = st.sb("te_row", [1, P])
        mean = st.sb("mean", [P, 16])
        wg = st.sb("wg", [P, 3, P])
        attn = st.sb("attn", [P, 3])
        head = st.sb("head", [P, H1])
        abd = st.sb("abd", [P, 3, H1])
        p_te, p_teb = st.ps("p_te", [P, 512]), st.ps("p_teb", [P, 512])
        p_w = st.ps("p_w", [P, 512])
        p_a = st.ps("p_a", [P, 512])
        loaded, cols_stored, stored = st.sem("loaded"), st.sem("cols_stored"), st.sem("stored")
        pool_made, dve_made, chain = st.sem("pool_made"), st.sem("dve_made"), st.sem("chain")
        temb_ready, te_ready, teb_ready = st.sem("temb_ready"), st.sem("te_ready"), st.sem("teb_ready")
        te_copied, wt_ready, heads_ready = st.sem("te_copied"), st.sem("wt_ready"), st.sem("heads_ready")

        loads = [(dst_b[:, :], w["dst_b"]), (dst_r[:, :], w["dst_r"]), (n0_b[:, :], w["n0_b"]),
                 (sc_i[:, 0, :], w["n0_c"]), (sc_i[:, 1, :], w["n0_next"]),
                 (temb[:, :], w["t_emb"].rearrange("(p c) -> p c", p=P)),
                 (tmw[:, :, :], w["tm_w"].rearrange("(p c) f -> p c f", p=P)),
                 (tmb[:, :], w["tm_b"].unsqueeze(0))]
        for l in (1, 2):
            loads += [(C[f"wab{l}"][:, 0, :], w[f"c{l}_w1"][0:P, :]), (C[f"wab{l}"][:, 1, :], w[f"c{l}_w1"][P:2 * P, :]),
                      (C[f"wc{l}"][0:ED, :], w[f"c{l}_w1"][2 * P:2 * P + ED, :]),
                      (C[f"wc{l}"][ED:ED + 1, :], w[f"c{l}_b1"].unsqueeze(0)), (C[f"w2{l}"][:, :], w[f"c{l}_w2"])]
        loads += [(C["wq"][:, :], w["qw"]), (C["wkv"][:, 0, :], w["kw"]), (C["wkv"][:, 1, :], w["vw"]),
                  (C["wo"][:, :], w["ow"]), (C["we"][0:ED, :], w["ew"]), (C["we"][ED:ED + 1, :], w["eb"].unsqueeze(0))]
        for n in ROWS:
            loads.append((C["rows"][:, ROWS.index(n), :], w[n].unsqueeze(0).to_broadcast([P, P])))
        for n, s in enumerate(("src", "dst", "edge")):
            loads += [(wg[:, n, :], w["W_" + s]),
                      (attn[:, n:n + 1], w["attn_" + s].rearrange("h d -> (h d)").unsqueeze(1))]

        block = st.ctx.enter_context(nc.Block())

        @block.sync
        def _(sp):
            for dst, src in loads:
                sp.dma_start(dst, src).then_inc(loaded, 16)
            sp.wait_ge(pool_made, 3)
            for name, width in FOLDED.items():
                sp.dma_start(D[name].rearrange("(b p) c -> p b c", p=P),
                             bc(zero[:, 0:width].unsqueeze(1), [P, NBLK, width])).then_inc(stored, 16)
            for name in ("a1", "a2", "q"):
                sp.dma_start(D[name][NP:NW, :], zero[:, 0:P]).then_inc(stored, 16)
            sp.dma_start(D["ed"][NP:NW, :], zero[:, 0:NS]).then_inc(stored, 16)
            sp.wait_ge(dve_made, 1)
            sp.dma_start(D["cols"].rearrange("b p (a t) -> b a p t", a=2)[:, 0, :, :],
                         rel_c[:, 0, :].rearrange("b (p t) -> b p t", t=BT)).then_inc(stored, 16)
            sp.dma_start(D["cols"].rearrange("b p (a t) -> b a p t", a=2)[:, 1, :, :],
                         rel_c[:, 1, :].rearrange("b (p t) -> b p t", t=BT)).then_inc(stored, 16)
            sp.dma_start(D["places"], rel_h[:, :]).then_inc(stored, 16)
            m = D["mask"].rearrange("(b t h) e -> b t h e", t=BT, h=NS)
            for h in range(NS):
                sp.dma_start(m[:, :, h, :], mask[:, :, :]).then_inc(stored, 16)
            sp.wait_ge(stored, 16 * (len(FOLDED) + 4 + 3 + NS))

        @block.gpsimd
        def _(pool):
            pool.memset(C["ident"][:, :], 0.0).then_inc(pool_made, 1)
            pool.memset(head[:, :], 1.0).then_inc(pool_made, 1)
            pool.memset(zero[:, :], 0.0).then_inc(pool_made, 1)
            pool.memset(C["expand"][:, :, :], 1.0).then_inc(pool_made, 1)
            pool.iota(iota_i[:, :], pattern=[[1, P]], base=0, channel_multiplier=0).then_inc(pool_made, 1)
            pool.iota(iota_pi[:, :], pattern=[[1, 1]], base=0, channel_multiplier=1).then_inc(pool_made, 1)
            pool.wait_ge(pool_made, 6)
            pool.affine_select(out=C["ident"][:, :], in_=C["ident"][:, :], compare_op=ALU.not_equal, fill=1.0,
                               base=0, pattern=[[-1, P]], channel_multiplier=1).then_inc(pool_made, 1)
            pool.affine_select(out=head[:, :], in_=head[:, :], compare_op=ALU.is_ge, fill=0.0,
                               base=0, pattern=[[-D1, H1]], channel_multiplier=1).then_inc(pool_made, 1)
            for n, (first, width) in enumerate(((0, D0), (0, D1), (H1, D1))):
                e = C["expand"][:, n, :]
                pool.affine_select(out=e, in_=e, compare_op=ALU.is_ge, fill=0.0, base=width * (MR + first),
                                   pattern=[[1, P]], channel_multiplier=-width).then_inc(pool_made, 1)
            pool.wait_ge(pool_made, 11)
            pool.affine_select(out=head[:, :], in_=head[:, :], compare_op=ALU.is_ge, fill=0.0,
                               base=D1 - 1, pattern=[[D1, H1]], channel_multiplier=-1).then_inc(pool_made, 1)
            for n, (first, width) in enumerate(((0, D0), (0, D1), (H1, D1))):
                e = C["expand"][:, n, :]
                pool.affine_select(out=e, in_=e, compare_op=ALU.is_ge, fill=0.0, base=width - 1 - width * (MR + first),
                                   pattern=[[-1, P]], channel_multiplier=width).then_inc(pool_made, 1)

        @block.scalar
        def _(act):
            act.wait_ge(loaded, 16 * len(loads))
            act.activation(temb[:, :], temb[:, :], ACT.Silu).then_inc(temb_ready, 1)

        @block.tensor
        def _(pe):
            pe.wait_ge(loaded, 16 * len(loads))
            pe.wait_ge(temb_ready, 1)
            for c in range(4):
                mm = nc.tensor.matmul(p_te[0:1, 0:P], temb[:, c:c + 1], tmw[:, c, :], start=c == 0, stop=c == 3)
            mm.then_inc(te_ready, 1)
            pe.wait_ge(dve_made, 2)
            pe.wait_ge(pool_made, 15)
            nc.tensor.matmul(p_teb[:, 0:P], C["ones"][0:1, :], te_row[:, :], start=True, stop=True).then_inc(teb_ready, 1)
            for n in range(3):
                nc.tensor.transpose(p_w[:, n * P:(n + 1) * P], wg[:, n, :], C["ident"][:, :])
                mm = nc.tensor.matmul(p_a[:, n * H1:(n + 1) * H1], wg[:, n, :], abd[:, n, :], start=True, stop=True)
            mm.then_inc(wt_ready, 1)

        @block.vector
        def _(dve):
            link = Chain(dve, chain)
            dve.wait_ge(pool_made, 6)
            dve.wait_ge(loaded, 16 * len(loads))
            link(nc.vector.tensor_copy(C["iota_row"][:, :], iota_i[:, :]))
            link(nc.vector.tensor_copy(C["iota_col"][:, :], iota_pi[:, :]))
            link(nc.vector.memset(C["ones"][:, :], 1.0))
            n0_e = n0_b[:, :].unsqueeze(1)
            link(nc.vector.tensor_tensor(rel_c[:, 0, :].rearrange("b (p t) -> b p t", t=BT),
                                         dst_b[:, :].rearrange("b (p t) -> b p t", t=BT),
                                         bc(n0_e, [NB, P, BT]), ALU.subtract))
            rel_t = rel_f[:, :].rearrange("b (t e) -> b t e", e=P)
            link(nc.vector.tensor_tensor(rel_t, dst_r[:, :].rearrange("b (t e) -> b t e", e=P),
                                         bc(n0_b[:, :].unsqueeze(2), [NB, BT, P]), ALU.subtract))
            link(nc.vector.tensor_copy(rel_h[:, :], rel_f[:, :]))
            link(nc.vector.memset(rel_c[:, 1, 0:BT], 1.0))
            link(nc.vector.tensor_tensor(rel_c[:, 1, BT:], rel_c[:, 0, BT:], rel_c[:, 0, 0:BE - BT], ALU.not_equal))
            link(nc.vector.memset(mask[:, :, :], -BIG))
            link(nc.vector.tensor_tensor(mask[:, :, 1:P], rel_t[:, :, 1:P], rel_t[:, :, 0:P - 1], ALU.not_equal))
            link(nc.vector.tensor_scalar(mask[:, :, 1:P], mask[:, :, 1:P], -BIG, None, ALU.mult))
            nc.vector.engine_nop().then_inc(dve_made, 1) if False else dve.sem_inc(dve_made, 1)
            link(nc.vector.tensor_copy(sc_f[:, :, :], sc_i[:, :, :]))
            link(nc.vector.tensor_tensor(sc_f[:, 1, :], sc_f[:, 0, :], sc_f[:, 1, :], ALU.is_equal))
            link(nc.vector.scalar_tensor_tensor(C["fold_row"][:, :], sc_f[:, 1, :], SKIP, sc_f[:, 0, :], ALU.mult, ALU.add))
            for l in (1, 2):
                for t, rows, n in ((C[f"wab{l}"], P, 2), (C[f"wc{l}"], ED + 1, 1)):
                    v = t[0:rows].rearrange("p a (g w) -> p (a g) w", w=D0) if n == 2 else \
                        t[0:rows].rearrange("p (g w) -> p g w", w=D0)
                    link(nc.vector.tensor_reduce(mean[0:rows, 0:n * H0], v, AX.X, ALU.add))
                    link(nc.vector.tensor_scalar(mean[0:rows, 0:n * H0], mean[0:rows, 0:n * H0], 1.0 / D0, None, ALU.mult))
                    link(nc.vector.tensor_tensor(v, v, bc(mean[0:rows, 0:n * H0].unsqueeze(2), [rows, n * H0, D0]), ALU.subtract))
            dve.wait_ge(te_ready, 1)
            link(nc.vector.tensor_tensor(te_row[:, :], p_te[0:1, 0:P], tmb[:, :], ALU.add))
            dve.wait_ge(pool_made, 15)
            for n in range(3):
                link(nc.vector.tensor_scalar(abd[:, n, :], head[:, :], attn[:, n:n + 1], None, ALU.mult))
            dve.sem_inc(dve_made, 1)
            dve.wait_ge(teb_ready, 1)
            link(nc.vector.tensor_copy(C["te"][:, :], p_teb[:, 0:P]))
            dve.wait_ge(wt_ready, 1)
            link(nc.vector.tensor_copy(C["wsd"][:, :, :], p_w[:, 0:2 * P].rearrange("p (a f) -> p a f", a=2)))
            link(nc.vector.tensor_copy(C["wet"][:, :], p_w[:, 2 * P:3 * P]))
            link(nc.vector.tensor_copy(C["wsa"][:, 0:2 * H1], p_a[:, 0:2 * H1]))
            link(nc.vector.tensor_copy(C["wsa"][:, 2 * H1:3 * H1], p_a[:, H1:2 * H1]))
            link(nc.vector.tensor_copy(C["wea"][:, :], p_a[:, 2 * H1:3 * H1]))


ROWS = ["c1_g", "c1_bt", "c1_b2", "n1_g", "n1_b", "c2_g", "c2_bt", "c2_b2", "n2_g", "n2_b", "qb", "kb", "vb",
        "ob", "an_g", "an_b"]
FOLDED = {"fold1": P + 1, "fold2": P, "fold3": P + SMW, "fold4": 2 * P + SMW}


def row(C, name):
    return C["rows"][:, ROWS.index(name), :]


def conv_edges(nc, l, w, C, D, acc, first, count, first_count):
    a_table, b_table = D[f"a{l}"], D[f"b{l}"]
    gamma, beta, wc = row(C, f"c{l}_g"), row(C, f"c{l}_bt"), C[f"wc{l}"]
    GQ, WQ, PQ = RB * BQ, 4, 6
    ZQ, SQ = 6, 1 if l == 1 else 2
    with Stage(nc, f"conv{l}") as st:
        idx = st.sb("idx", [P, RB, BT], I32)
        cols = st.sb("cols", [P, RB, 2 * BT])
        n0 = st.sb("n0", [1, RB, BT], I32)
        gath = st.sb("gath", [P, GQ, QT, P])
        win = st.sb("win", [P, WQ, QT, P])
        ea = st.sb("ea", [ED + 1, WQ, QE])
        places = st.sb("places", [P, PQ, QE], BF16)
        hotT = st.sb("hotT", [P, PQ, QE])
        hot = st.sb("hot", [P, 2, QT, P])
        sq = st.sb("sq", [P, 2, QE])
        var, rstd, tmp = st.sb("var", [P, BT * H0]), st.sb("rstd", [P, BT * H0]), st.sb("tmp", [P, BT * H0])
        u = st.sb("u", [P, 2, QE])
        m = st.sb("m", [P, 2, QE])
        z = [st.ps(f"z{n}", [P, QE]) for n in range(ZQ)]
        sums = [st.ps(f"sums{n}", [P, QE]) for n in range(SQ)]
        counts = st.ps("counts", [P, QE]) if l == 1 else None

        meta_landed = [st.sem(f"meta_landed{c}") for c in range(RB)]
        gath_landed = [st.sem(f"gath_landed{n}") for n in range(GQ)]
        win_landed = [st.sem(f"win_landed{n}") for n in range(WQ)]
        places_landed = [st.sem(f"places_landed{n}") for n in range(PQ)]
        hotT_ready, hot_ready, var_ready, normed, u_ready = (
            st.sem(n) for n in ("hotT_ready", "hot_ready", "var_ready", "normed", "u_ready"))
        scaled, newton, stds_ready = st.sem("scaled"), st.sem("newton"), st.sem("stds_ready")
        z_ready, sums_ready, counts_ready = st.sem("z_ready"), st.sem("sums_ready"), st.sem("counts_ready")
        sq_ready, m_ready, sums_copied, sums_freed, counts_copied, counts_freed = (
            st.sem(n) for n in ("sq_ready", "m_ready", "sums_copied", "sums_freed", "counts_copied", "counts_freed"))
        cleared = st.sem("cleared")
        META = 3 * 16
        NEWTON = 12
        block = st.ctx.enter_context(nc.Block())

        @block.sync
        def _(sp):
            def fetch(b, *_):
                done(sp, z_ready, (b.i - RB + 1) * BQ)
                done(sp, hot_ready, (b.i - RB + 1) * BQ)
                done(sp, sums_copied, (b.i - RB) * BT + 1)
                settle(sp, st.passed)
                sp.dma_start(idx[:, b.c, :], w["src_b"][bass.ds(b.i, 1), :, :].rearrange("a p t -> (a p) t"))\
                  .then_inc(meta_landed[b.c], 16)
                sp.dma_start(cols[:, b.c, :], D["cols"][bass.ds(b.i, 1), :, :].rearrange("a p t -> (a p) t"))\
                  .then_inc(meta_landed[b.c], 16)
                sp.dma_start(n0[:, b.c, :], w["n0_b"][bass.ds(b.i, 1), :]).then_inc(meta_landed[b.c], 16)
                sp.wait_ge(meta_landed[b.c], (b.q + 1) * META)
                settle(sp, st.passed)
                _, starts = nc.values_load_multi_w_load_instructions(
                    n0[0:1, b.c, :], engines=(SP_ENGINE,), min_val=0, max_val=N,
                    skip_runtime_bounds_check_because="destinations are node numbers")
                for k in range(BQ):
                    s6, s4 = (b.c * BQ + k) % PQ, k
                    done(sp, hotT_ready, b.quad(k) - PQ + 1)
                    settle(sp, st.passed)
                    sp.dma_start(places[:, s6, :],
                                 D["places"][bass.ds(b.i, 1), k * QE:(k + 1) * QE].to_broadcast([P, QE]))\
                      .then_inc(places_landed[s6], 16)
                    done(sp, z_ready, b.quad(k) - WQ + 1)
                    settle(sp, st.passed)
                    sp.dma_start(ea[:, s4, :], w["ea"][:, bass.ds(b.i * BE + k * QE, QE)]).then_inc(win_landed[s4], 16)
                    for t in range(QT):
                        sp.dma_start(win[:, s4, t, :], a_table[bass.ds(starts[k * QT + t], P), :])\
                          .then_inc(win_landed[s4], 16)
            run_batches(sp, fetch)

        @block.gpsimd
        def _(pool):
            def gather(b, *_):
                pool.wait_ge(meta_landed[b.c], (b.q + 1) * META)
                for k in range(BQ):
                    done(pool, z_ready, b.quad(k) - GQ + 1)
                    settle(pool, st.passed)
                    for t in range(QT):
                        pool.indirect_dma_start(
                            gath[:, b.c * BQ + k, t, :], None, b_table,
                            bass.IndirectOffsetOnAxis(ap=idx[:, b.c, k * QT + t:k * QT + t + 1], axis=0))\
                            .then_inc(gath_landed[b.c * BQ + k], 16)
            run_batches(pool, gather)

        @block.tensor
        def _(pe):
            pe.sem_inc(z_ready, HEAD)
            pe.sem_inc(sums_ready, HEAD)
            pe.sem_inc(counts_ready, HEAD)

            def pre_activation(b, k):
                s6, s4, s12 = (b.c * BQ + k) % PQ, k, b.c * BQ + k
                zb = z[s12 % ZQ]
                pe.wait_ge(gath_landed[s12], (b.q + 1) * QT * 16)
                done(pe, normed, b.quad(k) - ZQ + 1)
                nc.tensor.matmul(zb[:, :], C["ident"][:, :], gath[:, s12, :, :].rearrange("p t f -> p (t f)"),
                                 start=True, stop=False, skip_group_check=True)
                pe.wait_ge(win_landed[s4], (b.i + 1) * (QT + 1) * 16)
                done(pe, hotT_ready, b.quad(k) + 1)
                for t in range(QT):
                    zt = zb[:, t * P:(t + 1) * P]
                    nc.tensor.matmul(zt, hotT[:, s6, t * P:(t + 1) * P], win[:, s4, t, :], start=False, stop=False,
                                     skip_group_check=True)
                    mm = nc.tensor.matmul(zt, ea[:, s4, t * P:(t + 1) * P], wc[:, :], start=False, stop=t == QT - 1,
                                          skip_group_check=True)
                mm.then_inc(z_ready, 1)

            def sum_up(b, k):
                s2, so, g = k % 2, k % SQ, b.quad(k)
                done(pe, hot_ready, g + 1)
                if l == 1:
                    done(pe, counts_freed, g)
                    nc.tensor.matmul(counts[0:1, :], C["ones"][:, 0:1], hot[:, s2, :, :].rearrange("p t n -> p (t n)"),
                                     start=True, stop=True).then_inc(counts_ready, 1)
                done(pe, m_ready, g + 1)
                done(pe, sums_freed, g - SQ + 1)
                for t in range(QT):
                    mm = nc.tensor.matmul(sums[so][:, t * P:(t + 1) * P], m[:, s2, t * P:(t + 1) * P], hot[:, s2, t, :],
                                          start=True, stop=True)
                mm.then_inc(sums_ready, 1)

            def step(b, nxt, after):
                for k in range(BQ):
                    if nxt and k + 1 < BQ:
                        pre_activation(nxt, k + 1)
                    elif after:
                        pre_activation(after, 0)
                    sum_up(b, k)
            for k in range(BQ):
                pre_activation(Batch(0, 0), k)
            pre_activation(Batch(0, 1), 0)
            run_batches(pe, step)

        @block.scalar
        def _(act):
            for s in (sq_ready, m_ready, sums_copied, sums_freed, counts_copied, counts_freed):
                act.sem_inc(s, HEAD)

            def square(b, k):
                g, s2 = b.quad(k), k % 2
                done(act, z_ready, g + 1)
                done(act, var_ready, g - 2 + 1)
                act.activation(sq[:, s2, :], z[(b.c * BQ + k) % ZQ][:, :], ACT.Square, scale=D0 ** -0.5).then_inc(sq_ready, 1)

            def copies(b, k, starts):
                g, so = b.quad(k), k % SQ
                outs = [(count, first_count, counts[0:1, :], counts_ready, counts_copied, counts_freed)] if l == 1 else []
                outs.append((acc, first, sums[so][:, :], sums_ready, sums_copied, sums_freed))
                for *_, ready, _, _ in outs:
                    done(act, ready, g + 1)
                for t in range(QT):
                    for kept, _, new, _, copied, _ in outs:
                        done(act, copied, g * QT + t)
                        act.copy(kept[:, bass.ds(starts[k * QT + t] + 1, P - 1)], new[:, t * P + 1:(t + 1) * P])\
                           .then_inc(copied, 1)
                for _, kept_first, new, _, _, freed in outs:
                    act.copy(kept_first[:, bass.ds(g * QT, QT)], new.rearrange("p (t n) -> p t n", n=P)[:, :, 0])\
                       .then_inc(freed, 1)

            def step(b, nxt, after):
                act.wait_ge(meta_landed[b.c], (b.q + 1) * META)
                settle(act, st.passed)
                _, starts = nc.values_load_multi_w_load_instructions(
                    n0[0:1, b.c, :], engines=(ACT_ENGINE,), min_val=0, max_val=N,
                    skip_runtime_bounds_check_because="destinations are node numbers")
                for k in range(BQ):
                    g, s2 = b.quad(k), k % 2
                    done(act, u_ready, g + 1)
                    done(act, sums_ready, g - 2 + 1)
                    act.activation(m[:, s2, :], u[:, s2, :], ACT.Silu).then_inc(m_ready, 1)
                    if nxt and k + 1 < BQ:
                        square(nxt, k + 1)
                    elif after:
                        square(after, 0)
                    copies(b, k, starts)
            act.wait_ge(cleared, 1)
            for k in range(BQ):
                square(Batch(0, 0), k)
            square(Batch(0, 1), 0)
            run_batches(act, step)

        @block.vector
        def _(dve):
            for s in (hotT_ready, hot_ready, var_ready, normed, scaled, u_ready, stds_ready):
                dve.sem_inc(s, HEAD)
            nc.vector.memset(first[:, :], 0.0)
            if l == 1:
                nc.vector.memset(count[:, :], 0.0)
                nc.vector.memset(first_count[:, :], 0.0)
            nc.vector.memset(acc[:, :], 0.0).then_inc(cleared, 1)

            def one_hot_T(b, k):
                s6 = (b.c * BQ + k) % PQ
                dve.wait_ge(places_landed[s6], ((b.i * BQ + k) // PQ + 1) * 16 if isinstance(b.i, int)
                            else (b.q * (GQ // PQ) + (b.c * BQ + k) // PQ + 1) * 16)
                done(dve, z_ready, b.quad(k) - PQ + 1)
                nc.vector.tensor_scalar(hotT[:, s6, :], places[:, s6, :], C["iota_col"][:, 0:1], None, ALU.is_equal)\
                  .then_inc(hotT_ready, 1)

            def variance(b, k):
                done(dve, sq_ready, b.quad(k) + 1)
                if k == 0:
                    done(dve, stds_ready, b.i)
                nc.vector.tensor_reduce(var[:, k * QT * H0:(k + 1) * QT * H0],
                                        sq[:, k % 2, :].rearrange("p (g w) -> p g w", w=D0), AX.X, ALU.add)\
                  .then_inc(var_ready, 1)

            def inverse_stds(b):
                done(dve, var_ready, b.quad(BQ))
                done(dve, normed, b.quad(0))
                link = Chain(dve, newton, b.i * NEWTON)
                link(nc.vector.tensor_scalar(var[:, :], var[:, :], EPS, None, ALU.add))
                rsqrt(nc, link, var[:, :], rstd[:, :], tmp[:, :])
                assert link.n == NEWTON
                dve.sem_inc(stds_ready, 1)

            def pre_message(b, k):
                g, s2 = b.quad(k), k % 2
                done(dve, m_ready, g - 2 + 1)
                ug = u[:, s2, :].rearrange("p (g w) -> p g w", w=D0)
                ut = u[:, s2, :].rearrange("p (t f) -> p t f", f=P)
                r = rstd[:, k * QT * H0:(k + 1) * QT * H0].unsqueeze(2)
                nc.vector.tensor_tensor(ug, z[(b.c * BQ + k) % ZQ][:, :].rearrange("p (g w) -> p g w", w=D0),
                                        bc(r, [P, QT * H0, D0]), ALU.mult).then_inc(normed, 1)
                done(dve, sums_ready, g - 2 + 1)
                nc.vector.tensor_tensor(hot[:, s2, :, :], bc(C["iota_row"][:, :].unsqueeze(1), [P, QT, P]),
                                        bc(cols[:, b.c, k * QT:(k + 1) * QT].unsqueeze(2), [P, QT, P]), ALU.is_equal)\
                  .then_inc(hot_ready, 1)
                done(dve, normed, g + 1)
                nc.vector.tensor_tensor(ut, ut, bc(gamma.unsqueeze(1), [P, QT, P]), ALU.mult).then_inc(scaled, 1)
                done(dve, scaled, g + 1)
                nc.vector.tensor_tensor(ut, ut, bc(beta.unsqueeze(1), [P, QT, P]), ALU.add).then_inc(u_ready, 1)

            def step(b, nxt, after):
                dve.wait_ge(meta_landed[b.c], (b.q + 1) * META)
                for k in range(BQ):
                    if nxt and k + 2 < BQ:
                        one_hot_T(nxt, k + 2)
                    elif after and k + 2 >= BQ:
                        one_hot_T(after, k + 2 - BQ)
                    pre_message(b, k)
                    if nxt:
                        variance(nxt, k)
                if nxt:
                    inverse_stds(nxt)
            for k in range(BQ):
                one_hot_T(Batch(0, 0), k)
            one_hot_T(Batch(0, 1), 0)
            one_hot_T(Batch(0, 1), 1)
            for k in range(BQ):
                variance(Batch(0, 0), k)
            inverse_stds(Batch(0, 0))
            run_batches(dve, step)


def attention_edges(nc, gat, w, C, D, acc, first, acc_e, first_e, small, first_small):
    table = D["g"] if gat else D["kv"]
    RW = P + H1 if gat else 2 * P
    win_table, WW = (D["ed"], NS) if gat else (D["q"], P)
    GQ, WQ, PQ = RB * BQ, 4, 4
    with Stage(nc, "gat" if gat else "attn") as st:
        idx = st.sb("idx", [P, RB, BT], I32)
        starts_in = st.sb("starts_in", [1, RB, BT], I32)
        n0 = st.sb("n0", [1, RB, BT], I32)
        cols = st.sb("cols", [P, RB, 2 * BT])
        mask = st.sb("mask", [P, RB, P + 1])
        gath = st.sb("gath", [P, GQ, QT, RW])
        win = st.sb("win", [P, WQ, QT, WW])
        places = st.sb("places", [P, PQ, QE], BF16)
        hotT = st.sb("hotT", [P, PQ, QE])
        hot = st.sb("hot", [P, 2, QT, P])
        logit = st.sb("logit", [P, BT, NS])
        logit2 = st.sb("logit2", [P, BT, NS])
        run_max, seg_max = st.sb("run_max", [P, P]), st.sb("seg_max", [P, P])
        below = st.sb("below", [P, P])
        sm = st.sb("sm", [P, RB, BT, SMW])
        val = st.sb("val", [P, 2, QT, P])
        p_logit = st.ps("p_logit", [P, 512])
        p_turn = st.ps("p_turn", [P, 512])
        if gat:
            xeT = st.sb("xeT", [P, GQ, QE])
            val_e = st.sb("val_e", [P, 2, QT, P])
            p_he = st.ps("p_he", [P, QE])
            sums = [st.ps(f"sums{n}", [P, QE]) for n in range(2)]
            sums_e = [st.ps(f"sums_e{n}", [P, QE]) for n in range(2)]
            smalls = [st.ps("smalls", [P, QE])]
        else:
            ea = st.sb("ea", [ED + 1, WQ, QE])
            prod = st.sb("prod", [P, 2, QE])
            p_q = [st.ps(f"p_q{n}", [P, QE]) for n in range(2)]
            sums = [st.ps(f"sums{n}", [P, QE]) for n in range(2)]
            smalls = [st.ps(f"smalls{n}", [P, QE]) for n in range(2)]
        NO, NSM = len(sums), len(smalls)

        early_landed = [st.sem(f"early_landed{c}") for c in range(RB)]
        late_landed = [st.sem(f"late_landed{c}") for c in range(RB)]
        gath_landed = [st.sem(f"gath_landed{n}") for n in range(GQ)]
        win_landed = [st.sem(f"win_landed{n}") for n in range(WQ)]
        places_landed = [st.sem(f"places_landed{n}") for n in range(PQ)]
        hotT_ready, hot_ready, cleared = st.sem("hotT_ready"), st.sem("hot_ready"), st.sem("cleared")
        scored, he_ready, part_ready, parts_summed = (
            st.sem(n) for n in ("scored", "he_ready", "part_ready", "parts_summed"))
        smalls_ready, sums_ready, sums_e_ready = (st.sem(n) for n in ("smalls_ready", "sums_ready", "sums_e_ready"))
        small_copied, sums_copied, sums_e_copied = (st.sem(n) for n in ("small_copied", "sums_copied", "sums_e_copied"))
        small_freed, sums_freed, sums_e_freed = (st.sem(n) for n in ("small_freed", "sums_freed", "sums_e_freed"))
        logit_ready, logitT_ready, below_ready, ex_ready, turned = (
            st.sem(n) for n in ("logit_ready", "logitT_ready", "below_ready", "ex_ready", "turned"))
        sm_ready, val_ready, val_e_ready = st.sem("sm_ready"), st.sem("val_ready"), st.sem("val_e_ready")
        maxima, logit_parts = st.sem("maxima"), st.sem("logit_parts")
        EARLY, LATE = 2 * 16, 3 * 16
        WINS = (QT + 1) * 16
        block = st.ctx.enter_context(nc.Block())

        @block.sync
        def _(sp):
            def early(b):
                done(sp, logit_ready, b.i - RB + 1)
                settle(sp, st.passed)
                sp.dma_start(idx[:, b.c, :], w["src_b"][bass.ds(b.i, 1), :, :].rearrange("a p t -> (a p) t"))\
                  .then_inc(early_landed[b.c], 16)
                sp.dma_start(starts_in[:, b.c, :], w["n0_b"][bass.ds(b.i, 1), :]).then_inc(early_landed[b.c], 16)

            def fetch(b, nxt, _):
                if nxt:
                    early(nxt)
                sp.wait_ge(early_landed[b.c], (b.q + 1) * EARLY)
                settle(sp, st.passed)
                _, starts = nc.values_load_multi_w_load_instructions(
                    starts_in[0:1, b.c, :], engines=(SP_ENGINE,), min_val=0, max_val=N,
                    skip_runtime_bounds_check_because="destinations are node numbers")
                for k in range(BQ):
                    s4 = k
                    done(sp, hotT_ready, b.quad(k) - PQ + 1)
                    settle(sp, st.passed)
                    sp.dma_start(places[:, s4, :],
                                 D["places"][bass.ds(b.i, 1), k * QE:(k + 1) * QE].to_broadcast([P, QE]))\
                      .then_inc(places_landed[s4], 16)
                    done(sp, scored, b.quad(k) - WQ + 1)
                    settle(sp, st.passed)
                    for t in range(QT):
                        sp.dma_start(win[:, s4, t, :], win_table[bass.ds(starts[k * QT + t], P), :])\
                          .then_inc(win_landed[s4], 16)
                    if gat:
                        done(sp, he_ready, b.quad(k) - GQ + 1)
                        settle(sp, st.passed)
                        sp.dma_start(xeT[:, b.c * BQ + k, :], w["xeT"][:, bass.ds(b.i * BE + k * QE, QE)])\
                          .then_inc(win_landed[s4], 16)
                    else:
                        sp.dma_start(ea[:, s4, :], w["ea"][:, bass.ds(b.i * BE + k * QE, QE)])\
                          .then_inc(win_landed[s4], 16)
                done(sp, hot_ready, (b.i - RB + 1) * BQ)
                done(sp, small_copied, (b.i - RB) * BT + 1)
                settle(sp, st.passed)
                sp.dma_start(cols[:, b.c, :], D["cols"][bass.ds(b.i, 1), :, :].rearrange("a p t -> (a p) t"))\
                  .then_inc(late_landed[b.c], 16)
                sp.dma_start(n0[:, b.c, :], w["n0_b"][bass.ds(b.i, 1), :]).then_inc(late_landed[b.c], 16)
                sp.dma_start(mask[:, b.c, :], D["mask"][bass.ds(b.i * P, P), :]).then_inc(late_landed[b.c], 16)
            early(Batch(0, 0))
            run_batches(sp, fetch)

        @block.gpsimd
        def _(pool):
            def gather(b, *_):
                pool.wait_ge(early_landed[b.c], (b.q + 1) * EARLY)
                for k in range(BQ):
                    done(pool, val_ready, b.quad(k) - GQ + 1)
                    settle(pool, st.passed)
                    for t in range(QT):
                        pool.indirect_dma_start(
                            gath[:, b.c * BQ + k, t, :], None, table,
                            bass.IndirectOffsetOnAxis(ap=idx[:, b.c, k * QT + t:k * QT + t + 1], axis=0))\
                            .then_inc(gath_landed[b.c * BQ + k], 16)
            run_batches(pool, gather)

        @block.tensor
        def _(pe):
            for s in (scored, he_ready, smalls_ready, sums_ready, sums_e_ready, logitT_ready, turned):
                pe.sem_inc(s, HEAD)

            def score(b, k):
                s4, g = k, b.quad(k)
                pe.wait_ge(win_landed[s4], (b.i + 1) * WINS)
                done(pe, hotT_ready, g + 1)
                if k == 0:
                    done(pe, logit_ready, b.i - RB + 1)
                if not gat:
                    done(pe, part_ready, g - 2 + 1)
                for t in range(QT):
                    e = slice(t * P, (t + 1) * P)
                    lt = p_logit[:, b.c * P + (k * QT + t) * NS:b.c * P + (k * QT + t + 1) * NS]
                    if gat:
                        nc.tensor.matmul(lt, hotT[:, s4, e], win[:, s4, t, :], start=True, stop=False,
                                         skip_group_check=True)
                        mm = nc.tensor.matmul(lt[:, H1:NS], xeT[:, b.c * BQ + k, e], C["wea"][:, :], start=False,
                                              stop=True, skip_group_check=True)
                    else:
                        nc.tensor.matmul(p_q[k % 2][:, e], hotT[:, s4, e], win[:, s4, t, :], start=True, stop=True)
                        mm = nc.tensor.matmul(lt, ea[:, s4, e], C["we"][:, :], start=True, stop=True)
                mm.then_inc(scored, 1)

            def turn(b):
                done(pe, logit_ready, b.i + 1)
                done(pe, below_ready, b.i)
                nc.tensor.transpose(p_turn[:, 0:P], logit2[:, :, :].rearrange("p t s -> p (t s)"), C["ident"][:, :])\
                  .then_inc(logitT_ready, 1)

            def turn_back(b):
                done(pe, ex_ready, b.i + 1)
                done(pe, sm_ready, 2 * b.i)
                nc.tensor.transpose(p_turn[:, P:2 * P], below[:, :], C["ident"][:, :])
                nc.tensor.transpose(p_turn[:, 2 * P:3 * P], seg_max[:, :], C["ident"][:, :]).then_inc(turned, 1)

            def sum_up(b, k):
                s2, g, so = k % 2, b.quad(k), k % NO
                if gat:
                    done(pe, val_e_ready, g)
                    for t in range(QT):
                        mm = nc.tensor.matmul(p_he[:, t * P:(t + 1) * P], xeT[:, b.c * BQ + k, t * P:(t + 1) * P],
                                              C["wet"][:, :], start=True, stop=True)
                    mm.then_inc(he_ready, 1)
                done(pe, hot_ready, g + 1)
                done(pe, val_ready, g + 1)
                done(pe, sums_freed, g - NO + 1)
                for t in range(QT):
                    mm = nc.tensor.matmul(sums[so][:, t * P:(t + 1) * P], val[:, s2, t, :], hot[:, s2, t, :],
                                          start=True, stop=True)
                mm.then_inc(sums_ready, 1)
                if gat:
                    done(pe, val_e_ready, g + 1)
                    done(pe, sums_e_freed, g - NO + 1)
                    for t in range(QT):
                        mm = nc.tensor.matmul(sums_e[so][:, t * P:(t + 1) * P], val_e[:, s2, t, :], hot[:, s2, t, :],
                                              start=True, stop=True)
                    mm.then_inc(sums_e_ready, 1)
                done(pe, sm_ready, 2 * (b.i + 1))
                done(pe, small_freed, g - NSM + 1)
                for t in range(QT):
                    mm = nc.tensor.matmul(smalls[k % NSM][0:SMW, t * P:(t + 1) * P], sm[:, b.c, k * QT + t, :],
                                          hot[:, s2, t, :], start=True, stop=True)
                mm.then_inc(smalls_ready, 1)

            def step(b, nxt, after):
                for k in range(BQ):
                    if after:
                        score(after, k)
                    if nxt and k == 0:
                        turn(nxt)
                    sum_up(b, k)
                    if nxt and k == 2:
                        turn_back(nxt)
            for b in (Batch(0, 0), Batch(0, 1)):
                for k in range(BQ):
                    score(b, k)
                if b.c == 0:
                    turn(b)
                    turn_back(b)
            run_batches(pe, step)

        @block.scalar
        def _(act):
            for s in (ex_ready, small_copied, sums_copied, sums_e_copied, small_freed, sums_freed, sums_e_freed):
                act.sem_inc(s, HEAD)

            def exponent(b):
                done(act, below_ready, b.i + 1)
                act.activation(below[:, :], below[:, :], ACT.Exp).then_inc(ex_ready, 1)

            def copies(b, k, starts):
                g, so = b.quad(k), k % NO
                outs = [(small, first_small, smalls[k % NSM][0:SMW, :], smalls_ready, small_copied, small_freed),
                        (acc, first, sums[so][:, :], sums_ready, sums_copied, sums_freed)]
                if gat:
                    outs.append((acc_e, first_e, sums_e[so][:, :], sums_e_ready, sums_e_copied, sums_e_freed))
                for *_, ready, _, _ in outs:
                    done(act, ready, g + 1)
                for t in range(QT):
                    for kept, _, new, _, copied, _ in outs:
                        done(act, copied, g * QT + t)
                        act.copy(kept[:, bass.ds(starts[k * QT + t] + 1, P - 1)], new[:, t * P + 1:(t + 1) * P])\
                           .then_inc(copied, 1)
                for _, kept_first, new, _, _, freed in outs:
                    act.copy(kept_first[:, bass.ds(g * QT, QT)], new.rearrange("p (t n) -> p t n", n=P)[:, :, 0])\
                       .then_inc(freed, 1)

            def step(b, nxt, _):
                act.wait_ge(late_landed[b.c], (b.q + 1) * LATE)
                settle(act, st.passed)
                _, starts = nc.values_load_multi_w_load_instructions(
                    n0[0:1, b.c, :], engines=(ACT_ENGINE,), min_val=0, max_val=N,
                    skip_runtime_bounds_check_because="destinations are node numbers")
                for k in range(BQ):
                    copies(b, k, starts)
                    if nxt and k == 0:
                        exponent(nxt)
            act.wait_ge(cleared, 1)
            exponent(Batch(0, 0))
            run_batches(act, step)

        @block.vector
        def _(dve):
            for s in (hotT_ready, hot_ready, logit_ready, below_ready, sm_ready, val_ready, part_ready, parts_summed,
                      val_e_ready, maxima, logit_parts):
                dve.sem_inc(s, HEAD)
            nc.vector.memset(sm[:, :, :, :], 0.0)
            nc.vector.memset(small[:, :], 0.0)
            nc.vector.memset(first_small[:, :], 0.0)
            nc.vector.memset(first[:, :], 0.0)
            if gat:
                nc.vector.memset(acc_e[:, :], 0.0)
                nc.vector.memset(first_e[:, :], 0.0)
            nc.vector.memset(acc[:, :], 0.0).then_inc(cleared, 1)
            dve.wait_ge(cleared, 1)

            def one_hot_T(b, k):
                dve.wait_ge(places_landed[k], (b.i + 1) * 16)
                done(dve, scored, b.quad(k) - PQ + 1)
                nc.vector.tensor_scalar(hotT[:, k, :], places[:, k, :], C["iota_col"][:, 0:1], None, ALU.is_equal)\
                  .then_inc(hotT_ready, 1)

            def score(b, k):
                g, s12, s2 = b.quad(k), b.c * BQ + k, k % 2
                dve.wait_ge(gath_landed[s12], (b.q + 1) * QT * 16)
                done(dve, scored, g + 1)
                nc.vector.tensor_tensor(prod[:, s2, :].rearrange("p (t f) -> p t f", f=P),
                                        p_q[s2][:, :].rearrange("p (t f) -> p t f", f=P), gath[:, s12, :, 0:P], ALU.mult)\
                  .then_inc(part_ready, 1)
                done(dve, part_ready, g + 1)
                if k == 0:
                    done(dve, logit_ready, b.i)
                nc.vector.tensor_reduce(logit[:, k * QT:(k + 1) * QT, :].rearrange("p t s -> p (t s)"),
                                        prod[:, s2, :].rearrange("p (g w) -> p g w", w=D0), AX.X, ALU.add)\
                  .then_inc(parts_summed, 1)

            def logits(b):
                pl = p_logit[:, b.c * P:(b.c + 1) * P].rearrange("p (t s) -> p t s", s=NS)
                done(dve, scored, b.quad(BQ))
                if gat:
                    for k in range(BQ):
                        dve.wait_ge(gath_landed[b.c * BQ + k], (b.q + 1) * QT * 16)
                    g = gath[:, b.c * BQ:(b.c + 1) * BQ, :, P:RW].rearrange("p q t s -> p (q t) s")
                    done(dve, logit_ready, b.i)
                    nc.vector.tensor_tensor(logit[:, :, 0:H1], pl[:, :, 0:H1], g, ALU.add).then_inc(logit_parts, 1)
                    nc.vector.tensor_copy(logit[:, :, H1:NS], pl[:, :, H1:NS]).then_inc(logit_parts, 1)
                    done(dve, logit_parts, 2 * (b.i + 1))
                    done(dve, logitT_ready, b.i)
                    nc.vector.scalar_tensor_tensor(logit2[:, :, :], logit[:, :, :], 0.2, logit[:, :, :],
                                                   ALU.mult, ALU.max).then_inc(logit_ready, 1)
                else:
                    done(dve, parts_summed, b.quad(BQ))
                    done(dve, logitT_ready, b.i)
                    nc.vector.tensor_tensor(logit2[:, :, :], logit[:, :, :], pl, ALU.add).then_inc(logit_ready, 1)

            def against_maxima(b):
                dve.wait_ge(late_landed[b.c], (b.q + 1) * LATE)
                done(dve, logitT_ready, b.i + 1)
                done(dve, turned, b.i)
                nc.vector.tensor_tensor_scan(run_max[:, :], mask[:, b.c, 0:P], p_turn[:, 0:P], -BIG, ALU.add, ALU.max)\
                  .then_inc(maxima, 1)
                done(dve, maxima, 2 * b.i + 1)
                nc.vector.tensor_tensor_scan(seg_max[:, ::-1], mask[:, b.c, P:0:-1], run_max[:, ::-1], -BIG,
                                             ALU.add, ALU.max).then_inc(maxima, 1)
                done(dve, maxima, 2 * b.i + 2)
                nc.vector.tensor_tensor(below[:, :], p_turn[:, 0:P], seg_max[:, :], ALU.subtract).then_inc(below_ready, 1)

            def weights(b):
                done(dve, turned, b.i + 1)
                done(dve, smalls_ready, (b.i - RB + 1) * BQ)
                pt = p_turn[:, P:3 * P].rearrange("p (a t s) -> p a t s", a=2, s=NS)
                nc.vector.tensor_copy(sm[:, b.c, :, 0:NS], pt[:, 0, :, :]).then_inc(sm_ready, 1)
                nc.vector.tensor_tensor(sm[:, b.c, :, MR:SMW], pt[:, 1, :, :],
                                        bc(cols[:, b.c, BT:2 * BT].unsqueeze(2), [P, BT, NS]), ALU.mult)\
                  .then_inc(sm_ready, 1)

            def weigh(b, k):
                g, s2, s12 = b.quad(k), k % 2, b.c * BQ + k
                done(dve, smalls_ready, g - 2 + 1)
                nc.vector.tensor_tensor(hot[:, s2, :, :], bc(C["iota_row"][:, :].unsqueeze(1), [P, QT, P]),
                                        bc(cols[:, b.c, k * QT:(k + 1) * QT].unsqueeze(2), [P, QT, P]), ALU.is_equal)\
                  .then_inc(hot_ready, 1)
                done(dve, sm_ready, 2 * (b.i + 1))
                wts = sm[:, b.c, k * QT:(k + 1) * QT, :]
                heads, width, v0 = (H1, D1, 0) if gat else (H0, D0, P)
                nc.vector.tensor_tensor(val[:, s2, :, :].rearrange("p t (h d) -> p t h d", d=width),
                                        gath[:, s12, :, v0:v0 + P].rearrange("p t (h d) -> p t h d", d=width),
                                        bc(wts[:, :, 0:heads].unsqueeze(3), [P, QT, heads, width]), ALU.mult)\
                  .then_inc(val_ready, 1)
                if gat:
                    done(dve, he_ready, g + 1)
                    nc.vector.tensor_tensor(val_e[:, s2, :, :].rearrange("p t (h d) -> p t h d", d=D1),
                                            p_he[:, :].rearrange("p (t h d) -> p t h d", h=H1, d=D1),
                                            bc(wts[:, :, H1:NS].unsqueeze(3), [P, QT, H1, D1]), ALU.mult)\
                      .then_inc(val_e_ready, 1)

            def step(b, nxt, after):
                for k in range(BQ):
                    if after:
                        one_hot_T(after, k)
                    weigh(b, k)
                    if after and not gat:
                        score(after, k)
                    if nxt and k == 0:
                        against_maxima(nxt)
                if nxt:
                    weights(nxt)
                if after:
                    logits(after)
            for b in (Batch(0, 0), Batch(0, 1)):
                for k in range(BQ):
                    one_hot_T(b, k)
                    if not gat:
                        score(b, k)
                logits(b)
                if b.c == 0:
                    against_maxima(b)
                    weights(b)
            run_batches(dve, step)


def fold(nc, name, w, C, table, first, first_e, first_small, soft):
    with Stage(nc, name) as st:
        n0 = st.sb("n0", [P, TP], I32)
        n0f = st.sb("n0f", [P, TP])
        same = st.sb("same", [P, TP])
        part = st.sb("part", [P, TP + 1])
        W = table.shape[1]
        rows = st.sb("rows", [P, 2, W])
        folded = [st.sb(f"folded{n}", [P, TP]) for n in range(2 if first_e is not None else 1)]
        parts = [first] + ([first_e] if first_e is not None else [])
        SW = 0 if first_small is None else SMW if soft else 1
        small = st.sb("small", [max(SW, 1), TP])
        p_f = [st.ps(f"p_f{n}", [P, 512]) for n in range(2)]
        p_s = st.ps("p_s", [P, 512])
        p_t = [st.ps(f"p_t{n}", [P, 512]) for n in range(2)]
        loaded, chain, ex_ready, expanded, scaled = (st.sem(n) for n in ("loaded", "chain", "ex_ready", "expanded", "scaled"))
        below_ready, summed, turned, rows_ready = (st.sem(n) for n in ("below_ready", "summed", "turned", "rows_ready"))
        stored = [st.sem(f"stored{n}") for n in range(2)]
        if soft:
            run_max, below = st.sb("run_max", [SMW, TP]), st.sb("below", [SMW, TP])
        CH = -(-TP // 512)
        block = st.ctx.enter_context(nc.Block())

        @block.sync
        def _(sp):
            sp.dma_start(n0[:, :], w["n0_p"].to_broadcast([P, TP])).then_inc(loaded, 16)

        @block.vector
        def _(dve):
            link = Chain(dve, chain)
            if soft:
                link(nc.vector.memset(small[:, :], 0.0))
            dve.wait_ge(loaded, 16)
            link(nc.vector.tensor_copy(n0f[:, :], n0[:, :]))
            link(nc.vector.memset(same[:, 0:1], 0.0))
            link(nc.vector.tensor_tensor(same[:, 1:TP], n0f[:, 1:TP], n0f[:, 0:TP - 1], ALU.is_equal))
            if soft:
                m = slice(MR, SMW)
                link(nc.vector.tensor_scalar(part[:, 0:TP], same[:, :], -1.0, BIG, ALU.add, ALU.mult))
                link(nc.vector.memset(part[:, TP:TP + 1], -BIG))
                link(nc.vector.tensor_tensor_scan(run_max[m, :], part[m, 0:TP], first_small[m, :], -BIG, ALU.add, ALU.max))
                link(nc.vector.tensor_tensor_scan(small[m, ::-1], part[m, TP:0:-1], run_max[m, ::-1], -BIG, ALU.add, ALU.max))
                nc.vector.tensor_tensor(below[m, :], first_small[m, :], small[m, :], ALU.subtract).then_inc(below_ready, 1)
                for c in range(CH):
                    e = slice(c * 512, min(TP, (c + 1) * 512))
                    n = e.stop - e.start
                    dve.wait_ge(expanded, c + 1)
                    for i, t in enumerate(parts):
                        link(nc.vector.tensor_tensor(t[:, e], t[:, e], p_f[i][:, 0:n], ALU.mult))
                    link(nc.vector.tensor_tensor(first_small[0:NS, e], first_small[0:NS, e], p_s[0:NS, 0:n], ALU.mult))
                    dve.sem_inc(scaled, 1)
            for i, t in enumerate(parts):
                link(nc.vector.tensor_tensor_scan(folded[i][:, :], same[:, :], t[:, :], 0.0, ALU.mult, ALU.add))
            if SW:
                r = NS if soft else 1
                link(nc.vector.tensor_tensor_scan(small[0:r, :], same[0:r, :], first_small[0:r, :], 0.0, ALU.mult, ALU.add))
            dve.sem_inc(summed, 1)
            for c in range(TC):
                dve.wait_ge(turned, c + 1)
                if c >= 2:
                    dve.wait_ge(stored[c % 2], c // 2 * 16)
                nc.vector.tensor_copy(rows[:, c % 2, :], p_t[c % 2][:, 0:W]).then_inc(rows_ready, 1)

        @block.scalar
        def _(act):
            if soft:
                act.wait_ge(below_ready, 1)
                act.activation(below[MR:SMW, :], below[MR:SMW, :], ACT.Exp).then_inc(ex_ready, 1)

        @block.tensor
        def _(pe):
            if soft:
                pe.wait_ge(ex_ready, 1)
                for c in range(CH):
                    e = slice(c * 512, min(TP, (c + 1) * 512))
                    n = e.stop - e.start
                    if c:
                        pe.wait_ge(scaled, c)
                    for i, lay in enumerate(soft):
                        nc.tensor.matmul(p_f[i][:, 0:n], C["expand"][MR:SMW, lay, :], below[MR:SMW, e], start=True, stop=True)
                    nc.tensor.matmul(p_s[0:NS, 0:n], C["ident"][MR:SMW, MR:SMW], below[MR:SMW, e], start=True, stop=True)\
                      .then_inc(expanded, 1)
            pe.wait_ge(summed, 1)
            for c in range(TC):
                e = slice(c * P, (c + 1) * P)
                if c >= 2:
                    pe.wait_ge(rows_ready, c - 1)
                for i in range(len(parts)):
                    mm = nc.tensor.transpose(p_t[c % 2][:, i * P:(i + 1) * P], folded[i][:, e], C["ident"][:, :])
                if SW:
                    mm = nc.tensor.transpose(p_t[c % 2][:, len(parts) * P:W], small[0:SW, e], C["ident"][0:SW, 0:SW])
                mm.then_inc(turned, 1)

        @block.gpsimd
        def _(pool):
            for c in range(TC):
                pool.wait_ge(rows_ready, c + 1)
                pool.indirect_dma_start(table, bass.IndirectOffsetOnAxis(ap=C["fold_row"][:, c:c + 1], axis=0),
                                        rows[:, c % 2, :], None, bounds_check=NP - 1, oob_is_err=False)\
                    .then_inc(stored[c % 2], 16)
            pool.wait_ge(stored[0], (TC + 1) // 2 * 16)
            pool.wait_ge(stored[1], TC // 2 * 16)


def blocks_of(table, g):
    return table[bass.ds(g * GW, GW), :].rearrange("(b p) c -> p b c", p=P)


def node_stage(nc, kind, w, C, D, hres, cnt, acc, acc_e, small, out):
    soft = kind in ("attn", "gat")
    fold_table = {"first": None, "conv1": D["fold1"], "conv2": D["fold2"], "attn": D["fold3"], "gat": D["fold4"]}[kind]
    FW = fold_table.shape[1] if fold_table is not None else 1
    with Stage(nc, "n_" + kind) as st:
        x = st.sb("x", [P, GB, P])
        fr = st.sb("fr", [P, GB, FW])
        h, sq, h2 = (st.sb(n, [P, GB, P]) for n in ("h", "sq", "h2"))
        totT = st.sb("totT", [P, GW])
        totT_e = st.sb("totT_e", [P, GW])
        mean, rstd, tmp = (st.sb(n, [P, GB * H0]) for n in ("mean", "rstd", "tmp"))
        cT = st.sb("cT", [SMW, GW])
        sb_small = st.sb("sb_small", [P, GB, SMW])
        M, fa, fb, S = (st.sb(n, [P, GB, NS]) for n in ("M", "fa", "fb", "S"))
        made = st.sb("made", [P, GB, 2 * P])
        made_s = st.sb("made_s", [P, GB, 3 * H1])
        p1, p2, p_w = st.ps("p1", [P, 1024]), st.ps("p2", [P, 1024]), st.ps("p_w", [P, 2048])
        p1b = p1[:, 0:GW].rearrange("p (b f) -> p b f", f=P)
        p2b = p2[:, 0:GW].rearrange("p (b f) -> p b f", f=P)
        pwb = p_w[:, 0:GB * 2 * P].rearrange("p (b f) -> p b f", f=2 * P)
        p_ws = p2[:, GW:GW + GB * 3 * H1].rearrange("p (b s) -> p b s", s=3 * H1)
        names = ("loaded", "chain", "copied", "turned1", "tot_ready", "mapped", "pre_act", "acted", "h_ready", "turned2",
                 "hT_ready", "tables_ready", "evacuated", "stored", "below_ready", "ex_ready", "o_ready", "o_turned", "oT_ready")
        (loaded, chain, copied, turned1, tot_ready, mapped, pre_act, acted, h_ready, turned2, hT_ready, tables_ready,
         evacuated, stored, below_ready, ex_ready, o_ready, o_turned, oT_ready) = (st.sem(n) for n in names)
        hT = totT_e if not kind == "gat" else totT
        LOADS = 16 * ((kind in ("first", "attn", "gat")) + (fold_table is not None))
        STORES = 16 * {"first": 2, "conv1": 2, "conv2": 2, "attn": 3, "gat": 1}[kind]
        wide = [P, GB, P]
        lens = {}

        block = st.ctx.enter_context(nc.Block())

        @block.sync
        def _(sp):
            with sp.Fori(0, NGRP) as g:
                sp.wait_ge(evacuated, g + 1)
                settle(sp, st.passed)
                if kind in ("first", "attn", "gat"):
                    sp.dma_start(x[:, :, :], blocks_of(D["base"] if kind == "gat" else w["x"], g)).then_inc(loaded, 16)
                if fold_table is not None:
                    sp.dma_start(fr[:, :, :], blocks_of(fold_table, g)).then_inc(loaded, 16)
                sp.wait_ge(evacuated, g + 2)
                settle(sp, st.passed)
                if kind in ("first", "conv1"):
                    l = 1 if kind == "first" else 2
                    sp.dma_start(blocks_of(D[f"a{l}"], g), made[:, :, 0:P]).then_inc(stored, 16)
                    sp.dma_start(blocks_of(D[f"b{l}"], g), made[:, :, P:2 * P]).then_inc(stored, 16)
                elif kind == "conv2":
                    sp.dma_start(blocks_of(D["q"], g), h[:, :, :]).then_inc(stored, 16)
                    sp.dma_start(blocks_of(D["kv"], g), made[:, :, :]).then_inc(stored, 16)
                elif kind == "attn":
                    sp.dma_start(blocks_of(D["g"], g), made[:, :, 0:P + H1]).then_inc(stored, 16)
                    sp.dma_start(blocks_of(D["base"], g), x[:, :, :]).then_inc(stored, 16)
                    sp.dma_start(blocks_of(D["ed"], g), made_s[:, :, H1:3 * H1]).then_inc(stored, 16)
                else:
                    sp.dma_start(blocks_of(out, g), h[:, :, :]).then_inc(stored, 16)
                sp.wait_ge(stored, (g + 1) * STORES)
                settle(sp, st.passed)

        @block.tensor
        def _(pe):
            ident = C["ident"][:, :]
            with pe.Fori(0, NGRP) as g:
                if kind in ("conv1", "conv2"):
                    pe.wait_ge(loaded, (g + 1) * LOADS)
                    pe.wait_ge(evacuated, g + 1)
                    for b in range(GB):
                        mm = nc.tensor.transpose(p1b[:, b, :], fr[:, b, 0:P], ident)
                    if kind == "conv1":
                        pe.wait_ge(copied, g + 1)
                        settle(pe, st.passed)
                        for b in range(GB):
                            mm = nc.tensor.transpose(p2[:, b:b + 1], cT[0:1, b * P:(b + 1) * P], ident[0:1, 0:1])
                    mm.then_inc(turned1, 1)
                    pe.wait_ge(tot_ready, g + 1)
                    w2 = C["w21" if kind == "conv1" else "w22"]
                    for b in range(GB):
                        mm = nc.tensor.matmul(p1b[:, b, :], totT[:, b * P:(b + 1) * P], w2[:, :], start=True, stop=True)
                    mm.then_inc(mapped, 1)
                if soft:
                    pe.wait_ge(copied, g + 1)
                    pe.wait_ge(evacuated, g + 1)
                    for b in range(GB):
                        e = slice(b * P, (b + 1) * P)
                        nc.tensor.transpose(p1b[:, b, :], totT[:, e], ident)
                        if kind == "gat":
                            nc.tensor.transpose(p2b[:, b, :], totT_e[:, e], ident)
                        mm = nc.tensor.transpose(p_w[:, b * SMW:(b + 1) * SMW], cT[:, e], ident[0:SMW, 0:SMW])
                    mm.then_inc(turned1, 1)
                if kind == "attn":
                    pe.wait_ge(o_ready, g + 1)
                    for b in range(GB):
                        mm = nc.tensor.transpose(p2b[:, b, :], h[:, b, :], ident)
                    mm.then_inc(o_turned, 1)
                    pe.wait_ge(oT_ready, g + 1)
                    for b in range(GB):
                        mm = nc.tensor.matmul(p1b[:, b, :], totT[:, b * P:(b + 1) * P], C["wo"][:, :], start=True, stop=True)
                    mm.then_inc(mapped, 1)
                if kind != "gat":
                    pe.wait_ge(h_ready, g + 1)
                    for b in range(GB):
                        mm = nc.tensor.transpose(p2b[:, b, :], h2[:, b, :], ident)
                    mm.then_inc(turned2, 1)
                    pe.wait_ge(hT_ready, g + 1)
                    rhs = {"first": "wab1", "conv1": "wab2", "conv2": "wkv", "attn": "wsd"}[kind]
                    for b in range(GB):
                        hb = hT[:, b * P:(b + 1) * P]
                        mm = nc.tensor.matmul(pwb[:, b, :], hb, C[rhs][:, :, :].rearrange("p a f -> p (a f)"), start=True, stop=True)
                        if kind == "conv2":
                            mm = nc.tensor.matmul(p1b[:, b, :], hb, C["wq"][:, :], start=True, stop=True)
                        if kind == "attn":
                            mm = nc.tensor.matmul(p_ws[:, b, :], hb, C["wsa"][:, :], start=True, stop=True)
                    mm.then_inc(tables_ready, 1)

        @block.scalar
        def _(act):
            with act.Fori(0, NGRP) as g:
                nodes = bass.ds(g * GW, GW)
                if kind == "conv1":
                    act.wait_ge(evacuated, g + 1)
                    act.copy(cT[0:1, :], small[:, nodes]).then_inc(copied, 1)
                if soft:
                    act.wait_ge(evacuated, g + 1)
                    act.copy(totT[:, :], acc[:, nodes])
                    if kind == "gat":
                        act.copy(totT_e[:, :], acc_e[:, nodes])
                    act.copy(cT[:, :], small[:, nodes]).then_inc(copied, 1)
                    act.wait_ge(below_ready, g + 1)
                    act.activation(fa[:, :, :], fa[:, :, :], ACT.Exp)
                    act.activation(fb[:, :, :], fb[:, :, :], ACT.Exp).then_inc(ex_ready, 1)
                if kind in ("conv1", "conv2"):
                    act.wait_ge(pre_act, g + 1)
                    act.activation(h[:, :, :], h[:, :, :], ACT.Silu).then_inc(acted, 1)
                if kind == "conv2":
                    act.wait_ge(acted, g + 1)

        def vector_pass(dve, g, link):
            nodes, blks = bass.ds(g * GW, GW), bass.ds(g * GB, GB)
            hb = hres[:, blks, :]
            if LOADS:
                dve.wait_ge(loaded, (g + 1) * LOADS)
            if kind == "first":
                link(nc.vector.tensor_copy(h[:, :, :], x[:, :, :]))
                group_norm(nc, link, h, sq, mean, rstd, tmp, None, None, P)
                link(nc.vector.tensor_scalar(h2[:, :, :], h[:, :, :], 0.0, None, ALU.max))
                settle(dve, st.passed)
                link(nc.vector.tensor_copy(hb, h2[:, :, :]))
            if kind in ("conv1", "conv2"):
                l = 1 if kind == "conv1" else 2
                dve.wait_ge(turned1, g + 1)
                cg = cnt[:, :, blks]
                if kind == "conv1":
                    link(nc.vector.tensor_tensor(tmp[:, 0:GB], p2[:, 0:GB], fr[:, :, P:P + 1].rearrange("p b o -> p (b o)"), ALU.add))
                    link(nc.vector.tensor_scalar(mean[:, 0:GB], tmp[:, 0:GB], 1.0, None, ALU.max))
                    link(nc.vector.reciprocal(rstd[:, 0:GB], mean[:, 0:GB]))
                    settle(dve, st.passed)
                    link(nc.vector.tensor_copy(cg[:, 0, :], rstd[:, 0:GB]))
                    link(nc.vector.tensor_scalar(cg[:, 1, :], tmp[:, 0:GB], 1.0, None, ALU.min))
                link(nc.vector.tensor_tensor(totT[:, :], acc[:, nodes], p1[:, 0:GW], ALU.add))
                dve.sem_inc(tot_ready, 1)
                dve.wait_ge(mapped, g + 1)
                link(nc.vector.tensor_tensor(h[:, :, :], p1b, bc(cg[:, 0, :].unsqueeze(2), wide), ALU.mult))
                link(nc.vector.tensor_tensor(sq[:, :, :], bc(row(C, f"c{l}_b2").unsqueeze(1), wide),
                                             bc(cg[:, 1, :].unsqueeze(2), wide), ALU.mult))
                link(nc.vector.tensor_tensor(h[:, :, :], h[:, :, :], sq[:, :, :], ALU.add))
                group_norm(nc, link, h, sq, mean, rstd, tmp, row(C, f"n{l}_g"), row(C, f"n{l}_b"), D0)
                dve.sem_inc(pre_act, 1)
                dve.wait_ge(acted, g + 1)
                if kind == "conv1":
                    link(nc.vector.tensor_tensor(h2[:, :, :], h[:, :, :], bc(C["te"][:, :].unsqueeze(1), wide), ALU.add))
                else:
                    link(nc.vector.tensor_tensor(h2[:, :, :], h[:, :, :], hb, ALU.add))
                    settle(dve, st.passed)
                    link(nc.vector.tensor_copy(hb, h2[:, :, :]))
            if soft:
                dve.wait_ge(turned1, g + 1)
                link(nc.vector.tensor_copy(sb_small[:, :, :], p_w[:, 0:GB * SMW].rearrange("p (b s) -> p b s", s=SMW)))
                F = FW - SMW
                sa, ma = sb_small[:, :, 0:NS], sb_small[:, :, MR:SMW]
                sf, mf = fr[:, :, F:F + NS], fr[:, :, F + MR:FW]
                for s_, m_, f_ in ((sa, ma, fa), (sf, mf, fb)):
                    link(nc.vector.tensor_scalar(f_[:, :, :], s_, 0.0, -BIG, ALU.is_le, ALU.mult))
                    link(nc.vector.tensor_tensor(f_[:, :, :], f_[:, :, :], m_, ALU.add))
                link(nc.vector.tensor_tensor(M[:, :, :], fa[:, :, :], fb[:, :, :], ALU.max))
                link(nc.vector.tensor_tensor(fa[:, :, :], fa[:, :, :], M[:, :, :], ALU.subtract))
                link(nc.vector.tensor_tensor(fb[:, :, :], fb[:, :, :], M[:, :, :], ALU.subtract))
                dve.sem_inc(below_ready, 1)
                dve.wait_ge(ex_ready, g + 1)
                link(nc.vector.tensor_tensor(S[:, :, :], sa, fa[:, :, :], ALU.mult))
                link(nc.vector.tensor_tensor(M[:, :, :], sf, fb[:, :, :], ALU.mult))
                link(nc.vector.tensor_tensor(S[:, :, :], S[:, :, :], M[:, :, :], ALU.add))
                link(nc.vector.tensor_scalar(S[:, :, :], S[:, :, :], 1e-6, None, ALU.max))
                link(nc.vector.reciprocal(M[:, :, :], S[:, :, :]))
                link(nc.vector.tensor_tensor(fa[:, :, :], fa[:, :, :], M[:, :, :], ALU.mult))
                link(nc.vector.tensor_tensor(fb[:, :, :], fb[:, :, :], M[:, :, :], ALU.mult))

                def weighed(dst, psum, rows_, s0, heads, width):
                    hw = [P, GB, heads, width]
                    for d, v, f_ in ((dst, psum, fa), (sq, rows_, fb)):
                        link(nc.vector.tensor_tensor(d[:, :, :].rearrange("p b (h d) -> p b h d", d=width),
                                                     v.rearrange("p b (h d) -> p b h d", d=width),
                                                     bc(f_[:, :, s0:s0 + heads].unsqueeze(3), hw), ALU.mult))
                    link(nc.vector.tensor_tensor(dst[:, :, :], dst[:, :, :], sq[:, :, :], ALU.add))
            if kind == "attn":
                weighed(h, p1b, fr[:, :, 0:P], 0, H0, D0)
                dve.sem_inc(o_ready, 1)
                dve.wait_ge(o_turned, g + 1)
                link(nc.vector.tensor_copy(totT[:, :], p2[:, 0:GW]))
                dve.sem_inc(oT_ready, 1)
                dve.wait_ge(mapped, g + 1)
                link(nc.vector.tensor_tensor(h[:, :, :], p1b, bc(row(C, "ob").unsqueeze(1), wide), ALU.add))
                group_norm(nc, link, h, sq, mean, rstd, tmp, row(C, "an_g"), row(C, "an_b"), D0)
                link(nc.vector.tensor_tensor(h[:, :, :], h[:, :, :], hb, ALU.add))
                link(nc.vector.tensor_tensor(x[:, :, :], x[:, :, :], h[:, :, :], ALU.add))
                link(nc.vector.tensor_copy(h[:, :, :], x[:, :, :]))
                group_norm(nc, link, h, sq, mean, rstd, tmp, None, None, P)
                link(nc.vector.tensor_scalar(h2[:, :, :], h[:, :, :], 0.0, None, ALU.max))
            if kind == "gat":
                weighed(h, p1b, fr[:, :, 0:P], 0, H1, D1)
                link(nc.vector.tensor_tensor(h[:, :, :], h[:, :, :], x[:, :, :], ALU.add))
                weighed(h2, p2b, fr[:, :, P:2 * P], H1, H1, D1)
                link(nc.vector.tensor_tensor(h[:, :, :], h[:, :, :], h2[:, :, :], ALU.add))
            else:
                dve.sem_inc(h_ready, 1)
                dve.wait_ge(turned2, g + 1)
                link(nc.vector.tensor_copy(hT[:, :], p2[:, 0:GW]))
                dve.sem_inc(hT_ready, 1)
                dve.wait_ge(tables_ready, g + 1)
                if kind in ("first", "conv1"):
                    link(nc.vector.tensor_copy(made[:, :, :], pwb))
                if kind == "conv2":
                    link(nc.vector.tensor_tensor(h[:, :, :], p1b, bc(row(C, "qb").unsqueeze(1), wide), ALU.add))
                    link(nc.vector.tensor_scalar(h[:, :, :], h[:, :, :], D0 ** -0.5, None, ALU.mult))
                    link(nc.vector.tensor_tensor(made[:, :, 0:P], pwb[:, :, 0:P], bc(row(C, "kb").unsqueeze(1), wide), ALU.add))
                    link(nc.vector.tensor_tensor(made[:, :, P:2 * P], pwb[:, :, P:2 * P], bc(row(C, "vb").unsqueeze(1), wide), ALU.add))
                if kind == "attn":
                    link(nc.vector.tensor_copy(made_s[:, :, :], p_ws))
                    link(nc.vector.tensor_copy(made[:, :, 0:P], pwb[:, :, 0:P]))
                    link(nc.vector.tensor_copy(made[:, :, P:P + H1], made_s[:, :, 0:H1]))
                    link(nc.vector.tensor_tensor(x[:, :, :], x[:, :, :], pwb[:, :, P:2 * P], ALU.add))
            dve.sem_inc(evacuated, 1)
            if STORES:
                dve.wait_ge(stored, (g + 1) * STORES)

        @block.vector
        def _(dve):
            dve.sem_inc(evacuated, 1)
            LINKS = {"first": 23, "conv1": 32, "conv2": 31, "attn": 67, "gat": 23}[kind]
            with dve.Fori(0, NGRP) as g:
                link = Chain(dve, chain, g * LINKS)
                vector_pass(dve, g, link)
                assert link.n == LINKS, (kind, link.n)


def build(nc, w, out):
    with ExitStack() as ctx:
        def sb(name, shape, dt=F32):
            return ctx.enter_context(nc.sbuf_tensor(name, shape, dt))

        def dram(name, shape, dt=F32):
            return nc.dram_tensor(name, shape, dt, kind="Internal").ap()

        D = {"cols": dram("cols", (NB, P, 2 * BT)), "places": dram("places", (NB, BE), BF16),
             "mask": dram("mask", (T * NS, P + 1)),
             "a1": dram("a1", (NW, P)), "b1": dram("b1", (NP, P)), "a2": dram("a2", (NW, P)), "b2": dram("b2", (NP, P)),
             "base": dram("base", (NP, P)), "q": dram("q", (NW, P)), "kv": dram("kv", (NP, 2 * P)), "g": dram("g", (NP, P + H1)), "ed": dram("ed", (NW, NS))}
        for name, width in FOLDED.items():
            D[name] = dram(name, (NP, width))
        C = {"ident": sb("ident", [P, P]), "ones": sb("ones", [P, P]), "iota_row": sb("iota_row", [P, P], BF16),
             "iota_col": sb("iota_col", [P, 1]), "fold_row": sb("fold_row", [P, TC], I32),
             "expand": sb("expand", [P, 3, P]), "te": sb("te", [P, P]), "rows": sb("rows", [P, len(ROWS), P]),
             "wq": sb("wq", [P, P]), "wkv": sb("wkv", [P, 2, P]), "wo": sb("wo", [P, P]), "we": sb("we", [ED + 1, H0]),
             "wsd": sb("wsd", [P, 2, P]), "wet": sb("wet", [P, P]), "wsa": sb("wsa", [P, 3 * H1]), "wea": sb("wea", [P, H1])}
        for l in (1, 2):
            C[f"wab{l}"], C[f"wc{l}"], C[f"w2{l}"] = sb(f"wab{l}", [P, 2, P]), sb(f"wc{l}", [ED + 1, P]), sb(f"w2{l}", [P, P])
        res = sb("res", [P, NW])
        hres = res[:, 0:NP].rearrange("p (b f) -> p b f", f=P)
        cnt = sb("cnt", [P, 2, NBLK])

        prepare(nc, w, C, D)
        node_stage(nc, "first", w, C, D, hres, cnt, None, None, None, out)
        with nc.sbuf_tensor("acc1", [P, NW], F32) as acc, nc.sbuf_tensor("first1", [P, TP], F32) as first:
            with nc.sbuf_tensor("count", [1, NW], F32) as count, nc.sbuf_tensor("first_count", [1, TP], F32) as first_count:
                conv_edges(nc, 1, w, C, D, acc, first, count, first_count)
                fold(nc, "fold1", w, C, D["fold1"], first, None, first_count, None)
                node_stage(nc, "conv1", w, C, D, hres, cnt, acc, None, count, out)
            conv_edges(nc, 2, w, C, D, acc, first, None, None)
            fold(nc, "fold2", w, C, D["fold2"], first, None, None, None)
            node_stage(nc, "conv2", w, C, D, hres, cnt, acc, None, None, out)
        with nc.sbuf_tensor("acc2", [P, NW], F32) as acc, nc.sbuf_tensor("first2", [P, TP], F32) as first, \
                nc.sbuf_tensor("small", [SMW, NW], F32) as small, nc.sbuf_tensor("first_small", [SMW, TP], F32) as first_small:
            attention_edges(nc, False, w, C, D, acc, first, None, None, small, first_small)
            fold(nc, "fold3", w, C, D["fold3"], first, None, first_small, [0])
            node_stage(nc, "attn", w, C, D, hres, cnt, acc, None, small, out)
            acc_e = res
            with nc.sbuf_tensor("first_e", [P, TP], F32) as first_e:
                attention_edges(nc, True, w, C, D, acc, first, acc_e, first_e, small, first_small)
                fold(nc, "fold4", w, C, D["fold4"], first, first_e, first_small, [1, 2])
                node_stage(nc, "gat", w, C, D, hres, cnt, acc, acc_e, small, out)


def kernel(**inputs):
    import concourse.bacc as bacc
    from concourse.bass_utils import run_bass_kernel_spmd

    src, dst = np.asarray(inputs["src"]), np.asarray(inputs["dst"])
    pad = EP - E
    src = np.concatenate([src, np.zeros(pad, np.int32)])
    dst = np.concatenate([dst, np.full(pad, N, np.int32)])
    n0 = np.concatenate([dst[::P], np.full(TP - T + 1, N, np.int32)])
    arrays = {
        "x": np.concatenate([np.asarray(inputs["x"]), np.zeros((NP - N, P), np.float32)]),
        "src_b": src.reshape(NB, BT, P).transpose(0, 2, 1),
        "dst_b": dst.reshape(NB, BT, P).transpose(0, 2, 1).reshape(NB, BE),
        "dst_r": dst.reshape(NB, BE),
        "n0_b": n0[:T].reshape(NB, BT),
        "n0_p": n0[:TP].reshape(1, TP),
        "n0_c": n0[:TP].reshape(TC, P).T,
        "n0_next": n0[1:].reshape(TC, P).T,
        "ea": np.concatenate([np.concatenate([np.asarray(inputs["edge_attr_4"]), np.zeros((pad, ED), np.float32)]).T,
                              np.ones((1, EP), np.float32)]),
        "xeT": np.concatenate([np.asarray(inputs["edge_attr_128"]), np.zeros((pad, P), np.float32)]).T,
    }
    for name, a in inputs.items():
        if name.startswith(("L0_gnn_", "L1_gnn_")):
            arrays[name[7:]] = np.asarray(a)
    nc = bacc.Bacc("TRN2", target_bir_lowering=False, num_devices=1)
    feeds, w = {}, {}
    for name, a in arrays.items():
        a = np.ascontiguousarray(a)
        feeds["in_" + name] = a
        w[name] = nc.dram_tensor("in_" + name, a.shape, mybir.dt.from_np(a.dtype), kind="ExternalInput").ap()
    out = nc.dram_tensor("out", (NP, P), F32, kind="ExternalOutput").ap()
    build(nc, w, out)
    result = run_bass_kernel_spmd(nc, [feeds], core_ids=[0])
    return result.results[0]["out"][:N]
```

```python
import numpy as np
from contextlib import ExitStack

import concourse.bass as bass
from concourse import mybir

F32, BF16, I32 = mybir.dt.float32, mybir.dt.bfloat16, mybir.dt.int32
ALU, ACT, AX = mybir.AluOpType, mybir.ActivationFunctionType, mybir.AxisListType
ACT_ENGINE, SP_ENGINE = mybir.EngineType.Activation, mybir.EngineType.SP

P = 128
N = 6250
E = 206250
NBLK = -(-N // P)
NP = NBLK * P
NW = NP + P
GB = 7
NGRP = NBLK // GB
GW = GB * P
QT = 4
BT = 16
BQ = BT // QT
QE, BE = QT * P, BT * P
NB = -(-E // BE)
T = NB * BT
EP = T * P
FR = -(-NP // NB)
RB = 3
BODY = (NB - 2) // RB
assert NBLK % GB == 0 and NGRP % 2 == 1 and BODY * RB + 2 == NB
TC = -(-T // P)
TP = TC * P
ED = 4
H0, D0 = 8, 16
H1, D1 = 4, 32
NS = 8
MR = 32
SMW = MR + NS
EPS = 1e-5
BIG = 1e30
SKIP = 1e6
MAGIC = float(0x5F3759DF)
HEAD = 64


class Batch:

    def __init__(self, q, c):
        self.q, self.c = q, c
        self.i = q * RB + c

    def next(self):
        return Batch(self.q, self.c + 1) if self.c + 1 < RB else Batch(self.q + 1, 0)

    def quad(self, k):
        return self.i * BQ + k


def done(eng, sem, n):
    if not isinstance(n, int) or n > 0:
        eng.wait_ge(sem, n + HEAD)


def settle(eng, passed):
    eng.sem_inc(passed, 1)


def run_batches(eng, step):
    with eng.Fori(0, BODY) as j:
        for c in range(RB):
            b = Batch(j, c)
            step(b, b.next(), b.next().next())
    step(Batch(BODY, 0), Batch(BODY, 1), None)
    step(Batch(BODY, 1), None, None)


def run_groups(eng, step):
    with eng.Fori(0, NGRP // 2) as j:
        step(j * 2, 0, j, j * 2 + 1)
        step(j * 2 + 1, 1, j, j * 2 + 2)
    step(NGRP - 1, 0, NGRP // 2, None)


class Chain:

    def __init__(self, eng, sem, base=0):
        self.eng, self.sem, self.base, self.n = eng, sem, base, 0

    def __call__(self, ins):
        self.n += 1
        ins.then_inc(self.sem, 1)
        self.eng.wait_ge(self.sem, self.base + self.n)


def bc(ap, shape):
    return ap.to_broadcast(shape)


def rsqrt(nc, link, x, y, a):
    yi, xi = y.bitcast(I32), x.bitcast(I32)
    link(nc.vector.tensor_scalar(yi, xi, 1, None, ALU.logical_shift_right))
    link(nc.vector.tensor_scalar(yi, yi, -1.0, MAGIC, ALU.mult, ALU.add))
    for _ in range(3):
        link(nc.vector.tensor_tensor(a, y, y, ALU.mult))
        link(nc.vector.scalar_tensor_tensor(a, a, -0.5, x, ALU.mult, ALU.mult))
        link(nc.vector.scalar_tensor_tensor(y, a, 1.5, y, ALU.add, ALU.mult))


def group_norm(nc, link, h, sq, mean, rstd, tmp, gamma, beta, width):
    G = GW // width
    h, sq = h[:, :, :], sq[:, :, :]
    mean, rstd, tmp = mean[:, 0:G], rstd[:, 0:G], tmp[:, 0:G]
    hg, sg = (v.rearrange("p b (g w) -> p (b g) w", w=width) for v in (h, sq))
    wide = [P, G, width]
    if gamma is None:
        link(nc.vector.tensor_reduce(mean, hg, AX.X, ALU.add))
        link(nc.vector.tensor_scalar(mean, mean, 1.0 / width, None, ALU.mult))
        link(nc.vector.tensor_tensor(hg, hg, bc(mean.unsqueeze(2), wide), ALU.subtract))
    link(nc.vector.tensor_tensor(sq, h, h, ALU.mult))
    link(nc.vector.tensor_reduce(mean, sg, AX.X, ALU.add))
    link(nc.vector.tensor_scalar(mean, mean, 1.0 / width, EPS, ALU.mult, ALU.add))
    rsqrt(nc, link, mean, rstd, tmp)
    link(nc.vector.tensor_tensor(hg, hg, bc(rstd.unsqueeze(2), wide), ALU.mult))
    if gamma is not None:
        link(nc.vector.tensor_tensor(h, h, bc(gamma.unsqueeze(1), [P, GB, P]), ALU.mult))
        link(nc.vector.tensor_tensor(h, h, bc(beta.unsqueeze(1), [P, GB, P]), ALU.add))


class Stage:

    def __init__(self, nc, name):
        self.nc, self.name, self.ctx, self.sems = nc, name, ExitStack(), []
        self.passed = self.sem("passed")

    def __enter__(self):
        return self

    def __exit__(self, *exc):
        self.ctx.close()
        if exc[0] is None:
            self.nc.clear_and_free_semaphores(self.sems)
            self.nc.all_engine_barrier()

    def sb(self, name, shape, dt=F32):
        return self.ctx.enter_context(self.nc.sbuf_tensor(f"{self.name}_{name}", shape, dt))

    def ps(self, name, shape):
        return self.ctx.enter_context(self.nc.psum_tensor(f"{self.name}_{name}", shape, F32))

    def sem(self, name):
        s = self.nc.alloc_semaphore(f"{self.name}_{name}")
        self.sems.append(s)
        return s


def prepare(nc, w, C, D):
    with Stage(nc, "prep") as st:
        dst_b = st.sb("dst_b", [NB, P * BT], I32)
        dst_r = st.sb("dst_r", [NB, BE], I32)
        n0_b = st.sb("n0_b", [NB, BT], I32)
        rel_c = st.sb("rel_c", [NB, 2, P * BT])
        rel_f = st.sb("rel_f", [NB, BE])
        rel_h = st.sb("rel_h", [NB, BE], BF16)
        mask = st.sb("mask", [NB, BT, P + 1])
        iota_i = st.sb("iota_i", [P, P], I32)
        iota_pi = st.sb("iota_pi", [P, 1], I32)
        sc_i = st.sb("sc_i", [P, 2, TC], I32)
        sc_f = st.sb("sc_f", [P, 2, TC])
        zero = st.sb("zero", [P, P])
        temb = st.sb("temb", [P, 4])
        tmw = st.sb("tmw", [P, 4, P])
        tmb = st.sb("tmb", [1, P])
        te_row = st.sb("te_row", [1, P])
        mean = st.sb("mean", [P, 16])
        wg = st.sb("wg", [P, 3, P])
        attn = st.sb("attn", [P, 3])
        head = st.sb("head", [P, H1])
        abd = st.sb("abd", [P, 3, H1])
        p_te, p_teb = st.ps("p_te", [P, 512]), st.ps("p_teb", [P, 512])
        p_w = st.ps("p_w", [P, 512])
        p_a = st.ps("p_a", [P, 512])
        loaded, stored = st.sem("loaded"), st.sem("stored")
        pool_made, dve_made, chain = st.sem("pool_made"), st.sem("dve_made"), st.sem("chain")
        temb_ready, te_ready, teb_ready = st.sem("temb_ready"), st.sem("te_ready"), st.sem("teb_ready")
        wt_ready = st.sem("wt_ready")

        loads = [(dst_b[:, :], w["dst_b"]), (dst_r[:, :], w["dst_r"]), (n0_b[:, :], w["n0_b"]),
                 (sc_i[:, 0, :], w["n0_c"]), (sc_i[:, 1, :], w["n0_next"]),
                 (temb[:, :], w["t_emb"].rearrange("(p c) -> p c", p=P)),
                 (tmw[:, :, :], w["tm_w"].rearrange("(p c) f -> p c f", p=P)),
                 (tmb[:, :], w["tm_b"].unsqueeze(0))]
        for l in (1, 2):
            loads += [(C[f"wab{l}"][:, 0, :], w[f"c{l}_w1"][0:P, :]), (C[f"wab{l}"][:, 1, :], w[f"c{l}_w1"][P:2 * P, :]),
                      (C[f"wc{l}"][0:ED, :], w[f"c{l}_w1"][2 * P:2 * P + ED, :]),
                      (C[f"wc{l}"][ED:ED + 1, :], w[f"c{l}_b1"].unsqueeze(0)), (C[f"w2{l}"][:, :], w[f"c{l}_w2"])]
        loads += [(C["wq"][:, :], w["qw"]), (C["wkv"][:, 0, :], w["kw"]), (C["wkv"][:, 1, :], w["vw"]),
                  (C["wo"][:, :], w["ow"]), (C["we"][0:ED, :], w["ew"]), (C["we"][ED:ED + 1, :], w["eb"].unsqueeze(0))]
        for n in ROWS:
            loads.append((C["rows"][:, ROWS.index(n), :], w[n].unsqueeze(0).to_broadcast([P, P])))
        for n, s in enumerate(("src", "dst", "edge")):
            loads += [(wg[:, n, :], w["W_" + s]),
                      (attn[:, n:n + 1], w["attn_" + s].rearrange("h d -> (h d)").unsqueeze(1))]

        block = st.ctx.enter_context(nc.Block())

        @block.sync
        def _(sp):
            for dst, src in loads:
                sp.dma_start(dst, src).then_inc(loaded, 16)
            sp.wait_ge(pool_made, 3)
            for name in ("a1", "a2", "q"):
                sp.dma_start(D[name][NP:NW, :], zero[:, 0:P]).then_inc(stored, 16)
            sp.dma_start(D["ed"][NP:NW, :], zero[:, 0:NS]).then_inc(stored, 16)
            sp.wait_ge(dve_made, 1)
            sp.dma_start(D["cols"].rearrange("b p (a t) -> b a p t", a=2)[:, 0, :, :],
                         rel_c[:, 0, :].rearrange("b (p t) -> b p t", t=BT)).then_inc(stored, 16)
            sp.dma_start(D["cols"].rearrange("b p (a t) -> b a p t", a=2)[:, 1, :, :],
                         rel_c[:, 1, :].rearrange("b (p t) -> b p t", t=BT)).then_inc(stored, 16)
            sp.dma_start(D["places"], rel_h[:, :]).then_inc(stored, 16)
            m = D["mask"].rearrange("(b t h) e -> b t h e", t=BT, h=NS)
            for h in range(NS):
                sp.dma_start(m[:, :, h, :], mask[:, :, :]).then_inc(stored, 16)
            sp.wait_ge(stored, 16 * (4 + 3 + NS))

        @block.gpsimd
        def _(pool):
            pool.memset(C["ident"][:, :], 0.0).then_inc(pool_made, 1)
            pool.memset(head[:, :], 1.0).then_inc(pool_made, 1)
            pool.memset(zero[:, :], 0.0).then_inc(pool_made, 1)
            pool.memset(C["expand"][:, :, :], 1.0).then_inc(pool_made, 1)
            pool.iota(iota_i[:, :], pattern=[[1, P]], base=0, channel_multiplier=0).then_inc(pool_made, 1)
            pool.iota(iota_pi[:, :], pattern=[[1, 1]], base=0, channel_multiplier=1).then_inc(pool_made, 1)
            pool.wait_ge(pool_made, 6)
            pool.affine_select(out=C["ident"][:, :], in_=C["ident"][:, :], compare_op=ALU.not_equal, fill=1.0,
                               base=0, pattern=[[-1, P]], channel_multiplier=1).then_inc(pool_made, 1)
            pool.affine_select(out=head[:, :], in_=head[:, :], compare_op=ALU.is_ge, fill=0.0,
                               base=0, pattern=[[-D1, H1]], channel_multiplier=1).then_inc(pool_made, 1)
            for n, (first, width) in enumerate(((0, D0), (0, D1), (H1, D1))):
                e = C["expand"][:, n, :]
                pool.affine_select(out=e, in_=e, compare_op=ALU.is_ge, fill=0.0, base=width * (MR + first),
                                   pattern=[[1, P]], channel_multiplier=-width).then_inc(pool_made, 1)
            pool.wait_ge(pool_made, 11)
            pool.affine_select(out=head[:, :], in_=head[:, :], compare_op=ALU.is_ge, fill=0.0,
                               base=D1 - 1, pattern=[[D1, H1]], channel_multiplier=-1).then_inc(pool_made, 1)
            for n, (first, width) in enumerate(((0, D0), (0, D1), (H1, D1))):
                e = C["expand"][:, n, :]
                pool.affine_select(out=e, in_=e, compare_op=ALU.is_ge, fill=0.0, base=width - 1 - width * (MR + first),
                                   pattern=[[-1, P]], channel_multiplier=width).then_inc(pool_made, 1)

        @block.scalar
        def _(act):
            act.wait_ge(loaded, 16 * len(loads))
            act.activation(temb[:, :], temb[:, :], ACT.Silu).then_inc(temb_ready, 1)

        @block.tensor
        def _(pe):
            pe.wait_ge(loaded, 16 * len(loads))
            pe.wait_ge(temb_ready, 1)
            for c in range(4):
                mm = nc.tensor.matmul(p_te[0:1, 0:P], temb[:, c:c + 1], tmw[:, c, :], start=c == 0, stop=c == 3)
            mm.then_inc(te_ready, 1)
            pe.wait_ge(dve_made, 2)
            pe.wait_ge(pool_made, 15)
            nc.tensor.matmul(p_teb[:, 0:P], C["ones"][0:1, :], te_row[:, :], start=True, stop=True).then_inc(teb_ready, 1)
            for n in range(3):
                nc.tensor.transpose(p_w[:, n * P:(n + 1) * P], wg[:, n, :], C["ident"][:, :])
                mm = nc.tensor.matmul(p_a[:, n * H1:(n + 1) * H1], wg[:, n, :], abd[:, n, :], start=True, stop=True)
            mm.then_inc(wt_ready, 1)

        @block.vector
        def _(dve):
            link = Chain(dve, chain)
            dve.wait_ge(pool_made, 6)
            dve.wait_ge(loaded, 16 * len(loads))
            link(nc.vector.tensor_copy(C["iota_row"][:, :], iota_i[:, :]))
            link(nc.vector.tensor_copy(C["iota_col"][:, :], iota_pi[:, :]))
            link(nc.vector.memset(C["ones"][:, :], 1.0))
            link(nc.vector.memset(C["ones_b"][:, :], 1.0))
            n0_e = n0_b[:, :].unsqueeze(1)
            link(nc.vector.tensor_tensor(rel_c[:, 0, :].rearrange("b (p t) -> b p t", t=BT),
                                         dst_b[:, :].rearrange("b (p t) -> b p t", t=BT),
                                         bc(n0_e, [NB, P, BT]), ALU.subtract))
            rel_t = rel_f[:, :].rearrange("b (t e) -> b t e", e=P)
            link(nc.vector.tensor_tensor(rel_t, dst_r[:, :].rearrange("b (t e) -> b t e", e=P),
                                         bc(n0_b[:, :].unsqueeze(2), [NB, BT, P]), ALU.subtract))
            link(nc.vector.tensor_copy(rel_h[:, :], rel_f[:, :]))
            link(nc.vector.memset(rel_c[:, 1, 0:BT], 1.0))
            link(nc.vector.tensor_tensor(rel_c[:, 1, BT:], rel_c[:, 0, BT:], rel_c[:, 0, 0:BE - BT], ALU.not_equal))
            link(nc.vector.memset(mask[:, :, :], -BIG))
            link(nc.vector.tensor_tensor(mask[:, :, 1:P], rel_t[:, :, 1:P], rel_t[:, :, 0:P - 1], ALU.not_equal))
            link(nc.vector.tensor_scalar(mask[:, :, 1:P], mask[:, :, 1:P], -BIG, None, ALU.mult))
            dve.sem_inc(dve_made, 1)
            link(nc.vector.tensor_copy(sc_f[:, :, :], sc_i[:, :, :]))
            link(nc.vector.tensor_tensor(sc_f[:, 1, :], sc_f[:, 0, :], sc_f[:, 1, :], ALU.is_equal))
            link(nc.vector.scalar_tensor_tensor(C["fold_row"][:, :], sc_f[:, 1, :], SKIP, sc_f[:, 0, :], ALU.mult, ALU.add))
            centred = [(row(C, "ob"), P, 1), (C["wo"][:, :], P, 1)]
            for l in (1, 2):
                centred += [(C[f"wab{l}"][:, :, :].rearrange("p a f -> p (a f)"), P, 2), (C[f"wc{l}"][:, :], ED + 1, 1),
                            (C[f"w2{l}"][:, :], P, 1), (row(C, f"c{l}_b2"), P, 1)]
            for t, rows, n in centred:
                v = t.rearrange("p (g w) -> p g w", w=D0)
                link(nc.vector.tensor_reduce(mean[0:rows, 0:n * H0], v, AX.X, ALU.add))
                link(nc.vector.tensor_scalar(mean[0:rows, 0:n * H0], mean[0:rows, 0:n * H0], 1.0 / D0, None, ALU.mult))
                link(nc.vector.tensor_tensor(v, v, bc(mean[0:rows, 0:n * H0].unsqueeze(2), [rows, n * H0, D0]), ALU.subtract))
            dve.wait_ge(te_ready, 1)
            link(nc.vector.tensor_tensor(te_row[:, :], p_te[0:1, 0:P], tmb[:, :], ALU.add))
            dve.wait_ge(pool_made, 15)
            for n in range(3):
                link(nc.vector.tensor_scalar(abd[:, n, :], head[:, :], attn[:, n:n + 1], None, ALU.mult))
            dve.sem_inc(dve_made, 1)
            dve.wait_ge(teb_ready, 1)
            link(nc.vector.tensor_copy(C["te"][:, :], p_teb[:, 0:P]))
            dve.wait_ge(wt_ready, 1)
            link(nc.vector.tensor_copy(C["wsd"][:, :, :], p_w[:, 0:2 * P].rearrange("p (a f) -> p a f", a=2)))
            link(nc.vector.tensor_copy(C["weta"][:, 0:P], p_w[:, 2 * P:3 * P]))
            link(nc.vector.memset(C["weta"][:, P:P + H1], 0.0))
            link(nc.vector.tensor_copy(C["wsa"][:, 0:2 * H1], p_a[:, 0:2 * H1]))
            link(nc.vector.tensor_copy(C["wsa"][:, 2 * H1:3 * H1], p_a[:, H1:2 * H1]))
            link(nc.vector.tensor_copy(C["weta"][:, P + H1:P + NS], p_a[:, 2 * H1:3 * H1]))


ROWS = ["c1_g", "c1_bt", "c1_b2", "n1_g", "n1_b", "c2_g", "c2_bt", "c2_b2", "n2_g", "n2_b", "qb", "kb", "vb",
        "ob", "an_g", "an_b"]
FOLDED = {"fold1": P + 1, "fold2": P, "fold3": P + SMW, "fold4": 2 * P + SMW}


def row(C, name):
    return C["rows"][:, ROWS.index(name), :]


def conv_edges(nc, l, w, C, D, acc, first, count, first_count):
    a_table, b_table = D[f"a{l}"], D[f"b{l}"]
    gamma, beta, wc = row(C, f"c{l}_g"), row(C, f"c{l}_bt"), C[f"wc{l}"]
    GQ, WQ, PQ = RB * BQ, 4, 6
    ZQ, SQ = 6, 1 if l == 1 else 2
    with Stage(nc, f"conv{l}") as st:
        idx = st.sb("idx", [P, RB, BT], I32)
        cols = st.sb("cols", [P, RB, 2 * BT])
        starts_in = st.sb("starts_in", [1, RB, BT], I32)
        n0 = st.sb("n0", [1, RB, BT], I32)
        gath = st.sb("gath", [P, GQ, QT, P])
        win = st.sb("win", [P, WQ, QT, P])
        ea = st.sb("ea", [ED + 1, RB, BE])
        places = st.sb("places", [P, RB, BE], BF16)
        hotT = st.sb("hotT", [P, PQ, QE])
        hot = st.sb("hot", [P, BQ, QT, P])
        sq = st.sb("sq", [P, 2, QE])
        var, tmp = st.sb("var", [P, BT * H0]), st.sb("tmp", [P, BT * H0])
        rstd = st.sb("rstd", [P, RB, BT * H0])
        u = st.sb("u", [P, 2, QE])
        m = st.sb("m", [P, BQ, QE])
        z = [st.ps(f"z{n}", [P, QE]) for n in range(ZQ)]
        sums = [st.ps(f"sums{n}", [P, QE]) for n in range(SQ)]
        counts = st.ps("counts", [P, QE]) if l == 1 else None
        hot_b = st.sb("hot_b", [P, 2, QE], BF16) if l == 1 else None

        meta_landed = [st.sem(f"meta_landed{c}") for c in range(RB)]
        gath_landed = [st.sem(f"gath_landed{n}") for n in range(GQ)]
        win_landed = [st.sem(f"win_landed{n}") for n in range(WQ)]
        starts_landed = [st.sem(f"starts_landed{c}") for c in range(RB)]
        hotT_ready, hot_ready, var_ready, normed, u_ready = (
            st.sem(n) for n in ("hotT_ready", "hot_ready", "var_ready", "normed", "u_ready"))
        scaled, newton = st.sem("scaled"), st.sem("newton")
        z_ready, sums_ready, counts_ready = st.sem("z_ready"), st.sem("sums_ready"), st.sem("counts_ready")
        hot_b_ready = st.sem("hot_b_ready")
        sq_ready, m_ready, sums_copied, sums_freed, counts_copied, counts_freed = (
            st.sem(n) for n in ("sq_ready", "m_ready", "sums_copied", "sums_freed", "counts_copied", "counts_freed"))
        cleared, zeroed, filled = st.sem("cleared"), st.sem("zeroed"), st.sem("filled")
        fold_table = D[f"fold{l}"]
        zero = st.sb("zero", [FR, fold_table.shape[1]])
        META = 5 * 16
        NEWTON = 12
        block = st.ctx.enter_context(nc.Block())

        @block.sync
        def _(sp):
            def fetch_starts(b):
                sp.dma_start(starts_in[:, b.c, :], w["n0_b"][bass.ds(b.i, 1), :]).then_inc(starts_landed[b.c], 16)

            def fetch(b, nxt, _):
                if nxt:
                    fetch_starts(nxt)
                done(sp, z_ready, (b.i - RB + 1) * BQ)
                done(sp, hot_ready, (b.i - RB + 1) * BQ)
                done(sp, sums_copied, (b.i - RB) * BT + 1)
                settle(sp, st.passed)
                for dst, src in ((idx[:, b.c, :], w["src_b"][bass.ds(b.i, 1), :, :].rearrange("a p t -> (a p) t")),
                                 (places[:, b.c, :], D["places"][bass.ds(b.i, 1), :].to_broadcast([P, BE])),
                                 (cols[:, b.c, :], D["cols"][bass.ds(b.i, 1), :, :].rearrange("a p t -> (a p) t")),
                                 (ea[:, b.c, :], w["ea"][:, bass.ds(b.i * BE, BE)]),
                                 (n0[:, b.c, :], w["n0_b"][bass.ds(b.i, 1), :])):
                    sp.dma_start(dst, src).then_inc(meta_landed[b.c], 16)
                sp.wait_ge(starts_landed[b.c], (b.q + 1) * 16)
                settle(sp, st.passed)
                _, starts = nc.values_load_multi_w_load_instructions(
                    starts_in[0:1, b.c, :], engines=(SP_ENGINE,), min_val=0, max_val=N,
                    skip_runtime_bounds_check_because="destinations are node numbers")
                for k in range(BQ):
                    done(sp, z_ready, b.quad(k) - WQ + 1)
                    settle(sp, st.passed)
                    for t in range(QT):
                        sp.dma_start(win[:, k, t, :], a_table[bass.ds(starts[k * QT + t], P), :])\
                          .then_inc(win_landed[k], 16)
                sp.dma_start(fold_table[bass.ds(b.i * FR, FR), :], zero[:, :]).then_inc(filled, 16)
            fetch_starts(Batch(0, 0))
            sp.wait_ge(zeroed, 1)
            run_batches(sp, fetch)
            sp.wait_ge(filled, NB * 16)

        @block.gpsimd
        def _(pool):
            def gather(b, *_):
                pool.wait_ge(meta_landed[b.c], (b.q + 1) * META)
                for k in range(BQ):
                    done(pool, z_ready, b.quad(k) - GQ + 1)
                    settle(pool, st.passed)
                    for t in range(QT):
                        pool.indirect_dma_start(
                            gath[:, b.c * BQ + k, t, :], None, b_table,
                            bass.IndirectOffsetOnAxis(ap=idx[:, b.c, k * QT + t:k * QT + t + 1], axis=0))\
                            .then_inc(gath_landed[b.c * BQ + k], 16)
            run_batches(pool, gather)

        @block.tensor
        def _(pe):
            pe.sem_inc(z_ready, HEAD)
            pe.sem_inc(sums_ready, HEAD)
            pe.sem_inc(counts_ready, HEAD)

            def pre_activation(b, k):
                s6, s4, s12 = (b.c * BQ + k) % PQ, k, b.c * BQ + k
                zb = z[s12 % ZQ]
                pe.wait_ge(gath_landed[s12], (b.q + 1) * QT * 16)
                done(pe, normed, b.quad(k) - ZQ + 1)
                nc.tensor.matmul(zb[:, :], C["ident"][:, :], gath[:, s12, :, :].rearrange("p t f -> p (t f)"),
                                 start=True, stop=False, skip_group_check=True)
                pe.wait_ge(win_landed[s4], (b.i + 1) * QT * 16)
                pe.wait_ge(meta_landed[b.c], (b.q + 1) * META)
                done(pe, hotT_ready, b.quad(k) + 1)
                for t in range(QT):
                    zt = zb[:, t * P:(t + 1) * P]
                    nc.tensor.matmul(zt, hotT[:, s6, t * P:(t + 1) * P], win[:, s4, t, :], start=False, stop=False,
                                     skip_group_check=True)
                    mm = nc.tensor.matmul(zt, ea[:, b.c, k * QE + t * P:k * QE + (t + 1) * P], wc[:, :], start=False, stop=t == QT - 1,
                                          skip_group_check=True)
                mm.then_inc(z_ready, 1)

            def sum_up(b, k):
                so, g = k % SQ, b.quad(k)
                done(pe, hot_ready, g + 1)
                if l == 1:
                    done(pe, counts_freed, g)
                    done(pe, hot_b_ready, g + 1)
                    nc.tensor.matmul(counts[0:1, :], C["ones_b"][:, :], hot_b[:, k % 2, :], start=True, stop=True)\
                      .then_inc(counts_ready, 1)
                done(pe, m_ready, g + 1)
                done(pe, sums_freed, g - SQ + 1)
                for t in range(QT):
                    mm = nc.tensor.matmul(sums[so][:, t * P:(t + 1) * P], m[:, k, t * P:(t + 1) * P], hot[:, k, t, :],
                                          start=True, stop=True)
                mm.then_inc(sums_ready, 1)

            def step(b, nxt, after):
                if nxt:
                    pre_activation(nxt, 1)
                    pre_activation(nxt, 2)
                sum_up(b, 0)
                if nxt:
                    pre_activation(nxt, 3)
                sum_up(b, 1)
                if after:
                    pre_activation(after, 0)
                sum_up(b, 2)
                sum_up(b, 3)
            for k in range(BQ):
                pre_activation(Batch(0, 0), k)
            pre_activation(Batch(0, 1), 0)
            run_batches(pe, step)

        @block.scalar
        def _(act):
            for s in (hot_b_ready, sq_ready, m_ready, sums_copied, sums_freed, counts_copied, counts_freed):
                act.sem_inc(s, HEAD)

            def square(b, k):
                g, s2 = b.quad(k), k % 2
                done(act, z_ready, g + 1)
                done(act, var_ready, g - 2 + 1)
                act.activation(sq[:, s2, :], z[(b.c * BQ + k) % ZQ][:, :], ACT.Square, scale=D0 ** -0.5).then_inc(sq_ready, 1)

            def copies(b, k, starts):
                g, so = b.quad(k), k % SQ
                outs = [(count, first_count, counts[0:1, :], counts_ready, counts_copied, counts_freed)] if l == 1 else []
                outs.append((acc, first, sums[so][:, :], sums_ready, sums_copied, sums_freed))
                for *_, ready, _, _ in outs:
                    done(act, ready, g + 1)
                for t in range(QT):
                    for kept, _, new, _, copied, _ in outs:
                        done(act, copied, g * QT + t)
                        act.copy(kept[:, bass.ds(starts[k * QT + t] + 1, P - 1)], new[:, t * P + 1:(t + 1) * P])\
                           .then_inc(copied, 1)
                for _, kept_first, new, _, _, freed in outs:
                    act.copy(kept_first[:, bass.ds(g * QT, QT)], new.rearrange("p (t n) -> p t n", n=P)[:, :, 0])\
                       .then_inc(freed, 1)

            def step(b, nxt, after):
                act.wait_ge(meta_landed[b.c], (b.q + 1) * META)
                settle(act, st.passed)
                _, starts = nc.values_load_multi_w_load_instructions(
                    n0[0:1, b.c, :], engines=(ACT_ENGINE,), min_val=0, max_val=N,
                    skip_runtime_bounds_check_because="destinations are node numbers")
                for k in range(BQ):
                    g = b.quad(k)
                    if l == 1:
                        done(act, hot_ready, g + 1)
                        done(act, counts_ready, g - 2 + 1)
                        act.copy(hot_b[:, k % 2, :], hot[:, k, :, :].rearrange("p t n -> p (t n)")).then_inc(hot_b_ready, 1)
                    done(act, u_ready, g + 1)
                    done(act, sums_ready, g - BQ + 1)
                    act.activation(m[:, k, :], u[:, k % 2, :], ACT.Silu).then_inc(m_ready, 1)
                    if nxt and k + 1 < BQ:
                        square(nxt, k + 1)
                    elif after:
                        square(after, 0)
                    if k > 0:
                        copies(b, k - 1, starts)
                copies(b, BQ - 1, starts)
            act.wait_ge(cleared, 1)
            for k in range(BQ):
                square(Batch(0, 0), k)
            square(Batch(0, 1), 0)
            run_batches(act, step)

        @block.vector
        def _(dve):
            for s in (hotT_ready, hot_ready, var_ready, normed, scaled, u_ready, newton):
                dve.sem_inc(s, HEAD)
            nc.vector.memset(zero[:, :], 0.0).then_inc(zeroed, 1)
            nc.vector.memset(first[:, :], 0.0)
            if l == 1:
                nc.vector.memset(count[:, :], 0.0)
                nc.vector.memset(first_count[:, :], 0.0)
            nc.vector.memset(acc[:, :], 0.0).then_inc(cleared, 1)

            def one_hot_T(b, k):
                s6 = (b.c * BQ + k) % PQ
                dve.wait_ge(meta_landed[b.c], (b.q + 1) * META)
                done(dve, z_ready, b.quad(k) - PQ + 1)
                nc.vector.tensor_scalar(hotT[:, s6, :], places[:, b.c, k * QE:(k + 1) * QE], C["iota_col"][:, 0:1], None, ALU.is_equal)\
                  .then_inc(hotT_ready, 1)

            def variance(b, k):
                done(dve, sq_ready, b.quad(k) + 1)
                if k == 0:
                    done(dve, newton, b.i * NEWTON)
                nc.vector.tensor_reduce(var[:, k * QT * H0:(k + 1) * QT * H0],
                                        sq[:, k % 2, :].rearrange("p (g w) -> p g w", w=D0), AX.X, ALU.add)\
                  .then_inc(var_ready, 1)

            def inverse_std(b, first_link, last_link):
                y = rstd[:, b.c, :]
                yi, xi = y.bitcast(I32), var[:, :].bitcast(I32)
                for n in range(first_link, last_link):
                    if n == 0:
                        done(dve, var_ready, b.quad(BQ))
                        done(dve, normed, (b.i - RB + 1) * BQ)
                        ins = nc.vector.tensor_scalar(var[:, :], var[:, :], EPS, None, ALU.add)
                    else:
                        done(dve, newton, b.i * NEWTON + n)
                        if n == 1:
                            ins = nc.vector.tensor_scalar(yi, xi, 1, None, ALU.logical_shift_right)
                        elif n == 2:
                            ins = nc.vector.tensor_scalar(yi, yi, -1.0, MAGIC, ALU.mult, ALU.add)
                        elif n % 3 == 0:
                            ins = nc.vector.tensor_tensor(tmp[:, :], y, y, ALU.mult)
                        elif n % 3 == 1:
                            ins = nc.vector.scalar_tensor_tensor(tmp[:, :], tmp[:, :], -0.5, var[:, :], ALU.mult, ALU.mult)
                        else:
                            ins = nc.vector.scalar_tensor_tensor(y, tmp[:, :], 1.5, y, ALU.add, ALU.mult)
                    ins.then_inc(newton, 1)

            def one_hot(b, k):
                done(dve, sums_ready, b.quad(k) - BQ + 1)
                if l == 1:
                    done(dve, hot_b_ready, b.quad(k) - BQ + 1)
                nc.vector.tensor_tensor(hot[:, k, :, :], bc(C["iota_row"][:, :].unsqueeze(1), [P, QT, P]),
                                        bc(cols[:, b.c, k * QT:(k + 1) * QT].unsqueeze(2), [P, QT, P]), ALU.is_equal)\
                  .then_inc(hot_ready, 1)

            def normalize(b, k):
                done(dve, m_ready, b.quad(k) - 2 + 1)
                done(dve, newton, (b.i + 1) * NEWTON)
                r = rstd[:, b.c, k * QT * H0:(k + 1) * QT * H0].unsqueeze(2)
                nc.vector.tensor_tensor(u[:, k % 2, :].rearrange("p (g w) -> p g w", w=D0),
                                        z[(b.c * BQ + k) % ZQ][:, :].rearrange("p (g w) -> p g w", w=D0),
                                        bc(r, [P, QT * H0, D0]), ALU.mult).then_inc(normed, 1)

            def scale(b, k):
                done(dve, normed, b.quad(k) + 1)
                ut = u[:, k % 2, :].rearrange("p (t f) -> p t f", f=P)
                nc.vector.tensor_tensor(ut, ut, bc(gamma.unsqueeze(1), [P, QT, P]), ALU.mult).then_inc(scaled, 1)

            def shift(b, k):
                done(dve, scaled, b.quad(k) + 1)
                ut = u[:, k % 2, :].rearrange("p (t f) -> p t f", f=P)
                nc.vector.tensor_tensor(ut, ut, bc(beta.unsqueeze(1), [P, QT, P]), ALU.add).then_inc(u_ready, 1)

            def step(b, nxt, after):
                for k in range(BQ - 1):
                    if nxt and k + 2 < BQ:
                        one_hot_T(nxt, k + 2)
                    elif after:
                        one_hot_T(after, 0)
                    normalize(b, k)
                    if k + 2 < BQ:
                        one_hot(b, k + 2)
                    scale(b, k)
                    shift(b, k)
                    if nxt:
                        variance(nxt, k)
                k = BQ - 1
                normalize(b, k)
                if nxt:
                    variance(nxt, k)
                scale(b, k)
                if nxt:
                    inverse_std(nxt, 0, 1)
                shift(b, k)
                if nxt:
                    inverse_std(nxt, 1, 2)
                    if after:
                        one_hot_T(after, 1)
                    inverse_std(nxt, 2, 3)
                    dve.wait_ge(meta_landed[nxt.c], (nxt.q + 1) * META)
                    one_hot(nxt, 0)
                    inverse_std(nxt, 3, 4)
                    one_hot(nxt, 1)
                    inverse_std(nxt, 4, NEWTON)
            dve.wait_ge(meta_landed[0], META)
            one_hot(Batch(0, 0), 0)
            one_hot(Batch(0, 0), 1)
            for k in range(BQ):
                one_hot_T(Batch(0, 0), k)
            one_hot_T(Batch(0, 1), 0)
            one_hot_T(Batch(0, 1), 1)
            for k in range(BQ):
                variance(Batch(0, 0), k)
            inverse_std(Batch(0, 0), 0, NEWTON)
            run_batches(dve, step)


def attention_edges(nc, gat, w, C, D, acc, first, acc_e, first_e, small, first_small):
    table = D["g"] if gat else D["kv"]
    RW = P + H1 if gat else 2 * P
    win_table, WW = (D["ed"], NS) if gat else (D["q"], P)
    GQ, WQ, PQ = RB * BQ, 4, 4
    LQ = BQ if gat else RB * BQ
    with Stage(nc, "gat" if gat else "attn") as st:
        idx = st.sb("idx", [P, RB, BT], I32)
        starts_in = st.sb("starts_in", [1, RB, BT], I32)
        n0 = st.sb("n0", [1, RB, BT], I32)
        cols = st.sb("cols", [P, RB, 2 * BT])
        mask = st.sb("mask", [P, RB, P + 1])
        gath = st.sb("gath", [P, GQ, QT, RW])
        win = st.sb("win", [P, WQ, QT, WW])
        places = st.sb("places", [P, LQ, QE], BF16)
        hotT = st.sb("hotT", [P, PQ, QE])
        hot = st.sb("hot", [P, 2, QT, P])
        logit = st.sb("logit", [P, BT, NS])
        logit2 = st.sb("logit2", [P, BT, NS])
        run_max, seg_max = st.sb("run_max", [P, P]), st.sb("seg_max", [P, P])
        below = st.sb("below", [P, P])
        sm = st.sb("sm", [P, RB, BT, SMW])
        val = st.sb("val", [P, 2, QT, P])
        p_turn = st.ps("p_turn", [P, 512])
        if gat:
            xeT = st.sb("xeT", [P, WQ, QE])
            edge = st.sb("edge", [P, GQ, QT, P + NS])
            val_e = C["rows"][:, 0:2 * QT, :].rearrange("p (s t) f -> p s t f", s=2)
            p_edge = [st.ps(f"p_edge{n}", [P, 512]) for n in range(2)]
            sums = [st.ps(f"sums{n}", [P, QE]) for n in range(2)]
            sums_e = [st.ps(f"sums_e{n}", [P, QE]) for n in range(2)]
            smalls = [st.ps("smalls", [P, QE])]
        else:
            ea = st.sb("ea", [ED + 1, RB, BE])
            prod = st.sb("prod", [P, 2, QE])
            p_logit = st.ps("p_logit", [P, 512])
            p_q = [st.ps(f"p_q{n}", [P, QE]) for n in range(2)]
            sums = [st.ps(f"sums{n}", [P, QE]) for n in range(2)]
            smalls = [st.ps(f"smalls{n}", [P, QE]) for n in range(2)]
        NO, NSM = len(sums), len(smalls)

        early_landed = [st.sem(f"early_landed{c}") for c in range(RB)]
        late_landed = [st.sem(f"late_landed{c}") for c in range(RB)]
        gath_landed = [st.sem(f"gath_landed{n}") for n in range(GQ)]
        win_landed = [st.sem(f"win_landed{n}") for n in range(WQ)]
        places_landed = [st.sem(f"places_landed{n}") for n in range(BQ if gat else RB)]
        hotT_ready, hot_ready = st.sem("hotT_ready"), st.sem("hot_ready")
        cleared, zeroed, filled = st.sem("cleared"), st.sem("zeroed"), st.sem("filled")
        fold_table = D["fold4" if gat else "fold3"]
        zero = st.sb("zero", [FR, fold_table.shape[1]])
        scored, edge_copied, part_ready, parts_summed = (
            st.sem(n) for n in ("scored", "edge_copied", "part_ready", "parts_summed"))
        smalls_ready, sums_ready, sums_e_ready = (st.sem(n) for n in ("smalls_ready", "sums_ready", "sums_e_ready"))
        small_copied, sums_copied, sums_e_copied = (st.sem(n) for n in ("small_copied", "sums_copied", "sums_e_copied"))
        small_freed, sums_freed, sums_e_freed = (st.sem(n) for n in ("small_freed", "sums_freed", "sums_e_freed"))
        logit_ready, logitT_ready, below_ready, ex_ready, turned = (
            st.sem(n) for n in ("logit_ready", "logitT_ready", "below_ready", "ex_ready", "turned"))
        sm_ready, val_ready, val_e_ready = st.sem("sm_ready"), st.sem("val_ready"), st.sem("val_e_ready")
        maxima, logit_parts = st.sem("maxima"), st.sem("logit_parts")
        EARLY, LATE = 2 * 16, 3 * 16
        WINS = (QT + 1 if gat else QT) * 16
        block = st.ctx.enter_context(nc.Block())

        @block.sync
        def _(sp):
            def early(b):
                done(sp, logit_ready, 2 * (b.i - RB + 1))
                settle(sp, st.passed)
                sp.dma_start(idx[:, b.c, :], w["src_b"][bass.ds(b.i, 1), :, :].rearrange("a p t -> (a p) t"))\
                  .then_inc(early_landed[b.c], 16)
                sp.dma_start(starts_in[:, b.c, :], w["n0_b"][bass.ds(b.i, 1), :]).then_inc(early_landed[b.c], 16)

            def fetch(b, nxt, _):
                if nxt:
                    early(nxt)
                sp.wait_ge(early_landed[b.c], (b.q + 1) * EARLY)
                settle(sp, st.passed)
                _, starts = nc.values_load_multi_w_load_instructions(
                    starts_in[0:1, b.c, :], engines=(SP_ENGINE,), min_val=0, max_val=N,
                    skip_runtime_bounds_check_because="destinations are node numbers")
                if not gat:
                    done(sp, hotT_ready, (b.i - RB + 1) * BQ)
                    done(sp, scored, (b.i - RB + 1) * BQ)
                    settle(sp, st.passed)
                    sp.dma_start(places[:, b.c * BQ:(b.c + 1) * BQ, :].rearrange("p q e -> p (q e)"),
                                 D["places"][bass.ds(b.i, 1), :].to_broadcast([P, BE])).then_inc(places_landed[b.c], 16)
                    sp.dma_start(ea[:, b.c, :], w["ea"][:, bass.ds(b.i * BE, BE)]).then_inc(places_landed[b.c], 16)
                for k in range(BQ):
                    s4 = k
                    if gat:
                        done(sp, hotT_ready, b.quad(k) - LQ + 1)
                        settle(sp, st.passed)
                        sp.dma_start(places[:, s4, :],
                                     D["places"][bass.ds(b.i, 1), k * QE:(k + 1) * QE].to_broadcast([P, QE]))\
                          .then_inc(places_landed[s4], 16)
                    done(sp, scored, b.quad(k) - WQ + 1)
                    settle(sp, st.passed)
                    for t in range(QT):
                        sp.dma_start(win[:, s4, t, :], win_table[bass.ds(starts[k * QT + t], P), :])\
                          .then_inc(win_landed[s4], 16)
                    if gat:
                        sp.dma_start(xeT[:, s4, :], w["xeT"][:, bass.ds(b.i * BE + k * QE, QE)])\
                          .then_inc(win_landed[s4], 16)
                done(sp, hot_ready, (b.i - RB + 1) * BQ)
                done(sp, small_copied, (b.i - RB) * BT + 1)
                settle(sp, st.passed)
                sp.dma_start(cols[:, b.c, :], D["cols"][bass.ds(b.i, 1), :, :].rearrange("a p t -> (a p) t"))\
                  .then_inc(late_landed[b.c], 16)
                sp.dma_start(n0[:, b.c, :], w["n0_b"][bass.ds(b.i, 1), :]).then_inc(late_landed[b.c], 16)
                sp.dma_start(mask[:, b.c, :], D["mask"][bass.ds(b.i * P, P), :]).then_inc(late_landed[b.c], 16)
                sp.dma_start(fold_table[bass.ds(b.i * FR, FR), :], zero[:, :]).then_inc(filled, 16)
            early(Batch(0, 0))
            sp.wait_ge(zeroed, 1)
            run_batches(sp, fetch)
            sp.wait_ge(filled, NB * 16)

        @block.gpsimd
        def _(pool):
            def gather(b, *_):
                pool.wait_ge(early_landed[b.c], (b.q + 1) * EARLY)
                for k in range(BQ):
                    done(pool, val_ready, b.quad(k) - GQ + 1)
                    settle(pool, st.passed)
                    for t in range(QT):
                        pool.indirect_dma_start(
                            gath[:, b.c * BQ + k, t, :], None, table,
                            bass.IndirectOffsetOnAxis(ap=idx[:, b.c, k * QT + t:k * QT + t + 1], axis=0))\
                            .then_inc(gath_landed[b.c * BQ + k], 16)
            run_batches(pool, gather)

        @block.tensor
        def _(pe):
            for s in (scored, smalls_ready, sums_ready, sums_e_ready, logitT_ready, turned):
                pe.sem_inc(s, HEAD)

            def score(b, k):
                s4, g = k, b.quad(k)
                pe.wait_ge(win_landed[s4], (b.i + 1) * WINS)
                if not gat:
                    pe.wait_ge(places_landed[b.c], (b.q + 1) * 2 * 16)
                done(pe, hotT_ready, g + 1)
                if gat:
                    done(pe, edge_copied, g)
                else:
                    done(pe, part_ready, g - 2 + 1)
                    if k == 0:
                        done(pe, logit_ready, 2 * (b.i - RB + 1))
                for t in range(QT):
                    e = slice(t * P, (t + 1) * P)
                    if gat:
                        et = p_edge[t // 2][:, t % 2 * (P + NS):(t % 2 + 1) * (P + NS)]
                        nc.tensor.matmul(et, xeT[:, s4, e], C["weta"][:, :], start=True, stop=False,
                                         skip_group_check=True)
                        mm = nc.tensor.matmul(et[:, P:P + NS], hotT[:, s4, e], win[:, s4, t, :], start=False,
                                              stop=True, skip_group_check=True)
                    else:
                        nc.tensor.matmul(p_q[k % 2][:, e], hotT[:, s4, e], win[:, s4, t, :], start=True, stop=True)
                        lt = p_logit[:, b.c * P + (k * QT + t) * NS:b.c * P + (k * QT + t + 1) * NS]
                        mm = nc.tensor.matmul(lt, ea[:, b.c, k * QE + t * P:k * QE + (t + 1) * P], C["we"][:, :], start=True, stop=True)
                mm.then_inc(scored, 1)

            def turn(b):
                done(pe, logit_ready, 2 * (b.i + 1))
                done(pe, below_ready, b.i)
                nc.tensor.transpose(p_turn[:, 0:P], logit2[:, :, :].rearrange("p t s -> p (t s)"), C["ident"][:, :])\
                  .then_inc(logitT_ready, 1)

            def turn_back(b):
                done(pe, ex_ready, b.i + 1)
                done(pe, sm_ready, 2 * b.i)
                nc.tensor.transpose(p_turn[:, P:2 * P], below[:, :], C["ident"][:, :])
                nc.tensor.transpose(p_turn[:, 2 * P:3 * P], seg_max[:, :], C["ident"][:, :]).then_inc(turned, 1)

            def sum_up(b, k):
                s2, g, so = k % 2, b.quad(k), k % NO
                done(pe, hot_ready, g + 1)
                done(pe, val_ready, g + 1)
                done(pe, sums_freed, g - NO + 1)
                for t in range(QT):
                    mm = nc.tensor.matmul(sums[so][:, t * P:(t + 1) * P], val[:, s2, t, :], hot[:, s2, t, :],
                                          start=True, stop=True)
                mm.then_inc(sums_ready, 1)
                if gat:
                    done(pe, val_e_ready, g + 1)
                    done(pe, sums_e_freed, g - NO + 1)
                    for t in range(QT):
                        mm = nc.tensor.matmul(sums_e[so][:, t * P:(t + 1) * P], val_e[:, s2, t, :], hot[:, s2, t, :],
                                              start=True, stop=True)
                    mm.then_inc(sums_e_ready, 1)
                done(pe, sm_ready, 2 * (b.i + 1))
                done(pe, small_freed, g - NSM + 1)
                for t in range(QT):
                    mm = nc.tensor.matmul(smalls[k % NSM][0:SMW, t * P:(t + 1) * P], sm[:, b.c, k * QT + t, :],
                                          hot[:, s2, t, :], start=True, stop=True)
                mm.then_inc(smalls_ready, 1)

            def step(b, nxt, after):
                for k in range(BQ):
                    if after:
                        score(after, k)
                    if nxt and k == 0:
                        turn(nxt)
                    sum_up(b, k)
                    if nxt and k == 2:
                        turn_back(nxt)
            for b in (Batch(0, 0), Batch(0, 1)):
                for k in range(BQ):
                    score(b, k)
                if b.c == 0:
                    turn(b)
                    turn_back(b)
            run_batches(pe, step)

        @block.scalar
        def _(act):
            for s in (edge_copied, ex_ready, small_copied, sums_copied, sums_e_copied, small_freed, sums_freed, sums_e_freed):
                act.sem_inc(s, HEAD)

            def keep_edges(b, k):
                g = b.quad(k)
                done(act, scored, g + 1)
                done(act, val_e_ready, g - GQ + 1)
                for n in range(2):
                    ins = act.copy(edge[:, b.c * BQ + k, 2 * n:2 * n + 2, :].rearrange("p t f -> p (t f)"),
                                   p_edge[n][:, 0:2 * (P + NS)])
                ins.then_inc(edge_copied, 1)

            def exponent(b):
                done(act, below_ready, b.i + 1)
                act.activation(below[:, :], below[:, :], ACT.Exp).then_inc(ex_ready, 1)

            def copies(b, k, starts):
                g, so = b.quad(k), k % NO
                outs = [(small, first_small, smalls[k % NSM][0:SMW, :], smalls_ready, small_copied, small_freed),
                        (acc, first, sums[so][:, :], sums_ready, sums_copied, sums_freed)]
                if gat:
                    outs.append((acc_e, first_e, sums_e[so][:, :], sums_e_ready, sums_e_copied, sums_e_freed))
                for *_, ready, _, _ in outs:
                    done(act, ready, g + 1)
                for t in range(QT):
                    for kept, _, new, _, copied, _ in outs:
                        done(act, copied, g * QT + t)
                        act.copy(kept[:, bass.ds(starts[k * QT + t] + 1, P - 1)], new[:, t * P + 1:(t + 1) * P])\
                           .then_inc(copied, 1)
                for _, kept_first, new, _, _, freed in outs:
                    act.copy(kept_first[:, bass.ds(g * QT, QT)], new.rearrange("p (t n) -> p t n", n=P)[:, :, 0])\
                       .then_inc(freed, 1)

            def step(b, nxt, after):
                act.wait_ge(late_landed[b.c], (b.q + 1) * LATE)
                settle(act, st.passed)
                _, starts = nc.values_load_multi_w_load_instructions(
                    n0[0:1, b.c, :], engines=(ACT_ENGINE,), min_val=0, max_val=N,
                    skip_runtime_bounds_check_because="destinations are node numbers")
                for k in range(BQ):
                    if gat and after:
                        keep_edges(after, k)
                    copies(b, k, starts)
                    if nxt and k == 0:
                        exponent(nxt)
            act.wait_ge(cleared, 1)
            if gat:
                for k in range(BQ):
                    keep_edges(Batch(0, 0), k)
                exponent(Batch(0, 0))
                for k in range(BQ):
                    keep_edges(Batch(0, 1), k)
            else:
                exponent(Batch(0, 0))
            run_batches(act, step)

        @block.vector
        def _(dve):
            for s in (hotT_ready, hot_ready, logit_ready, below_ready, sm_ready, val_ready, part_ready, parts_summed,
                      val_e_ready, maxima, logit_parts):
                dve.sem_inc(s, HEAD)
            nc.vector.memset(zero[:, :], 0.0).then_inc(zeroed, 1)
            nc.vector.memset(sm[:, :, :, :], 0.0)
            nc.vector.memset(small[:, :], 0.0)
            nc.vector.memset(first_small[:, :], 0.0)
            nc.vector.memset(first[:, :], 0.0)
            if gat:
                nc.vector.memset(acc_e[:, :], 0.0)
                nc.vector.memset(first_e[:, :], 0.0)
            nc.vector.memset(acc[:, :], 0.0).then_inc(cleared, 1)
            dve.wait_ge(cleared, 1)

            def one_hot_T(b, k):
                if gat:
                    dve.wait_ge(places_landed[k], (b.i + 1) * 16)
                else:
                    dve.wait_ge(places_landed[b.c], (b.q + 1) * 2 * 16)
                done(dve, scored, b.quad(k) - PQ + 1)
                nc.vector.tensor_scalar(hotT[:, k, :], places[:, (b.c * BQ + k) % LQ, :], C["iota_col"][:, 0:1], None, ALU.is_equal)\
                  .then_inc(hotT_ready, 1)

            def score(b, k):
                g, s12, s2 = b.quad(k), b.c * BQ + k, k % 2
                dve.wait_ge(gath_landed[s12], (b.q + 1) * QT * 16)
                done(dve, scored, g + 1)
                nc.vector.tensor_tensor(prod[:, s2, :].rearrange("p (t f) -> p t f", f=P),
                                        p_q[s2][:, :].rearrange("p (t f) -> p t f", f=P), gath[:, s12, :, 0:P], ALU.mult)\
                  .then_inc(part_ready, 1)
                done(dve, part_ready, g + 1)
                if k == 0:
                    done(dve, logit_ready, 2 * b.i)
                nc.vector.tensor_reduce(logit[:, k * QT:(k + 1) * QT, :].rearrange("p t s -> p (t s)"),
                                        prod[:, s2, :].rearrange("p (g w) -> p g w", w=D0), AX.X, ALU.add)\
                  .then_inc(parts_summed, 1)

            def logits(b):
                if gat:
                    quads = slice(b.c * BQ, (b.c + 1) * BQ)
                    done(dve, edge_copied, b.quad(BQ))
                    for k in range(BQ):
                        dve.wait_ge(gath_landed[b.c * BQ + k], (b.q + 1) * QT * 16)
                    mine = edge[:, quads, :, P:P + NS].rearrange("p q t s -> p (q t) s")
                    g = gath[:, quads, :, P:RW].rearrange("p q t s -> p (q t) s")
                    done(dve, logit_ready, 2 * b.i)
                    nc.vector.tensor_tensor(logit[:, :, 0:H1], mine[:, :, 0:H1], g, ALU.add).then_inc(logit_parts, 1)
                    done(dve, logitT_ready, b.i)
                    nc.vector.scalar_tensor_tensor(logit2[:, :, H1:NS], mine[:, :, H1:NS], 0.2, mine[:, :, H1:NS],
                                                   ALU.mult, ALU.max).then_inc(logit_ready, 1)
                    done(dve, logit_parts, b.i + 1)
                    nc.vector.scalar_tensor_tensor(logit2[:, :, 0:H1], logit[:, :, 0:H1], 0.2, logit[:, :, 0:H1],
                                                   ALU.mult, ALU.max).then_inc(logit_ready, 1)
                else:
                    done(dve, scored, b.quad(BQ))
                    done(dve, parts_summed, b.quad(BQ))
                    done(dve, logitT_ready, b.i)
                    pl = p_logit[:, b.c * P:(b.c + 1) * P].rearrange("p (t s) -> p t s", s=NS)
                    nc.vector.tensor_tensor(logit2[:, :, :], logit[:, :, :], pl, ALU.add).then_inc(logit_ready, 2)

            def against_maxima(b):
                dve.wait_ge(late_landed[b.c], (b.q + 1) * LATE)
                done(dve, logitT_ready, b.i + 1)
                done(dve, turned, b.i)
                nc.vector.tensor_tensor_scan(run_max[:, :], mask[:, b.c, 0:P], p_turn[:, 0:P], -BIG, ALU.add, ALU.max)\
                  .then_inc(maxima, 1)
                done(dve, maxima, 2 * b.i + 1)
                nc.vector.tensor_tensor_scan(seg_max[:, ::-1], mask[:, b.c, P:0:-1], run_max[:, ::-1], -BIG,
                                             ALU.add, ALU.max).then_inc(maxima, 1)
                done(dve, maxima, 2 * b.i + 2)
                nc.vector.tensor_tensor(below[:, :], p_turn[:, 0:P], seg_max[:, :], ALU.subtract).then_inc(below_ready, 1)

            def weights(b):
                done(dve, turned, b.i + 1)
                done(dve, smalls_ready, (b.i - RB + 1) * BQ)
                pt = p_turn[:, P:3 * P].rearrange("p (a t s) -> p a t s", a=2, s=NS)
                nc.vector.tensor_copy(sm[:, b.c, :, 0:NS], pt[:, 0, :, :]).then_inc(sm_ready, 1)
                nc.vector.tensor_tensor(sm[:, b.c, :, MR:SMW], pt[:, 1, :, :],
                                        bc(cols[:, b.c, BT:2 * BT].unsqueeze(2), [P, BT, NS]), ALU.mult)\
                  .then_inc(sm_ready, 1)

            def weigh(b, k):
                g, s2, s12 = b.quad(k), k % 2, b.c * BQ + k
                done(dve, smalls_ready, g - 2 + 1)
                nc.vector.tensor_tensor(hot[:, s2, :, :], bc(C["iota_row"][:, :].unsqueeze(1), [P, QT, P]),
                                        bc(cols[:, b.c, k * QT:(k + 1) * QT].unsqueeze(2), [P, QT, P]), ALU.is_equal)\
                  .then_inc(hot_ready, 1)
                done(dve, sm_ready, 2 * (b.i + 1))
                wts = sm[:, b.c, k * QT:(k + 1) * QT, :]
                heads, width, v0 = (H1, D1, 0) if gat else (H0, D0, P)
                nc.vector.tensor_tensor(val[:, s2, :, :].rearrange("p t (h d) -> p t h d", d=width),
                                        gath[:, s12, :, v0:v0 + P].rearrange("p t (h d) -> p t h d", d=width),
                                        bc(wts[:, :, 0:heads].unsqueeze(3), [P, QT, heads, width]), ALU.mult)\
                  .then_inc(val_ready, 1)
                if gat:
                    nc.vector.tensor_tensor(val_e[:, s2, :, :].rearrange("p t (h d) -> p t h d", d=D1),
                                            edge[:, s12, :, 0:P].rearrange("p t (h d) -> p t h d", d=D1),
                                            bc(wts[:, :, H1:NS].unsqueeze(3), [P, QT, H1, D1]), ALU.mult)\
                      .then_inc(val_e_ready, 1)

            def step(b, nxt, after):
                for k in range(BQ):
                    if after and k == 0:
                        one_hot_T(after, 0)
                    if after and k + 1 < BQ:
                        one_hot_T(after, k + 1)
                    weigh(b, k)
                    if after and not gat:
                        score(after, k)
                    if nxt and k == 0:
                        against_maxima(nxt)
                if nxt:
                    weights(nxt)
                if after:
                    logits(after)
            for b in (Batch(0, 0), Batch(0, 1)):
                for k in range(BQ):
                    one_hot_T(b, k)
                    if not gat:
                        score(b, k)
                logits(b)
                if b.c == 0:
                    against_maxima(b)
                    weights(b)
            run_batches(dve, step)


def fold(nc, name, w, C, table, first, first_e, first_small, soft):
    with Stage(nc, name) as st:
        n0 = st.sb("n0", [P, TP], I32)
        n0f = st.sb("n0f", [P, TP])
        same = st.sb("same", [P, TP])
        part = st.sb("part", [P, TP + 1])
        W = table.shape[1]
        rows = st.sb("rows", [P, 2, W])
        folded = [st.sb(f"folded{n}", [P, TP]) for n in range(2 if first_e is not None else 1)]
        parts = [first] + ([first_e] if first_e is not None else [])
        SW = 0 if first_small is None else SMW if soft else 1
        small = st.sb("small", [max(SW, 1), TP])
        p_f = [st.ps(f"p_f{n}", [P, 512]) for n in range(2)]
        p_s = st.ps("p_s", [P, 512])
        p_t = [st.ps(f"p_t{n}", [P, 512]) for n in range(2)]
        loaded, chain, ex_ready, expanded, scaled = (st.sem(n) for n in ("loaded", "chain", "ex_ready", "expanded", "scaled"))
        below_ready, summed, turned, rows_ready = (st.sem(n) for n in ("below_ready", "summed", "turned", "rows_ready"))
        stored = [st.sem(f"stored{n}") for n in range(2)]
        if soft:
            run_max, below = st.sb("run_max", [SMW, TP]), st.sb("below", [SMW, TP])
        CH = -(-TP // 512)
        block = st.ctx.enter_context(nc.Block())

        @block.sync
        def _(sp):
            sp.dma_start(n0[:, :], w["n0_p"].to_broadcast([P, TP])).then_inc(loaded, 16)

        @block.vector
        def _(dve):
            link = Chain(dve, chain)
            if soft:
                link(nc.vector.memset(small[:, :], 0.0))
            dve.wait_ge(loaded, 16)
            link(nc.vector.tensor_copy(n0f[:, :], n0[:, :]))
            link(nc.vector.memset(same[:, 0:1], 0.0))
            link(nc.vector.tensor_tensor(same[:, 1:TP], n0f[:, 1:TP], n0f[:, 0:TP - 1], ALU.is_equal))
            if soft:
                m = slice(MR, SMW)
                link(nc.vector.tensor_scalar(part[:, 0:TP], same[:, :], -1.0, BIG, ALU.add, ALU.mult))
                link(nc.vector.memset(part[:, TP:TP + 1], -BIG))
                link(nc.vector.tensor_tensor_scan(run_max[m, :], part[m, 0:TP], first_small[m, :], -BIG, ALU.add, ALU.max))
                link(nc.vector.tensor_tensor_scan(small[m, ::-1], part[m, TP:0:-1], run_max[m, ::-1], -BIG, ALU.add, ALU.max))
                nc.vector.tensor_tensor(below[m, :], first_small[m, :], small[m, :], ALU.subtract).then_inc(below_ready, 1)
                for c in range(CH):
                    e = slice(c * 512, min(TP, (c + 1) * 512))
                    n = e.stop - e.start
                    dve.wait_ge(expanded, c + 1)
                    for i, t in enumerate(parts):
                        link(nc.vector.tensor_tensor(t[:, e], t[:, e], p_f[i][:, 0:n], ALU.mult))
                    link(nc.vector.tensor_tensor(first_small[0:NS, e], first_small[0:NS, e], p_s[0:NS, 0:n], ALU.mult))
                    dve.sem_inc(scaled, 1)
            for i, t in enumerate(parts):
                link(nc.vector.tensor_tensor_scan(folded[i][:, :], same[:, :], t[:, :], 0.0, ALU.mult, ALU.add))
            if SW:
                r = NS if soft else 1
                link(nc.vector.tensor_tensor_scan(small[0:r, :], same[0:r, :], first_small[0:r, :], 0.0, ALU.mult, ALU.add))
            dve.sem_inc(summed, 1)
            for c in range(TC):
                dve.wait_ge(turned, c + 1)
                if c >= 2:
                    dve.wait_ge(stored[c % 2], c // 2 * 16)
                nc.vector.tensor_copy(rows[:, c % 2, :], p_t[c % 2][:, 0:W]).then_inc(rows_ready, 1)

        @block.scalar
        def _(act):
            if soft:
                act.wait_ge(below_ready, 1)
                act.activation(below[MR:SMW, :], below[MR:SMW, :], ACT.Exp).then_inc(ex_ready, 1)

        @block.tensor
        def _(pe):
            if soft:
                pe.wait_ge(ex_ready, 1)
                for c in range(CH):
                    e = slice(c * 512, min(TP, (c + 1) * 512))
                    n = e.stop - e.start
                    if c:
                        pe.wait_ge(scaled, c)
                    for i, lay in enumerate(soft):
                        nc.tensor.matmul(p_f[i][:, 0:n], C["expand"][MR:SMW, lay, :], below[MR:SMW, e], start=True, stop=True)
                    nc.tensor.matmul(p_s[0:NS, 0:n], C["ident"][MR:SMW, MR:SMW], below[MR:SMW, e], start=True, stop=True)\
                      .then_inc(expanded, 1)
            pe.wait_ge(summed, 1)
            for c in range(TC):
                e = slice(c * P, (c + 1) * P)
                if c >= 2:
                    pe.wait_ge(rows_ready, c - 1)
                for i in range(len(parts)):
                    mm = nc.tensor.transpose(p_t[c % 2][:, i * P:(i + 1) * P], folded[i][:, e], C["ident"][:, :])
                if SW:
                    mm = nc.tensor.transpose(p_t[c % 2][:, len(parts) * P:W], small[0:SW, e], C["ident"][0:SW, 0:SW])
                mm.then_inc(turned, 1)

        @block.gpsimd
        def _(pool):
            for c in range(TC):
                pool.wait_ge(rows_ready, c + 1)
                pool.indirect_dma_start(table, bass.IndirectOffsetOnAxis(ap=C["fold_row"][:, c:c + 1], axis=0),
                                        rows[:, c % 2, :], None, bounds_check=NP - 1, oob_is_err=False)\
                    .then_inc(stored[c % 2], 16)
            pool.wait_ge(stored[0], (TC + 1) // 2 * 16)
            pool.wait_ge(stored[1], TC // 2 * 16)


def blocks_of(table, g):
    return table[bass.ds(g * GW, GW), :].rearrange("(b p) c -> p b c", p=P)


def node_stage(nc, kind, w, C, D, cnt, acc, acc_e, small, out):
    soft = kind in ("attn", "gat")
    fold_table = {"first": None, "conv1": D["fold1"], "conv2": D["fold2"], "attn": D["fold3"], "gat": D["fold4"]}[kind]
    FW = fold_table.shape[1] if fold_table is not None else 1
    with Stage(nc, "n_" + kind) as st:
        slots = []
        for n in range(2):
            totT, totT_e = st.sb(f"totT{n}", [P, GW]), st.sb(f"totT_e{n}", [P, GW])
            slots.append((st.sb(f"x{n}", [P, GB, P]),
                          st.sb(f"fr{n}", [P, GB, FW]),
                          st.sb(f"h{n}", [P, GB, P]), st.sb(f"made{n}", [P, GB, 2 * P + H1]),
                          st.sb(f"made_s{n}", [P, GB, 3 * H1]), st.sb(f"cT{n}", [SMW, GW]),
                          totT, totT_e, totT if kind == "gat" else totT_e))
        sq, h2 = (st.sb(n, [P, GB, P]) for n in ("sq", "h2"))
        mean, rstd, tmp = (st.sb(n, [P, GB * H0]) for n in ("mean", "rstd", "tmp"))
        sb_small = st.sb("sb_small", [P, GB, SMW])
        M, fa, fb, S = (st.sb(n, [P, GB, NS]) for n in ("M", "fa", "fb", "S"))
        p1, p2, p_w = st.ps("p1", [P, 1024]), st.ps("p2", [P, 1024]), st.ps("p_w", [P, 2048])
        p1b = p1[:, 0:GW].rearrange("p (b f) -> p b f", f=P)
        p2b = p2[:, 0:GW].rearrange("p (b f) -> p b f", f=P)
        pwb = p_w[:, 0:GB * 2 * P].rearrange("p (b f) -> p b f", f=2 * P)
        p_small = p_w if kind == "gat" else p2
        p_ws = p_w[:, GB * 2 * P:GB * (2 * P + 3 * H1)].rearrange("p (b s) -> p b s", s=3 * H1)
        loaded, stored = ([st.sem(f"{n}{s}") for s in range(2)] for n in ("loaded", "stored"))
        names = ("chain", "copied", "turned1", "tot_ready", "mapped", "pre_act", "acted", "h_ready", "turned2",
                 "hT_ready", "tables_ready", "evacuated", "below_ready", "ex_ready", "o_ready", "o_turned", "oT_ready")
        (chain, copied, turned1, tot_ready, mapped, pre_act, acted, h_ready, turned2, hT_ready, tables_ready,
         evacuated, below_ready, ex_ready, o_ready, o_turned, oT_ready) = (st.sem(n) for n in names)
        LOADS = 16 * {"first": 1, "conv1": 1, "conv2": 2, "attn": 3, "gat": 3}[kind]
        STORES = 16 * {"first": 3, "conv1": 2, "conv2": 3, "attn": 4, "gat": 1}[kind]
        wide = [P, GB, P]

        block = st.ctx.enter_context(nc.Block())

        @block.sync
        def _(sp):
            sp.sem_inc(stored[0], HEAD)
            sp.sem_inc(stored[1], HEAD)

            def load(g, slot):
                x, fr, _, made, *_ = slots[slot]
                if kind != "conv1":
                    source = {"first": w["x"], "conv2": D["h"], "attn": w["x"], "gat": D["base"]}[kind]
                    sp.dma_start(x[:, :, :], blocks_of(source, g)).then_inc(loaded[slot], 16)
                if kind == "attn":
                    sp.dma_start(made[:, :, 0:P], blocks_of(D["h"], g)).then_inc(loaded[slot], 16)
                if kind == "gat":
                    sp.dma_start(made[:, :, 0:P], blocks_of(D["hd"], g)).then_inc(loaded[slot], 16)
                if fold_table is not None:
                    sp.dma_start(fr[:, :, :], blocks_of(fold_table, g)).then_inc(loaded[slot], 16)

            def step(g, s, q, nxt):
                x, _, h, made, made_s, *_ = slots[s]
                if nxt is not None:
                    sp.wait_ge(evacuated, g + 2)
                    sp.wait_ge(stored[1 - s], (q + s) * STORES + HEAD)
                    settle(sp, st.passed)
                    load(nxt, 1 - s)
                sp.wait_ge(evacuated, g + 3)
                settle(sp, st.passed)
                if kind in ("first", "conv2"):
                    sp.dma_start(blocks_of(D["h"], g), x[:, :, :]).then_inc(stored[s], 16)
                if kind in ("first", "conv1"):
                    l = 1 if kind == "first" else 2
                    sp.dma_start(blocks_of(D[f"a{l}"], g), made[:, :, 0:P]).then_inc(stored[s], 16)
                    sp.dma_start(blocks_of(D[f"b{l}"], g), made[:, :, P:2 * P]).then_inc(stored[s], 16)
                elif kind == "conv2":
                    sp.dma_start(blocks_of(D["q"], g), h[:, :, :]).then_inc(stored[s], 16)
                    sp.dma_start(blocks_of(D["kv"], g), made[:, :, 0:2 * P]).then_inc(stored[s], 16)
                elif kind == "attn":
                    sp.dma_start(blocks_of(D["g"], g), made[:, :, 0:P + H1]).then_inc(stored[s], 16)
                    sp.dma_start(blocks_of(D["base"], g), x[:, :, :]).then_inc(stored[s], 16)
                    sp.dma_start(blocks_of(D["hd"], g), made[:, :, P + H1:]).then_inc(stored[s], 16)
                    sp.dma_start(blocks_of(D["ed"], g), made_s[:, :, H1:3 * H1]).then_inc(stored[s], 16)
                else:
                    sp.dma_start(blocks_of(out, g), h[:, :, :]).then_inc(stored[s], 16)
            load(0, 0)
            run_groups(sp, step)
            sp.wait_ge(stored[0], (NGRP // 2 + 1) * STORES + HEAD)
            sp.wait_ge(stored[1], NGRP // 2 * STORES + HEAD)

        @block.tensor
        def _(pe):
            ident = C["ident"][:, :]

            def turn(g, slot, q):
                _, fr, _, _, _, cT, totT, totT_e, _ = slots[slot]
                if kind in ("conv2", "gat"):
                    pe.wait_ge(evacuated, g + 2)
                if kind in ("conv1", "conv2"):
                    pe.wait_ge(loaded[slot], (q + 1) * LOADS)
                    for b in range(GB):
                        mm = nc.tensor.transpose(p1b[:, b, :], fr[:, b, 0:P], ident)
                    if kind == "conv1":
                        pe.wait_ge(copied, g + 1)
                        settle(pe, st.passed)
                        for b in range(GB):
                            mm = nc.tensor.transpose(p2[:, b:b + 1], cT[0:1, b * P:(b + 1) * P], ident[0:1, 0:1])
                    mm.then_inc(turned1, 1)
                if soft:
                    pe.wait_ge(copied, g + 1)
                    settle(pe, st.passed)
                    for b in range(GB):
                        e = slice(b * P, (b + 1) * P)
                        nc.tensor.transpose(p1b[:, b, :], totT[:, e], ident)
                        if kind == "gat":
                            nc.tensor.transpose(p2b[:, b, :], totT_e[:, e], ident)
                        mm = nc.tensor.transpose(p_small[:, b * SMW:(b + 1) * SMW], cT[:, e], ident[0:SMW, 0:SMW])
                    mm.then_inc(turned1, 1)

            def step(g, s, q, nxt):
                h, totT, hT = slots[s][2], slots[s][6], slots[s][8]
                if kind in ("conv1", "conv2"):
                    pe.wait_ge(tot_ready, g + 1)
                    settle(pe, st.passed)
                    w2 = C["w21" if kind == "conv1" else "w22"]
                    for b in range(GB):
                        mm = nc.tensor.matmul(p1b[:, b, :], totT[:, b * P:(b + 1) * P], w2[:, :], start=True, stop=True)
                    mm.then_inc(mapped, 1)
                if kind == "attn":
                    pe.wait_ge(o_ready, g + 1)
                    settle(pe, st.passed)
                    for b in range(GB):
                        mm = nc.tensor.transpose(p2b[:, b, :], h[:, b, :], ident)
                    mm.then_inc(o_turned, 1)
                    pe.wait_ge(oT_ready, g + 1)
                    settle(pe, st.passed)
                    for b in range(GB):
                        mm = nc.tensor.matmul(p1b[:, b, :], totT[:, b * P:(b + 1) * P], C["wo"][:, :], start=True, stop=True)
                    mm.then_inc(mapped, 1)
                if kind != "gat":
                    pe.wait_ge(h_ready, g + 1)
                    settle(pe, st.passed)
                    for b in range(GB):
                        mm = nc.tensor.transpose(p2b[:, b, :], h2[:, b, :], ident)
                    mm.then_inc(turned2, 1)
                    pe.wait_ge(hT_ready, g + 1)
                    settle(pe, st.passed)
                    if nxt is not None and kind in ("conv1", "attn"):
                        turn(nxt, 1 - s, q + s)
                    pe.wait_ge(evacuated, g + 2)
                    settle(pe, st.passed)
                    rhs = {"first": "wab1", "conv1": "wab2", "conv2": "wkv", "attn": "wsd"}[kind]
                    for b in range(GB):
                        hb = hT[:, b * P:(b + 1) * P]
                        mm = nc.tensor.matmul(pwb[:, b, :], hb, C[rhs][:, :, :].rearrange("p a f -> p (a f)"), start=True, stop=True)
                        if kind == "conv2":
                            mm = nc.tensor.matmul(p1b[:, b, :], hb, C["wq"][:, :], start=True, stop=True)
                        if kind == "attn":
                            mm = nc.tensor.matmul(p_ws[:, b, :], hb, C["wsa"][:, :], start=True, stop=True)
                    mm.then_inc(tables_ready, 1)
                if nxt is not None and kind in ("conv2", "gat"):
                    turn(nxt, 1 - s, q + s)
            turn(0, 0, 0)
            run_groups(pe, step)

        @block.scalar
        def _(act):
            def columns(g, slot):
                _, _, _, _, _, cT, totT, totT_e, _ = slots[slot]
                nodes = bass.ds(g * GW, GW)
                if soft:
                    act.copy(totT[:, :], acc[:, nodes])
                if kind == "gat":
                    act.copy(totT_e[:, :], acc_e[:, nodes])
                if kind == "conv1" or soft:
                    act.copy(cT[0:1, :] if kind == "conv1" else cT[:, :], small[:, nodes]).then_inc(copied, 1)

            def tables(g, s, q):
                made, made_s = slots[s][3:5]
                act.wait_ge(tables_ready, g + 1)
                act.wait_ge(stored[s], q * STORES + HEAD)
                if kind == "attn":
                    act.copy(made[:, :, 0:P], pwb[:, :, 0:P])
                    act.copy(made[:, :, P:P + H1], p_ws[:, :, 0:H1])
                    act.copy(made[:, :, P + H1:], pwb[:, :, P:2 * P])
                    act.copy(made_s[:, :, :], p_ws).then_inc(evacuated, 1)
                else:
                    act.copy(made[:, :, 0:2 * P], pwb).then_inc(evacuated, 1)

            def step(g, s, q, nxt):
                h = slots[s][2]
                if kind in ("conv1", "conv2"):
                    act.wait_ge(pre_act, g + 1)
                    act.activation(h[:, :, :], h[:, :, :], ACT.Silu).then_inc(acted, 1)
                if soft:
                    act.wait_ge(below_ready, g + 1)
                    act.activation(fa[:, :, :], fa[:, :, :], ACT.Exp)
                    act.activation(fb[:, :, :], fb[:, :, :], ACT.Exp).then_inc(ex_ready, 1)
                if kind == "attn" and s == 1:
                    tables(g - 1, 0, q)
                if nxt is not None and (kind == "conv1" or soft):
                    act.wait_ge(evacuated, g + 2)
                    settle(act, st.passed)
                    columns(nxt, 1 - s)
                if kind in ("first", "conv1") or kind == "attn" and (s == 1 or nxt is None):
                    tables(g, s, q)

            columns(0, 0)
            run_groups(act, step)

        def vector_pass(dve, g, s, q, link):
            x, fr, h, made, _, _, totT, _, hT = slots[s]
            nodes, blks = bass.ds(g * GW, GW), bass.ds(g * GB, GB)
            dve.wait_ge(stored[s], q * STORES + HEAD)
            settle(dve, st.passed)
            if LOADS:
                dve.wait_ge(loaded[s], (q + 1) * LOADS)
            if kind == "first":
                link(nc.vector.tensor_copy(h[:, :, :], x[:, :, :]))
                group_norm(nc, link, h, sq, mean, rstd, tmp, None, None, P)
                link(nc.vector.tensor_scalar(h2[:, :, :], h[:, :, :], 0.0, None, ALU.max))
                link(nc.vector.tensor_copy(x[:, :, :], h2[:, :, :]))
            if kind in ("conv1", "conv2"):
                l = 1 if kind == "conv1" else 2
                dve.wait_ge(turned1, g + 1)
                cg = cnt[:, :, blks]
                if kind == "conv1":
                    link(nc.vector.tensor_tensor(tmp[:, 0:GB], p2[:, 0:GB], fr[:, :, P:P + 1].rearrange("p b o -> p (b o)"), ALU.add))
                    link(nc.vector.tensor_scalar(mean[:, 0:GB], tmp[:, 0:GB], 1.0, None, ALU.max))
                    link(nc.vector.reciprocal(rstd[:, 0:GB], mean[:, 0:GB]))
                    settle(dve, st.passed)
                    link(nc.vector.tensor_copy(cg[:, 0, :], rstd[:, 0:GB]))
                    link(nc.vector.tensor_scalar(cg[:, 1, :], tmp[:, 0:GB], 1.0, None, ALU.min))
                link(nc.vector.tensor_tensor(totT[:, :], acc[:, nodes], p1[:, 0:GW], ALU.add))
                dve.sem_inc(tot_ready, 1)
                dve.wait_ge(mapped, g + 1)
                link(nc.vector.tensor_tensor(h[:, :, :], p1b, bc(cg[:, 0, :].unsqueeze(2), wide), ALU.mult))
                link(nc.vector.tensor_tensor(sq[:, :, :], bc(row(C, f"c{l}_b2").unsqueeze(1), wide),
                                             bc(cg[:, 1, :].unsqueeze(2), wide), ALU.mult))
                link(nc.vector.tensor_tensor(h[:, :, :], h[:, :, :], sq[:, :, :], ALU.add))
                group_norm(nc, link, h, sq, mean, rstd, tmp, row(C, f"n{l}_g"), row(C, f"n{l}_b"), D0)
                dve.sem_inc(pre_act, 1)
                dve.wait_ge(acted, g + 1)
                if kind == "conv1":
                    link(nc.vector.tensor_tensor(h2[:, :, :], h[:, :, :], bc(C["te"][:, :].unsqueeze(1), wide), ALU.add))
                else:
                    link(nc.vector.tensor_tensor(h2[:, :, :], h[:, :, :], x[:, :, :], ALU.add))
                    link(nc.vector.tensor_copy(x[:, :, :], h2[:, :, :]))
            if soft:
                dve.wait_ge(turned1, g + 1)
                link(nc.vector.tensor_copy(sb_small[:, :, :], p_small[:, 0:GB * SMW].rearrange("p (b s) -> p b s", s=SMW)))
                F = FW - SMW
                sa, ma = sb_small[:, :, 0:NS], sb_small[:, :, MR:SMW]
                sf, mf = fr[:, :, F:F + NS], fr[:, :, F + MR:FW]
                for s_, m_, f_ in ((sa, ma, fa), (sf, mf, fb)):
                    link(nc.vector.tensor_scalar(f_[:, :, :], s_, 0.0, -BIG, ALU.is_le, ALU.mult))
                    link(nc.vector.tensor_tensor(f_[:, :, :], f_[:, :, :], m_, ALU.add))
                link(nc.vector.tensor_tensor(M[:, :, :], fa[:, :, :], fb[:, :, :], ALU.max))
                link(nc.vector.tensor_tensor(fa[:, :, :], fa[:, :, :], M[:, :, :], ALU.subtract))
                link(nc.vector.tensor_tensor(fb[:, :, :], fb[:, :, :], M[:, :, :], ALU.subtract))
                dve.sem_inc(below_ready, 1)
                dve.wait_ge(ex_ready, g + 1)
                link(nc.vector.tensor_tensor(S[:, :, :], sa, fa[:, :, :], ALU.mult))
                link(nc.vector.tensor_tensor(M[:, :, :], sf, fb[:, :, :], ALU.mult))
                link(nc.vector.tensor_tensor(S[:, :, :], S[:, :, :], M[:, :, :], ALU.add))
                link(nc.vector.tensor_scalar(S[:, :, :], S[:, :, :], 1e-6, None, ALU.max))
                link(nc.vector.reciprocal(M[:, :, :], S[:, :, :]))
                link(nc.vector.tensor_tensor(fa[:, :, :], fa[:, :, :], M[:, :, :], ALU.mult))
                link(nc.vector.tensor_tensor(fb[:, :, :], fb[:, :, :], M[:, :, :], ALU.mult))

                def weighed(dst, psum, rows_, s0, heads, width):
                    hw = [P, GB, heads, width]
                    for d, v, f_ in ((dst, psum, fa), (sq, rows_, fb)):
                        link(nc.vector.tensor_tensor(d[:, :, :].rearrange("p b (h d) -> p b h d", d=width),
                                                     v.rearrange("p b (h d) -> p b h d", d=width),
                                                     bc(f_[:, :, s0:s0 + heads].unsqueeze(3), hw), ALU.mult))
                    link(nc.vector.tensor_tensor(dst[:, :, :], dst[:, :, :], sq[:, :, :], ALU.add))
            if kind == "attn":
                weighed(h, p1b, fr[:, :, 0:P], 0, H0, D0)
                dve.sem_inc(o_ready, 1)
                dve.wait_ge(o_turned, g + 1)
                link(nc.vector.tensor_copy(totT[:, :], p2[:, 0:GW]))
                dve.sem_inc(oT_ready, 1)
                dve.wait_ge(mapped, g + 1)
                link(nc.vector.tensor_tensor(h[:, :, :], p1b, bc(row(C, "ob").unsqueeze(1), wide), ALU.add))
                group_norm(nc, link, h, sq, mean, rstd, tmp, row(C, "an_g"), row(C, "an_b"), D0)
                link(nc.vector.tensor_tensor(h[:, :, :], h[:, :, :], made[:, :, 0:P], ALU.add))
                link(nc.vector.tensor_tensor(x[:, :, :], x[:, :, :], h[:, :, :], ALU.add))
                link(nc.vector.tensor_copy(h[:, :, :], x[:, :, :]))
                group_norm(nc, link, h, sq, mean, rstd, tmp, None, None, P)
                link(nc.vector.tensor_scalar(h2[:, :, :], h[:, :, :], 0.0, None, ALU.max))
            if kind == "gat":
                weighed(h, p1b, fr[:, :, 0:P], 0, H1, D1)
                link(nc.vector.tensor_tensor(h[:, :, :], h[:, :, :], x[:, :, :], ALU.add))
                link(nc.vector.tensor_tensor(h[:, :, :], h[:, :, :], made[:, :, 0:P], ALU.add))
                weighed(h2, p2b, fr[:, :, P:2 * P], H1, H1, D1)
                link(nc.vector.tensor_tensor(h[:, :, :], h[:, :, :], h2[:, :, :], ALU.add))
            else:
                dve.sem_inc(h_ready, 1)
                dve.wait_ge(turned2, g + 1)
                link(nc.vector.tensor_copy(hT[:, :], p2[:, 0:GW]))
                dve.sem_inc(hT_ready, 1)
                if kind == "conv2":
                    dve.wait_ge(tables_ready, g + 1)
                    link(nc.vector.tensor_tensor(h[:, :, :], p1b, bc(row(C, "qb").unsqueeze(1), wide), ALU.add))
                    link(nc.vector.tensor_scalar(h[:, :, :], h[:, :, :], D0 ** -0.5, None, ALU.mult))
                    link(nc.vector.tensor_tensor(made[:, :, 0:P], pwb[:, :, 0:P], bc(row(C, "kb").unsqueeze(1), wide), ALU.add))
                    link(nc.vector.tensor_tensor(made[:, :, P:2 * P], pwb[:, :, P:2 * P], bc(row(C, "vb").unsqueeze(1), wide), ALU.add))
            if kind in ("conv2", "gat"):
                dve.sem_inc(evacuated, 1)

        @block.vector
        def _(dve):
            dve.sem_inc(evacuated, 2)
            LINKS = {"first": 22, "conv1": 28, "conv2": 28, "attn": 60, "gat": 24}[kind]

            def step(g, s, q, _):
                link = Chain(dve, chain, g * LINKS)
                vector_pass(dve, g, s, q, link)
                assert link.n == LINKS, (kind, link.n)
            run_groups(dve, step)


def build(nc, w, out):
    with ExitStack() as ctx:
        def sb(name, shape, dt=F32):
            return ctx.enter_context(nc.sbuf_tensor(name, shape, dt))

        def dram(name, shape, dt=F32):
            return nc.dram_tensor(name, shape, dt, kind="Internal").ap()

        D = {"cols": dram("cols", (NB, P, 2 * BT)), "places": dram("places", (NB, BE), BF16),
             "mask": dram("mask", (T * NS, P + 1)),
             "a1": dram("a1", (NW, P)), "b1": dram("b1", (NP, P)), "a2": dram("a2", (NW, P)), "b2": dram("b2", (NP, P)),
             "base": dram("base", (NP, P)), "h": dram("h", (NP, P)), "hd": dram("hd", (NP, P)), "q": dram("q", (NW, P)), "kv": dram("kv", (NP, 2 * P)), "g": dram("g", (NP, P + H1)), "ed": dram("ed", (NW, NS))}
        for name, width in FOLDED.items():
            D[name] = dram(name, (NB * FR, width))
        C = {"ident": sb("ident", [P, P]), "ones": sb("ones", [1, P]), "iota_row": sb("iota_row", [P, P], BF16),
             "iota_col": sb("iota_col", [P, 1]), "fold_row": sb("fold_row", [P, TC], I32),
             "expand": sb("expand", [P, 3, P]), "te": sb("te", [P, P]), "rows": sb("rows", [P, len(ROWS), P]),
             "wq": sb("wq", [P, P]), "wkv": sb("wkv", [P, 2, P]), "wo": sb("wo", [P, P]), "we": sb("we", [ED + 1, H0]),
             "wsd": sb("wsd", [P, 2, P]), "weta": sb("weta", [P, P + NS]), "ones_b": sb("ones_b", [P, 1], BF16), "wsa": sb("wsa", [P, 3 * H1])}
        for l in (1, 2):
            C[f"wab{l}"], C[f"wc{l}"], C[f"w2{l}"] = sb(f"wab{l}", [P, 2, P]), sb(f"wc{l}", [ED + 1, P]), sb(f"w2{l}", [P, P])
        cnt = sb("cnt", [P, 2, NBLK])

        prepare(nc, w, C, D)
        node_stage(nc, "first", w, C, D, cnt, None, None, None, out)
        with nc.sbuf_tensor("acc1", [P, NW], F32) as acc, nc.sbuf_tensor("first1", [P, TP], F32) as first:
            with nc.sbuf_tensor("count", [1, NW], F32) as count, nc.sbuf_tensor("first_count", [1, TP], F32) as first_count:
                conv_edges(nc, 1, w, C, D, acc, first, count, first_count)
                fold(nc, "fold1", w, C, D["fold1"], first, None, first_count, None)
                node_stage(nc, "conv1", w, C, D, cnt, acc, None, count, out)
            conv_edges(nc, 2, w, C, D, acc, first, None, None)
            fold(nc, "fold2", w, C, D["fold2"], first, None, None, None)
            node_stage(nc, "conv2", w, C, D, cnt, acc, None, None, out)
        with nc.sbuf_tensor("acc2", [P, NW], F32) as acc, nc.sbuf_tensor("first2", [P, TP], F32) as first, \
                nc.sbuf_tensor("small", [SMW, NW], F32) as small, nc.sbuf_tensor("first_small", [SMW, TP], F32) as first_small:
            attention_edges(nc, False, w, C, D, acc, first, None, None, small, first_small)
            fold(nc, "fold3", w, C, D["fold3"], first, None, first_small, [0])
            node_stage(nc, "attn", w, C, D, cnt, acc, None, small, out)
            with nc.sbuf_tensor("acc_e", [P, NW], F32) as acc_e, nc.sbuf_tensor("first_e", [P, TP], F32) as first_e:
                attention_edges(nc, True, w, C, D, acc, first, acc_e, first_e, small, first_small)
                fold(nc, "fold4", w, C, D["fold4"], first, first_e, first_small, [1, 2])
                node_stage(nc, "gat", w, C, D, cnt, acc, acc_e, small, out)


def kernel(**inputs):
    import concourse.bacc as bacc
    from concourse.bass_utils import run_bass_kernel_spmd

    src, dst = np.asarray(inputs["src"]), np.asarray(inputs["dst"])
    pad = EP - E
    src = np.concatenate([src, np.zeros(pad, np.int32)])
    dst = np.concatenate([dst, np.full(pad, N, np.int32)])
    n0 = np.concatenate([dst[::P], np.full(TP - T + 1, N, np.int32)])
    arrays = {
        "x": np.concatenate([np.asarray(inputs["x"]), np.zeros((NP - N, P), np.float32)]),
        "src_b": src.reshape(NB, BT, P).transpose(0, 2, 1),
        "dst_b": dst.reshape(NB, BT, P).transpose(0, 2, 1).reshape(NB, BE),
        "dst_r": dst.reshape(NB, BE),
        "n0_b": n0[:T].reshape(NB, BT),
        "n0_p": n0[:TP].reshape(1, TP),
        "n0_c": n0[:TP].reshape(TC, P).T,
        "n0_next": n0[1:].reshape(TC, P).T,
        "ea": np.concatenate([np.concatenate([np.asarray(inputs["edge_attr_4"]), np.zeros((pad, ED), np.float32)]).T,
                              np.ones((1, EP), np.float32)]),
        "xeT": np.concatenate([np.asarray(inputs["edge_attr_128"]), np.zeros((pad, P), np.float32)]).T,
    }
    for name, a in inputs.items():
        if name.startswith(("L0_gnn_", "L1_gnn_")):
            arrays[name[7:]] = np.asarray(a)
    nc = bacc.Bacc("TRN2", target_bir_lowering=False, num_devices=1)
    feeds, w = {}, {}
    for name, a in arrays.items():
        a = np.ascontiguousarray(a)
        feeds["in_" + name] = a
        w[name] = nc.dram_tensor("in_" + name, a.shape, mybir.dt.from_np(a.dtype), kind="ExternalInput").ap()
    out = nc.dram_tensor("out", (NP, P), F32, kind="ExternalOutput").ap()
    build(nc, w, out)
    result = run_bass_kernel_spmd(nc, [feeds], core_ids=[0])
    return result.results[0]["out"][:N]
```
